# Optimizing a Trainium2 kernel written in Bass

```python
import numpy as np
import jax
import jax.numpy as jnp

def _softmax(x, axis=-1):
    return jax.nn.softmax(x, axis=axis)

def _gelu(x):
    return jax.nn.gelu(x, approximate=True)

def _silu(x):
    return jax.nn.silu(x)

def _sigmoid(x):
    return jax.nn.sigmoid(x)

def _layernorm(x, axis=-1, eps=1e-05):
    m = jnp.mean(x, axis=axis, keepdims=True)
    v = jnp.var(x, axis=axis, keepdims=True)
    return (x - m) / jnp.sqrt(v + eps)

def _scatter_add(tgt, idx, src, axis=0):
    return tgt.at[idx].add(src)

def _segment_sum(src, seg, n):
    return jax.ops.segment_sum(src, seg, n)
kernel_name = 'mk_vit_tower_d4_tok_img256_r4_47f37a'

def setup_inputs(seed: int=0):
    np.random.seed(seed)
    _w = jnp.asarray

    def _rec_inputs():
        import jax
        import jax.numpy as jnp
        _rk = jax.random.key(seed)
        x = -0.0003702 + 0.999946 * jax.random.normal(jax.random.fold_in(_rk, 1), (64, 1, 112, 112), jnp.float32)
        return x
    x = _rec_inputs()

    def _L0_tok_setup():
        import jax, jax.numpy as jnp
        import numpy as np
        PH, PW = (64, 25)
        SH, SW = (64, 12)

        def _unfold(x, ph, pw, sh, sw):
            B, C, H, W = x.shape
            nh = (H - ph) // sh + 1
            nw = (W - pw) // sw + 1
            rows = jnp.arange(nh)[:, None] * sh + jnp.arange(ph)[None, :]
            cols = jnp.arange(nw)[:, None] * sw + jnp.arange(pw)[None, :]
            p = x[:, :, rows, :]
            p = p[:, :, :, :, cols]
            p = jnp.transpose(p, (0, 2, 4, 1, 3, 5))
            return p.reshape(B, nh * nw, C * ph * pw)
        key = jax.random.key(seed)
        kx, kw = jax.random.split(key, 2)
        x = jax.random.normal(kx, (64, 1, 64, 1000), dtype=jnp.float32)
        in_dim = 1 * PH * PW
        weight = jax.random.normal(kw, (in_dim, 64), dtype=jnp.float32) / np.sqrt(in_dim).astype(np.float32)
        bias = jnp.zeros((64,), dtype=jnp.float32)
        return {'x': x, 'weight': weight, 'bias': bias}
    _L0_tok_all = _L0_tok_setup()
    _L0_tok_in = {k: v for k, v in _L0_tok_all.items() if k in ('weight', 'bias')}
    del _L0_tok_all

    def _L0_attn_setup():
        import jax, jax.numpy as jnp
        import numpy as np
        key = jax.random.key(seed)
        k1, k2 = jax.random.split(key)
        B, N, D = (4, 1024, 64)
        inp = jax.random.normal(k1, (B, N, D), dtype=jnp.float32)
        q_weight = jax.random.normal(k2, (D, D), dtype=jnp.float32)
        return {'input': inp, 'q_weight': q_weight}
    _L0_attn_all = _L0_attn_setup()
    _L0_attn_in = {k: v for k, v in _L0_attn_all.items() if k in ('q_weight',)}
    del _L0_attn_all

    def _L0_ffn_setup():
        import jax, jax.numpy as jnp
        import numpy as np
        B, S, D = (8, 1024, 64)
        H = 4 * D
        CAPACITY = 0.5
        key = jax.random.key(seed)
        ks = jax.random.split(key, 6)
        x = jax.random.normal(ks[0], (B, S, D), dtype=jnp.float32)
        attention_mask = jnp.zeros((B, 1, 1, S), dtype=jnp.float32)
        wr = jax.random.normal(ks[1], (D, 1), dtype=jnp.float32) * 0.02
        br = jnp.zeros((1,), dtype=jnp.float32)
        w1 = jax.random.normal(ks[2], (D, H), dtype=jnp.float32) * 0.02
        b1 = jnp.zeros((H,), dtype=jnp.float32)
        w2 = jax.random.normal(ks[3], (H, D), dtype=jnp.float32) * 0.02
        b2 = jnp.zeros((D,), dtype=jnp.float32)
        return {'x': x, 'attention_mask': attention_mask, 'wr': wr, 'br': br, 'w1': w1, 'b1': b1, 'w2': w2, 'b2': b2}
    _L0_ffn_all = _L0_ffn_setup()
    _L0_ffn_in = {k: v for k, v in _L0_ffn_all.items() if k in ('attention_mask', 'wr', 'br', 'w1', 'b1', 'w2', 'b2')}
    del _L0_ffn_all

    def _L1_attn_setup():
        import jax, jax.numpy as jnp
        import numpy as np
        key = jax.random.key(seed)
        ks = jax.random.split(key, 5)
        b, t, e, h = (8, 256, 64, 8)
        w = lambda k, shape: jax.random.normal(k, shape, dtype=jnp.float32) * 0.02
        return {'x': jax.random.normal(ks[0], (b, t, e), dtype=jnp.float32), 'Wq': w(ks[1], (e, e * h)), 'bq': jnp.zeros((e * h,), jnp.float32), 'Wk': w(ks[2], (e, e * h)), 'bk': jnp.zeros((e * h,), jnp.float32), 'Wv': w(ks[3], (e, e * h)), 'bv': jnp.zeros((e * h,), jnp.float32), 'Wu': w(ks[4], (e * h, e)), 'bu': jnp.zeros((e,), jnp.float32)}
    _L1_attn_all = _L1_attn_setup()
    _L1_attn_in = {k: v for k, v in _L1_attn_all.items() if k in ('Wq', 'bq', 'Wk', 'bk', 'Wv', 'bv', 'Wu', 'bu')}
    del _L1_attn_all

    def _L1_ffn_setup():
        import jax, jax.numpy as jnp
        import numpy as np
        TOP_K = 2
        LN_EPS = 1e-05
        key = jax.random.key(seed)
        ks = jax.random.split(key, 8)
        B, S, D, E, H = (16, 256, 64, 8, 256)
        x = jax.random.normal(ks[0], (B, S, D), dtype=jnp.float32)
        Wr = jax.random.normal(ks[1], (D, E), dtype=jnp.float32) * 0.1
        br = jnp.zeros((E,), dtype=jnp.float32)
        ln_g = jnp.ones((E, D), dtype=jnp.float32)
        ln_b = jnp.zeros((E, D), dtype=jnp.float32)
        W1 = jax.random.normal(ks[2], (E, D, H), dtype=jnp.float32) * (1.0 / np.sqrt(D))
        b1 = jnp.zeros((E, H), dtype=jnp.float32)
        W2 = jax.random.normal(ks[3], (E, H, D), dtype=jnp.float32) * (1.0 / np.sqrt(H))
        b2 = jnp.zeros((E, D), dtype=jnp.float32)
        return {'x': x, 'Wr': Wr, 'br': br, 'ln_g': ln_g, 'ln_b': ln_b, 'W1': W1, 'b1': b1, 'W2': W2, 'b2': b2}
    _L1_ffn_all = _L1_ffn_setup()
    _L1_ffn_in = {k: v for k, v in _L1_ffn_all.items() if k in ('Wr', 'br', 'ln_g', 'ln_b', 'W1', 'b1', 'W2', 'b2')}
    del _L1_ffn_all

    def _L2_attn_setup():
        import math
        import jax, jax.numpy as jnp
        import numpy as np
        D_MODEL = 64
        N_HEADS = 4
        HEAD_DIM = D_MODEL // N_HEADS
        MAX_REL = 30

        def _rel_pos_encodings(t, d_model):
            n = 2 * MAX_REL + 1
            positions = jnp.arange(n, dtype=jnp.float32)[:, None]
            div_term = jnp.exp(jnp.arange(0, d_model, 2, dtype=jnp.float32) * (-math.log(10000.0) / d_model))
            ang = positions * div_term
            enc = jnp.stack([jnp.sin(ang), jnp.cos(ang)], axis=-1).reshape(n, d_model)
            rng = jnp.arange(t)
            final_mat = jnp.clip(rng[None, :] - rng[:, None], -MAX_REL, MAX_REL) + MAX_REL
            return enc[final_mat]
        key = jax.random.key(seed)
        ks = jax.random.split(key, 12)
        d = D_MODEL
        s = 1.0 / math.sqrt(d)
        inp = {'inputs': jax.random.normal(ks[0], (16, 128, d), dtype=jnp.float32), 'ln_gamma': jnp.ones((d,), jnp.float32), 'ln_beta': jnp.zeros((d,), jnp.float32), 'Wq': jax.random.normal(ks[1], (d, d), jnp.float32) * s, 'bq': jnp.zeros((d,), jnp.float32), 'Wk': jax.random.normal(ks[2], (d, d), jnp.float32) * s, 'bk': jnp.zeros((d,), jnp.float32), 'Wv': jax.random.normal(ks[3], (d, d), jnp.float32) * s, 'bv': jnp.zeros((d,), jnp.float32), 'Wpos': jax.random.normal(ks[4], (d, d), jnp.float32) * s, 'bpos': jnp.zeros((d,), jnp.float32), 'Wo': jax.random.normal(ks[5], (d, d), jnp.float32) * s, 'bo': jnp.zeros((d,), jnp.float32), 'u_bias': jax.random.normal(ks[6], (1, N_HEADS, 1, HEAD_DIM), jnp.float32) * 0.02, 'v_bias': jax.random.normal(ks[7], (1, N_HEADS, 1, HEAD_DIM), jnp.float32) * 0.02}
        return inp
    _L2_attn_all = _L2_attn_setup()
    _L2_attn_in = {k: v for k, v in _L2_attn_all.items() if k in ('ln_gamma', 'ln_beta', 'Wq', 'bq', 'Wk', 'bk', 'Wv', 'bv', 'Wpos', 'bpos', 'Wo', 'bo', 'u_bias', 'v_bias')}
    del _L2_attn_all

    def _L2_ffn_setup():
        import jax, jax.numpy as jnp
        import numpy as np
        INPUT_WIDTH = 64
        DEPTH = 7
        OUTPUT_WIDTH = 64
        N_NODES = 2 ** (DEPTH + 1) - 1
        key = jax.random.key(seed)
        k_x, k_w1, k_w2 = jax.random.split(key, 3)
        init1 = 1.0 / np.sqrt(INPUT_WIDTH)
        x = jax.random.normal(k_x, (2, 256, INPUT_WIDTH), dtype=jnp.float32)
        w1s = jax.random.uniform(k_w1, (N_NODES, INPUT_WIDTH), jnp.float32, -init1, init1)
        b1s = jnp.zeros((N_NODES,), jnp.float32)
        w2s = jax.random.uniform(k_w2, (N_NODES, INPUT_WIDTH, OUTPUT_WIDTH), jnp.float32, -init1, init1)
        b2s = jnp.zeros((N_NODES, OUTPUT_WIDTH), jnp.float32)
        return {'x': x, 'w1s': w1s, 'b1s': b1s, 'w2s': w2s, 'b2s': b2s}
    _L2_ffn_all = _L2_ffn_setup()
    _L2_ffn_in = {k: v for k, v in _L2_ffn_all.items() if k in ('w1s', 'b1s', 'w2s', 'b2s')}
    del _L2_ffn_all

    def _L3_attn_setup():
        import jax, jax.numpy as jnp
        import numpy as np
        TEMPERATURE = 1.0
        W_BLEND = 0.8
        EPS = 1e-12

        def _l2norm(x):
            n = jnp.sqrt(jnp.sum(x * x, axis=-1, keepdims=True))
            return x / jnp.maximum(n, EPS)
        key = jax.random.key(seed)
        feats = jax.random.normal(key, (4, 512, 64), dtype=jnp.float32)
        return {'feats': feats}
    _L3_attn_all = _L3_attn_setup()
    _L3_attn_in = {k: v for k, v in _L3_attn_all.items() if k in ()}
    del _L3_attn_all

    def _L3_ffn_setup():
        import jax, jax.numpy as jnp
        import numpy as np
        B, T, C = (64, 96, 64)
        NH, NKV = (4, 2)
        HD = C // NH
        NREP = NH // NKV
        NE, TOPK = (8, 2)
        HID = int(8 / 3 * C)
        EPS_RMS = 1e-06

        def _rope_tables(t_len):
            inv_freq = 1.0 / 10000.0 ** (np.arange(0, HD, 2, dtype=np.float32) / HD)
            t = np.arange(t_len, dtype=np.float32)
            freqs = np.outer(t, inv_freq)
            emb = np.concatenate([freqs, freqs], axis=-1)
            return (jnp.asarray(np.cos(emb)), jnp.asarray(np.sin(emb)))

        def _rotate_half(x):
            h = x.shape[-1] // 2
            return jnp.concatenate([-x[..., h:], x[..., :h]], axis=-1)

        def _rmsnorm(v, w):
            return v * jax.lax.rsqrt(jnp.mean(v * v, axis=-1, keepdims=True) + EPS_RMS) * w
        key = jax.random.key(seed)
        ks = jax.random.split(key, 10)
        s = lambda k, shape: jax.random.normal(k, shape, jnp.float32) * 0.02
        return {'x': jax.random.normal(ks[0], (B, T, C), jnp.float32), 'ln1_w': jnp.ones((C,), jnp.float32), 'ln2_w': jnp.ones((C,), jnp.float32), 'wq': s(ks[1], (NH * HD, C)), 'wk': s(ks[2], (NKV * HD, C)), 'wv': s(ks[3], (NKV * HD, C)), 'wo': s(ks[4], (C, C)), 'router_w': s(ks[5], (NE, C)), 'w1': s(ks[6], (NE, HID, C)), 'w2': s(ks[7], (NE, C, HID)), 'w3': s(ks[8], (NE, HID, C))}
    _L3_ffn_all = _L3_ffn_setup()
    _L3_ffn_in = {k: v for k, v in _L3_ffn_all.items() if k in ('ln1_w', 'ln2_w', 'wq', 'wk', 'wv', 'wo', 'router_w', 'w1', 'w2', 'w3')}
    del _L3_ffn_all
    return {'x': x, 'L0_tok_weight': _L0_tok_in['weight'], 'L0_tok_bias': _L0_tok_in['bias'], 'L0_attn_q_weight': _L0_attn_in['q_weight'], 'L0_ffn_attention_mask': _L0_ffn_in['attention_mask'], 'L0_ffn_wr': _L0_ffn_in['wr'], 'L0_ffn_br': _L0_ffn_in['br'], 'L0_ffn_w1': _L0_ffn_in['w1'], 'L0_ffn_b1': _L0_ffn_in['b1'], 'L0_ffn_w2': _L0_ffn_in['w2'], 'L0_ffn_b2': _L0_ffn_in['b2'], 'L1_attn_Wq': _L1_attn_in['Wq'], 'L1_attn_bq': _L1_attn_in['bq'], 'L1_attn_Wk': _L1_attn_in['Wk'], 'L1_attn_bk': _L1_attn_in['bk'], 'L1_attn_Wv': _L1_attn_in['Wv'], 'L1_attn_bv': _L1_attn_in['bv'], 'L1_attn_Wu': _L1_attn_in['Wu'], 'L1_attn_bu': _L1_attn_in['bu'], 'L1_ffn_Wr': _L1_ffn_in['Wr'], 'L1_ffn_br': _L1_ffn_in['br'], 'L1_ffn_ln_g': _L1_ffn_in['ln_g'], 'L1_ffn_ln_b': _L1_ffn_in['ln_b'], 'L1_ffn_W1': _L1_ffn_in['W1'], 'L1_ffn_b1': _L1_ffn_in['b1'], 'L1_ffn_W2': _L1_ffn_in['W2'], 'L1_ffn_b2': _L1_ffn_in['b2'], 'L2_attn_ln_gamma': _L2_attn_in['ln_gamma'], 'L2_attn_ln_beta': _L2_attn_in['ln_beta'], 'L2_attn_Wq': _L2_attn_in['Wq'], 'L2_attn_bq': _L2_attn_in['bq'], 'L2_attn_Wk': _L2_attn_in['Wk'], 'L2_attn_bk': _L2_attn_in['bk'], 'L2_attn_Wv': _L2_attn_in['Wv'], 'L2_attn_bv': _L2_attn_in['bv'], 'L2_attn_Wpos': _L2_attn_in['Wpos'], 'L2_attn_bpos': _L2_attn_in['bpos'], 'L2_attn_Wo': _L2_attn_in['Wo'], 'L2_attn_bo': _L2_attn_in['bo'], 'L2_attn_u_bias': _L2_attn_in['u_bias'], 'L2_attn_v_bias': _L2_attn_in['v_bias'], 'L2_ffn_w1s': _L2_ffn_in['w1s'], 'L2_ffn_b1s': _L2_ffn_in['b1s'], 'L2_ffn_w2s': _L2_ffn_in['w2s'], 'L2_ffn_b2s': _L2_ffn_in['b2s'], 'L3_ffn_ln1_w': _L3_ffn_in['ln1_w'], 'L3_ffn_ln2_w': _L3_ffn_in['ln2_w'], 'L3_ffn_wq': _L3_ffn_in['wq'], 'L3_ffn_wk': _L3_ffn_in['wk'], 'L3_ffn_wv': _L3_ffn_in['wv'], 'L3_ffn_wo': _L3_ffn_in['wo'], 'L3_ffn_router_w': _L3_ffn_in['router_w'], 'L3_ffn_w1': _L3_ffn_in['w1'], 'L3_ffn_w2': _L3_ffn_in['w2'], 'L3_ffn_w3': _L3_ffn_in['w3']}

def reference(x, L0_tok_weight, L0_tok_bias, L0_attn_q_weight, L0_ffn_attention_mask, L0_ffn_wr, L0_ffn_br, L0_ffn_w1, L0_ffn_b1, L0_ffn_w2, L0_ffn_b2, L1_attn_Wq, L1_attn_bq, L1_attn_Wk, L1_attn_bk, L1_attn_Wv, L1_attn_bv, L1_attn_Wu, L1_attn_bu, L1_ffn_Wr, L1_ffn_br, L1_ffn_ln_g, L1_ffn_ln_b, L1_ffn_W1, L1_ffn_b1, L1_ffn_W2, L1_ffn_b2, L2_attn_ln_gamma, L2_attn_ln_beta, L2_attn_Wq, L2_attn_bq, L2_attn_Wk, L2_attn_bk, L2_attn_Wv, L2_attn_bv, L2_attn_Wpos, L2_attn_bpos, L2_attn_Wo, L2_attn_bo, L2_attn_u_bias, L2_attn_v_bias, L2_ffn_w1s, L2_ffn_b1s, L2_ffn_w2s, L2_ffn_b2s, L3_ffn_ln1_w, L3_ffn_ln2_w, L3_ffn_wq, L3_ffn_wk, L3_ffn_wv, L3_ffn_wo, L3_ffn_router_w, L3_ffn_w1, L3_ffn_w2, L3_ffn_w3):
    import jax
    import jax.numpy as jnp

    def _L0_tok_ref(x, weight, bias):
        import jax, jax.numpy as jnp
        import numpy as np
        PH, PW = (64, 25)
        SH, SW = (64, 12)

        def _unfold(x, ph, pw, sh, sw):
            B, C, H, W = x.shape
            nh = (H - ph) // sh + 1
            nw = (W - pw) // sw + 1
            rows = jnp.arange(nh)[:, None] * sh + jnp.arange(ph)[None, :]
            cols = jnp.arange(nw)[:, None] * sw + jnp.arange(pw)[None, :]
            p = x[:, :, rows, :]
            p = p[:, :, :, :, cols]
            p = jnp.transpose(p, (0, 2, 4, 1, 3, 5))
            return p.reshape(B, nh * nw, C * ph * pw)
        p = _unfold(x, PH, PW, SH, SW)
        return jax.nn.gelu(jnp.einsum('bnk,kd->bnd', p, weight) + bias, approximate=False)

    def _L0_attn_ref(input, q_weight):
        import jax, jax.numpy as jnp
        import numpy as np
        query = jnp.einsum('bnd,de->bne', input, q_weight)
        att = jax.nn.sigmoid(jnp.einsum('bnd,bmd->bnm', query, input))
        value = jnp.einsum('bnm,bmd->bnd', att, input)
        return value

    def _L0_ffn_ref(x, attention_mask, wr, br, w1, b1, w2, b2):
        import jax, jax.numpy as jnp
        import numpy as np
        B, S, D = (8, 1024, 64)
        H = 4 * D
        CAPACITY = 0.5
        b, s, d = x.shape
        weights = (jnp.einsum('bsd,do->bso', x, wr) + br)[..., 0]
        k = max(1, int(CAPACITY * s))
        kk = k - 1 if k > 1 else 1
        _, idx = jax.lax.top_k(weights, k)
        sel_idx = idx[:, :kk]
        sel = jnp.take_along_axis(x, sel_idx[:, :, None], axis=1)
        h = jax.nn.gelu(jnp.einsum('bkd,dh->bkh', sel, w1) + b1)
        y = jnp.einsum('bkh,hd->bkd', h, w2) + b2
        w_sel = jnp.take_along_axis(weights, sel_idx, axis=1)
        y = y * w_sel[..., None]
        batch_idx = jnp.arange(b)[:, None]
        processed = jnp.zeros_like(x).at[batch_idx, sel_idx].set(y)
        return processed + x

    def _L1_attn_ref(x, Wq, bq, Wk, bk, Wv, bv, Wu, bu):
        import jax, jax.numpy as jnp
        import numpy as np
        b, t, e = x.shape
        h = Wq.shape[1] // e
        q = (x @ Wq + bq).reshape(b, t, h, e)
        k = (x @ Wk + bk).reshape(b, t, h, e)
        v = (x @ Wv + bv).reshape(b, t, h, e)
        scores = jnp.einsum('bihe,bjhe->bhij', q, k) / jnp.sqrt(jnp.asarray(e, jnp.float32))
        i = jnp.arange(t)[:, None]
        j = jnp.arange(t)[None, :]
        scores = jnp.where(j >= i, -jnp.inf, scores)
        scores = jnp.where(i == 0, 0.0, scores)
        att = jax.nn.softmax(scores, axis=-1)
        att = jnp.where(i == 0, 0.0, att)
        out = jnp.einsum('bhij,bjhe->bihe', att, v).reshape(b, t, h * e)
        return out @ Wu + bu

    def _L1_ffn_ref(x, Wr, br, ln_g, ln_b, W1, b1, W2, b2):
        import jax, jax.numpy as jnp
        import numpy as np
        TOP_K = 2
        LN_EPS = 1e-05
        B, S, D = x.shape
        N = B * S
        xt = x.reshape(N, D)
        logits = xt @ Wr + br
        probs = jax.nn.softmax(logits, axis=-1)
        top_p, top_idx = jax.lax.top_k(probs, TOP_K)
        weights = top_p / top_p.sum(axis=-1, keepdims=True)
        mu = xt.mean(axis=-1, keepdims=True)
        var = ((xt - mu) ** 2).mean(axis=-1, keepdims=True)
        xn = (xt - mu) * jax.lax.rsqrt(var + LN_EPS)
        xe = xn[None, :, :] * ln_g[:, None, :] + ln_b[:, None, :]
        h = jax.nn.gelu(jnp.einsum('end,edh->enh', xe, W1) + b1[:, None, :], approximate=False)
        y = jnp.einsum('enh,ehd->end', h, W2) + b2[:, None, :]
        y_tok = jnp.transpose(y, (1, 0, 2))
        sel = jnp.take_along_axis(y_tok, top_idx[:, :, None], axis=1)
        out = (weights[:, :, None] * sel).sum(axis=1)
        return out.reshape(B, S, D)

    def _L2_attn_ref(inputs, ln_gamma, ln_beta, Wq, bq, Wk, bk, Wv, bv, Wpos, bpos, Wo, bo, u_bias, v_bias):
        import math
        import jax, jax.numpy as jnp
        import numpy as np
        D_MODEL = 64
        N_HEADS = 4
        HEAD_DIM = D_MODEL // N_HEADS
        MAX_REL = 30

        def _rel_pos_encodings(t, d_model):
            n = 2 * MAX_REL + 1
            positions = jnp.arange(n, dtype=jnp.float32)[:, None]
            div_term = jnp.exp(jnp.arange(0, d_model, 2, dtype=jnp.float32) * (-math.log(10000.0) / d_model))
            ang = positions * div_term
            enc = jnp.stack([jnp.sin(ang), jnp.cos(ang)], axis=-1).reshape(n, d_model)
            rng = jnp.arange(t)
            final_mat = jnp.clip(rng[None, :] - rng[:, None], -MAX_REL, MAX_REL) + MAX_REL
            return enc[final_mat]
        b, t, d = inputs.shape
        h, hd = (N_HEADS, HEAD_DIM)
        mu = jnp.mean(inputs, axis=-1, keepdims=True)
        var = jnp.mean(jnp.square(inputs - mu), axis=-1, keepdims=True)
        x = (inputs - mu) * jax.lax.rsqrt(var + 1e-05) * ln_gamma + ln_beta

        def split_heads(y):
            return y.reshape(b, t, h, hd).transpose(0, 2, 1, 3)
        q = split_heads(x @ Wq.T + bq)
        k = split_heads(x @ Wk.T + bk)
        v = split_heads(x @ Wv.T + bv)
        rel = jax.lax.stop_gradient(_rel_pos_encodings(t, d))
        pos = (rel @ Wpos.T + bpos).reshape(t, t, h, hd)
        qk_score = jnp.einsum('bhtd,bhsd->bhts', q + u_bias, k)
        pos_score = jnp.einsum('bhtd,tshd->bhts', q + v_bias, pos)
        scores = (qk_score + pos_score) / math.sqrt(hd)
        attn = jax.nn.softmax(scores, axis=-1)
        ctx = jnp.einsum('bhts,bhsd->bhtd', attn, v)
        ctx = ctx.transpose(0, 2, 1, 3).reshape(b, t, d)
        return ctx @ Wo.T + bo

    def _L2_ffn_ref(x, w1s, b1s, w2s, b2s):
        import jax, jax.numpy as jnp
        import numpy as np
        INPUT_WIDTH = 64
        DEPTH = 7
        OUTPUT_WIDTH = 64
        N_NODES = 2 ** (DEPTH + 1) - 1
        B, S, D = x.shape
        flat_x = x.reshape(B * S, D)
        T = flat_x.shape[0]
        current = jnp.zeros((T,), dtype=jnp.int32)
        all_nodes = []
        all_logits = []
        for _ in range(DEPTH + 1):
            all_nodes.append(current)
            score = jnp.einsum('td,td->t', flat_x, w1s[current]) + b1s[current]
            all_logits.append(score)
            choice = ((jnp.sign(score) + 1.0) / 2.0).astype(jnp.int32)
            current = current * 2 + choice + 1
        logits = jnp.stack(all_logits, axis=1)
        path_weights = jax.nn.gelu(jnp.abs(logits), approximate=False)
        out = jnp.zeros((T, OUTPUT_WIDTH), dtype=x.dtype)
        for i in range(DEPTH + 1):
            nodes_i = all_nodes[i]
            t_i = jnp.einsum('td,tdo->to', flat_x, w2s[nodes_i]) + b2s[nodes_i]
            out = out + t_i * path_weights[:, i][:, None]
        return out.reshape(B, S, OUTPUT_WIDTH)

    def _L3_attn_ref(feats):
        import jax, jax.numpy as jnp
        import numpy as np
        TEMPERATURE = 1.0
        W_BLEND = 0.8
        EPS = 1e-12

        def _l2norm(x):
            n = jnp.sqrt(jnp.sum(x * x, axis=-1, keepdims=True))
            return x / jnp.maximum(n, EPS)
        B, N, C = feats.shape
        f = _l2norm(feats.reshape(B * N, C))
        scores = jnp.matmul(f, f.T) / TEMPERATURE
        attn = jax.nn.softmax(scores, axis=-1)
        feats_att = jnp.matmul(attn, f)
        feats_fcm = f * W_BLEND + feats_att * (1.0 - W_BLEND)
        return _l2norm(feats_fcm.reshape(B, N, C))

    def _L3_ffn_ref(x, ln1_w, ln2_w, wq, wk, wv, wo, router_w, w1, w2, w3):
        import jax, jax.numpy as jnp
        import numpy as np
        B, T, C = (64, 96, 64)
        NH, NKV = (4, 2)
        HD = C // NH
        NREP = NH // NKV
        NE, TOPK = (8, 2)
        HID = int(8 / 3 * C)
        EPS_RMS = 1e-06

        def _rope_tables(t_len):
            inv_freq = 1.0 / 10000.0 ** (np.arange(0, HD, 2, dtype=np.float32) / HD)
            t = np.arange(t_len, dtype=np.float32)
            freqs = np.outer(t, inv_freq)
            emb = np.concatenate([freqs, freqs], axis=-1)
            return (jnp.asarray(np.cos(emb)), jnp.asarray(np.sin(emb)))

        def _rotate_half(x):
            h = x.shape[-1] // 2
            return jnp.concatenate([-x[..., h:], x[..., :h]], axis=-1)

        def _rmsnorm(v, w):
            return v * jax.lax.rsqrt(jnp.mean(v * v, axis=-1, keepdims=True) + EPS_RMS) * w
        Bx, Tx, Cx = x.shape
        h = _rmsnorm(x, ln1_w)
        q = (h @ wq.T).reshape(Bx, Tx, NH, HD).transpose(0, 2, 1, 3)
        k = (h @ wk.T).reshape(Bx, Tx, NKV, HD).transpose(0, 2, 1, 3)
        v = (h @ wv.T).reshape(Bx, Tx, NKV, HD).transpose(0, 2, 1, 3)
        cos, sin = _rope_tables(Tx)
        cos, sin = (cos[None, None], sin[None, None])
        q = q * cos + _rotate_half(q) * sin
        k = k * cos + _rotate_half(k) * sin
        k = jnp.repeat(k, NREP, axis=1)
        v = jnp.repeat(v, NREP, axis=1)
        scores = jnp.einsum('bhtd,bhsd->bhts', q, k) / jnp.sqrt(jnp.float32(HD))
        causal = jnp.tril(jnp.ones((Tx, Tx), dtype=bool))
        scores = jnp.where(causal[None, None], scores, jnp.float32(-1e+30))
        att = jax.nn.softmax(scores, axis=-1)
        y = jnp.einsum('bhts,bhsd->bhtd', att, v).transpose(0, 2, 1, 3).reshape(Bx, Tx, Cx)
        x = x + y @ wo.T
        flat = _rmsnorm(x, ln2_w).reshape(-1, Cx)
        probs = jax.nn.softmax(flat @ router_w.T, axis=-1)
        tp, ti = jax.lax.top_k(probs, TOPK)
        tp = tp / (jnp.sum(tp, axis=-1, keepdims=True) + 1e-09)
        weights = jnp.sum(tp[..., None] * jax.nn.one_hot(ti, NE, dtype=flat.dtype), axis=1)
        out = jnp.zeros_like(flat)
        for e in range(NE):
            hh = jax.nn.silu(flat @ w1[e].T) * (flat @ w3[e].T)
            out = out + weights[:, e:e + 1] * (hh @ w2[e].T)
        return x + out.reshape(Bx, Tx, Cx)
    h = _L0_tok_ref(x, L0_tok_weight, L0_tok_bias)
    h = h + _L0_attn_ref(_layernorm(h, axis=-1), L0_attn_q_weight)
    h = h + _L0_ffn_ref(_layernorm(h, axis=-1), L0_ffn_attention_mask, L0_ffn_wr, L0_ffn_br, L0_ffn_w1, L0_ffn_b1, L0_ffn_w2, L0_ffn_b2)
    h = h + _L1_attn_ref(_layernorm(h, axis=-1), L1_attn_Wq, L1_attn_bq, L1_attn_Wk, L1_attn_bk, L1_attn_Wv, L1_attn_bv, L1_attn_Wu, L1_attn_bu)
    h = h + _L1_ffn_ref(_layernorm(h, axis=-1), L1_ffn_Wr, L1_ffn_br, L1_ffn_ln_g, L1_ffn_ln_b, L1_ffn_W1, L1_ffn_b1, L1_ffn_W2, L1_ffn_b2)
    h = h + _L2_attn_ref(_layernorm(h, axis=-1), L2_attn_ln_gamma, L2_attn_ln_beta, L2_attn_Wq, L2_attn_bq, L2_attn_Wk, L2_attn_bk, L2_attn_Wv, L2_attn_bv, L2_attn_Wpos, L2_attn_bpos, L2_attn_Wo, L2_attn_bo, L2_attn_u_bias, L2_attn_v_bias)
    h = h + _L2_ffn_ref(_layernorm(h, axis=-1), L2_ffn_w1s, L2_ffn_b1s, L2_ffn_w2s, L2_ffn_b2s)
    h = h + _L3_attn_ref(_layernorm(h, axis=-1))
    h = h + _L3_ffn_ref(_layernorm(h, axis=-1), L3_ffn_ln1_w, L3_ffn_ln2_w, L3_ffn_wq, L3_ffn_wk, L3_ffn_wv, L3_ffn_wo, L3_ffn_router_w, L3_ffn_w1, L3_ffn_w2, L3_ffn_w3)
    return h

_drawn_inputs = setup_inputs


def setup_inputs(seed=0):
    import zlib

    import numpy as np

    out = dict(_drawn_inputs(seed))
    spreads = {'L0_tok_bias': (0.0, 0.1),
     'L0_ffn_b1': (0.0, 0.8),
     'L0_ffn_b2': (0.0, 0.643),
     'L1_attn_bq': (0.0, 0.8),
     'L1_attn_bk': (0.0, 0.8),
     'L1_attn_bv': (0.0, 0.1),
     'L1_attn_bu': (0.0, 0.1),
     'L1_ffn_br': (0.0, 0.1),
     'L1_ffn_ln_g': (1.0, 0.2),
     'L1_ffn_ln_b': (0.0, 0.1),
     'L1_ffn_b1': (0.0, 0.1),
     'L1_ffn_b2': (0.0, 0.1),
     'L2_attn_ln_gamma': (1.0, 0.2),
     'L2_attn_ln_beta': (0.0, 0.1),
     'L2_attn_bq': (0.0, 0.354),
     'L2_attn_bk': (0.0, 0.8),
     'L2_attn_bv': (0.0, 0.1),
     'L2_attn_bpos': (0.0, 0.8),
     'L2_attn_bo': (0.0, 0.1),
     'L2_ffn_b1s': (0.0, 0.1),
     'L2_ffn_b2s': (0.0, 0.1),
     'L3_ffn_ln1_w': (1.0, 0.6),
     'L3_ffn_ln2_w': (1.0, 0.6)}
    factors = {'L0_ffn_wr': 3.906,
     'L0_ffn_w1': 8.0,
     'L0_ffn_w2': 8.0,
     'L1_attn_Wq': 8.0,
     'L1_attn_Wk': 8.0,
     'L2_attn_u_bias': 4.431,
     'L2_attn_v_bias': 8.0,
     'L3_ffn_wq': 8.0,
     'L3_ffn_wk': 8.0,
     'L3_ffn_wv': 8.0,
     'L3_ffn_wo': 8.0,
     'L3_ffn_router_w': 8.0,
     'L3_ffn_w1': 8.0,
     'L3_ffn_w2': 8.0,
     'L3_ffn_w3': 8.0}
    for name, (base, spread) in spreads.items():
        noise = np.random.default_rng([zlib.crc32(name.encode()), seed]).standard_normal(out[name].shape)
        drawn = base * np.exp(spread * noise) if base else spread * noise
        out[name] = jnp.asarray(drawn.astype(out[name].dtype))
    for name, factor in factors.items():
        out[name] = (out[name] * factor).astype(out[name].dtype)
    return out
```

```python
import math
from contextlib import ExitStack

import concourse.bass as bass
import numpy as np
from concourse import mybir

P = 128
D = 64
F32 = mybir.dt.float32
BF16 = mybir.dt.bfloat16
I32 = mybir.dt.int32
U32 = mybir.dt.uint32
ALU = mybir.AluOpType
ACT = mybir.ActivationFunctionType
X = mybir.AxisListType.X
ds = bass.ds

N_IMG = 64
IMG_H = IMG_W = 112
PATCH_H, PATCH_W, PATCH_STEP = 64, 25, 12
SEQ = (IMG_W - PATCH_W) // PATCH_STEP + 1
T = N_IMG * SEQ
Q = T // P
GRP = P // SEQ
HEADS4, HD, HPAD = 4, 16, 32
MAX_REL = 30
NE = 8
NODES = 255
PARENTS = NODES // 2
HID3 = int(8 / 3 * D)
TAIL = HID3 - P
RSQRT_MAGIC = 1597463007.0
BIG = 1e30


def shape_constants():
    inv_freq = 1.0 / 10000.0 ** (np.arange(0, HD, 2, dtype=np.float32) / HD)
    freqs = np.outer(np.arange(SEQ, dtype=np.float32), inv_freq)
    emb = np.concatenate([freqs, freqs], axis=-1).astype(np.float32)
    rope = np.zeros((P, 2, SEQ), np.float32)
    for h in range(HEADS4):
        rope[h * HPAD:h * HPAD + HD, 0] = np.cos(emb).T
        rope[h * HPAD:h * HPAD + HD, 1] = np.sin(emb).T
    n = 2 * MAX_REL + 1
    div = np.exp(np.arange(0, D, 2, dtype=np.float32) * np.float32(-math.log(10000.0) / D))
    ang = (np.arange(n, dtype=np.float32)[:, None] * div).astype(np.float32)
    enc = np.stack([np.sin(ang), np.cos(ang)], axis=-1).reshape(n, D).astype(np.float32)
    rel = np.ones((D + 1, 2 * SEQ), np.float32)
    rel[:D, 2 * SEQ - 1] = 0.0
    rel[:D, :2 * SEQ - 1] = enc[MAX_REL - SEQ + 1:MAX_REL + SEQ].T
    return rope, rel


def bc(ap, axis, n):
    ap = ap.unsqueeze(axis)
    shape = list(ap.shape)
    shape[axis] = n
    return ap.broadcast_to(tuple(shape))


def vit_tower(nc, a, rope_dram, rel_dram, out):
    ctx = ExitStack()
    with ctx:
        ctx.enter_context(nc.allow_non_contiguous_dma("weights in layouts of their own"))
        sems = {}
        STEPS = {
            "normed": ("x1_ready", "x2_ready", "x3_ready", "x4_ready", "x4n_ready", "x5_ready", "x5n_ready",
                       "x6_ready", "x7_ready", "f7_ready", "c7_ready", "x8_ready", "x8n_ready", "x9n_ready"),
            "features_tr": ("x1_tr", "x2_tr", "x3_tr", "x4_tr", "x4n_tr", "x5n_tr", "x6_tr", "f7_tr", "x8n_tr",
                            "x9n_tr"),
            "features_by_act": ("x1t_ready", "x2t_ready", "x3t_ready", "x4t_ready", "x4nt_ready", "x6t_ready",
                                "f7t_ready"),
            "features_by_dve": ("x5nt_ready", "x8nt_ready", "x9nt_ready"),
        }
        STEP = {name: (counter, n) for counter, names in STEPS.items() for n, name in enumerate(names)}

        def nth(name, value=1):
            return sem(name), value + (STEP[name][1] if name in STEP else 0)

        def sem(name):
            name = STEP[name][0] if name in STEP else name
            if name not in sems:
                sems[name] = ctx.enter_context(nc.semaphore(name))
            return sems[name]

        def sb(name, shape, dt=F32):
            return ctx.enter_context(nc.sbuf_tensor(name, shape, dt))

        bank = [ctx.enter_context(nc.psum_tensor(f"bank{i}", [P, 512], F32)) for i in range(8)]

        def tiles(b, n=D):
            return bank[b][:, 0:Q * n].rearrange("p (q n) -> p q n", q=Q)

        def views(region, *shapes):
            at = 0
            for shape in shapes:
                n = int(np.prod(shape))
                names = " ".join("abc"[:len(shape)])
                yield region[:, at:at + n].rearrange(f"p ({names}) -> p {names}", **dict(zip("abc", shape)))
                at += n

        region_a = sb("region_a", [P, N_IMG * IMG_W])
        region_b = sb("region_b", [P, 3 * 4 * T])
        region_c = sb("region_c", [P, PATCH_W * D])
        imgs, = views(region_a, (N_IMG, IMG_W))
        tacc, esim, silu, picked = views(region_a, (Q, 512), (Q, T), (4, T), (2, 512))
        silu = silu.rearrange("p (s c) t -> p s c t", s=2)
        qt0, att0 = region_b[0:D, 0:T], region_b[:, T:2 * T].rearrange("p (q n) -> p q n", q=Q)
        qt1, kt1, v1 = views(region_b, (4, T), (4, T), (Q, 512))
        xsplit_t, right, pathw = views(region_b, (7, T), (Q, 256), (Q, 256))
        tok_w, = views(region_c, (PATCH_W, D))
        masked, ranks = views(region_c, (2, 512), (2, Q * NE * NE))
        ident = sb("ident", [P, P])
        same = sb("same", [P, GRP])
        same_tok = sb("same_tok", [P, P])
        same_lt = sb("same_lt", [P, P])
        pos1h = sb("pos1h", [P, SEQ])
        before = sb("before", [P, SEQ])
        strict_bias = sb("strict_bias", [P, SEQ])
        causal_bias = sb("causal_bias", [P, SEQ])
        not_first = sb("not_first", [P, 1])
        lower8 = sb("lower8", [P, NE, NE])
        ones_row = sb("ones_row", [P, P])
        rope = sb("rope", [P, 2, SEQ])
        rel = sb("rel", [D + 1, 2 * SEQ])
        tok_b = sb("tok_b", [1, D])
        a0_w = sb("a0_w", [D, D])
        f0_wr = sb("f0_wr", [D + 1, 1])
        f0_w1 = sb("f0_w1", [D, 256])
        f0_w2 = sb("f0_w2", [P, 2, D])
        f0_b2 = sb("f0_b2", [1, D])
        rows128 = sb("rows128", [2 + 2 * NE, P])
        cols128 = sb("cols128", [P, 2 + 2 * NE])
        rows64 = sb("rows64", [2 * NE + 4, D])
        cols64 = sb("cols64", [D, 2 * NE + 4])
        a1_w = sb("a1_w", [D + 1, 3, 512])
        a1_wu = sb("a1_wu", [P, 4, D])
        a1_bu = sb("a1_bu", [1, D])
        f1_wr = sb("f1_wr", [D + 1, NE])
        f1_w1 = sb("f1_w1", [D, 2, 256])
        f1_w2 = sb("f1_w2", [P, 2, 2, D])
        f1_b2 = sb("f1_b2", [NE, D])
        wnat = sb("wnat", [D, 8, D])
        wo_pad = sb("wo_pad", [D, 2, P])
        wt = sb("wt", [D + 1, 9, P])
        wt_v3 = sb("wt_v3", [D + 1, P])
        uv_rows = sb("uv_rows", [D + 1, 2, D])
        wo_t = sb("wo_t", [P, 2, D])
        bo2 = sb("bo2", [1, D])
        router_t = sb("router_t", [D, NE])
        w1s_nat = sb("w1s_nat", [P, 2, D])
        w1s_t = sb("w1s_t", [D + 1, 256])
        b2s = sb("b2s", [P, 2, D])
        w2s = sb("w2s", [P, PARENTS, D])
        w2root = sb("w2root", [D, D])
        NB13 = -(-NE * HID3 // P)
        w13_nat = sb("w13_nat", [P, 2, NB13, D])
        w13_t = sb("w13_t", [D, 2, NB13 * P])
        w2e_nat = sb("w2e_nat", [P, NE // 2, HID3])
        w2e_t = sb("w2e_t", [P, 2, NE * D])
        e3_slot = sb("e3_slot", [D, 2, 3 * P])
        hs = [sb(f"h{i}", [P, Q, D]) for i in range(2)] * 4
        xs = [sb(f"x{i}", [P, Q, D]) for i in range(2)] * 4
        xc = sb("xc", [P, Q, D])
        sq = sb("sq", [P, Q, D])
        st = sb("st", [P, 8, Q])
        xt = [sb(f"xt{i}", [D + 1, T]) for i in range(3)]
        xt = [xt[i % 3] for i in range(10)]
        inner = sb("inner", [P, Q, D])
        small = sb("small", [P, 8, Q * NE])
        ht = sb("ht", [P, 2, 2, T])
        comp = sb("comp", [P, 32, SEQ])
        cexp = sb("cexp", [P, 32, SEQ])
        wide = sb("wide", [P, 2, 512])
        att_t = sb("att_t", [P, 2, 512])
        out_t = sb("out_t", [P, 4, T])
        onehot = out_t[:, 2:4, :].rearrange("p a (b n) -> p (a b) n", n=256)
        gates = sb("gates", [P, 2, Q, NE])
        gates_t = sb("gates_t", [NE, T])
        xe = sb("xe", [D, 2, T])
        yacc = sb("yacc", [P, Q, D])
        ytmp = sb("ytmp", [P, 2, Q, D])
        posadd = sb("posadd", [P, Q * HEADS4, SEQ])
        pos_bd = sb("pos_bd", [P, HEADS4, 2 * SEQ])
        qk4 = sb("qk4", [P, 4, T])
        v4 = sb("v4", [P, Q, P])
        pairw = v4
        xsplit = qk4[:, 0:2, :].rearrange("p b (q s d) -> p b q s d", q=Q, s=2)
        pathw_t = qk4[:, 2:4, :]
        went_right = sb("went_right", [P, 8, Q])
        fn = sb("fn", [P, Q, D + 1])
        outb = sb("outb", [P, Q, D])

        block = ctx.enter_context(nc.Block())
        def first_round(i):
            return isinstance(i, int) and i == 0

        def over_experts(eng, step):
            step(0, 0)
            step(0, 1)
            with eng.Fori(1, NE // 2) as i:
                step(i, 0)
                step(i, 1)

        CHUNKS = ((6, 8), (5, 4), (4, 2), (3, 1), (None, 1))

        def over_chunks(eng, step):
            n = 0
            for level, count in CHUNKS:
                step(0, level, n)
                if count > 1:
                    with eng.Fori(1, count) as i:
                        step(i, level, n)
                n += count

        W = {}

        @block.sync
        def _(sp):
            def load(name, dst, src):
                W[name] = W.get(name, 0) + 16
                sp.dma_start(dst, src).then_inc(sem(name), 16)

            patch_rows = a["x"][:, 0, 0:PATCH_H, :].rearrange("b r w -> r b w")
            tw = a["L0_tok_weight"].rearrange("(r c) d -> r c d", c=PATCH_W)
            load("tok_w_in", tok_w[0:PATCH_H, :, :], tw)
            load("tok_w_in", tok_w[PATCH_H:P, 0:PATCH_W - 1, :], tw[:, 1:PATCH_W, :])
            load("tok_w_in", tok_b[:, :], a["L0_tok_bias"].unsqueeze(0))
            for q in range(Q):
                mine = slice(q * GRP, (q + 1) * GRP)
                load(f"img_in{q}", imgs[0:PATCH_H, mine, :], patch_rows[:, mine, :])
                load(f"img_in{q}", imgs[PATCH_H:P, mine, 0:IMG_W - 1], patch_rows[:, mine, 1:IMG_W])
            load("l0_in", a0_w[:, :], a["L0_attn_q_weight"])
            load("l0_in", f0_wr[0:D, :], a["L0_ffn_wr"])
            load("l0_in", f0_wr[D:D + 1, :], a["L0_ffn_br"].unsqueeze(0))
            load("l0_in", f0_w1[:, :], a["L0_ffn_w1"])
            load("l0_in", f0_w2[:, :, :], a["L0_ffn_w2"].rearrange("(c k) d -> k c d", c=2))
            load("l0_in", f0_b2[:, :], a["L0_ffn_b2"].unsqueeze(0))
            load("rows_in", rows128[0:2, :], a["L0_ffn_b1"].rearrange("(c k) -> c k", c=2))
            load("rows_in", rows128[2:2 + 2 * NE, :], a["L1_ffn_b1"].rearrange("e (c k) -> (e c) k", c=2))
            load("rows_in", rows64[0:NE, :], a["L1_ffn_ln_g"])
            load("rows_in", rows64[NE:2 * NE, :], a["L1_ffn_ln_b"])
            for i, n in enumerate(("L2_attn_ln_gamma", "L2_attn_ln_beta", "L3_ffn_ln1_w", "L3_ffn_ln2_w")):
                load("rows_in", rows64[2 * NE + i:2 * NE + i + 1, :], a[n].unsqueeze(0))
            for i, n in enumerate("qkv"):
                load("l1_in", a1_w[0:D, i, :], a[f"L1_attn_W{n}"])
                load("l1_in", a1_w[D:D + 1, i, :], a[f"L1_attn_b{n}"].unsqueeze(0))
            load("l1_in", a1_wu[:, :, :], a["L1_attn_Wu"].rearrange("(c k) d -> k c d", c=4))
            load("l1_in", a1_bu[:, :], a["L1_attn_bu"].unsqueeze(0))
            load("l1_in", f1_wr[0:D, :], a["L1_ffn_Wr"])
            load("l1_in", f1_wr[D:D + 1, :], a["L1_ffn_br"].unsqueeze(0))
            load("l1_in", f1_b2[:, :], a["L1_ffn_b2"])

            load("heads_in", rope[:, :, :], rope_dram)
            load("heads_in", rel[:, :], rel_dram)
            for i, n in enumerate(("L2_attn_Wq", "L2_attn_Wk", "L2_attn_Wv", "L2_attn_Wpos")):
                load("heads_in", wnat[:, i, :], a[n])
            for i, (n, r) in enumerate((("L3_ffn_wq", D), ("L3_ffn_wk", D // 2), ("L3_ffn_wv", D // 2),
                                        ("L3_ffn_router_w", NE))):
                load("heads_in", wnat[0:r, 4 + i, :], a[n])
            sp.wait_ge(sem("pads_zeroed"), 3)
            for i, n in enumerate(("L2_attn_Wo", "L3_ffn_wo")):
                load("heads_in", wo_pad[:, i, :].rearrange("o (h d) -> o h d", h=HEADS4)[:, :, 0:HD],
                     a[n].rearrange("o (h d) -> o h d", h=HEADS4))
            for i, n in ((2, "k"), (3, "v"), (4, "pos")):
                load("heads_in", wt[D:D + 1, i, :].rearrange("o (h d) -> o h d", h=HEADS4)[:, :, 0:HD],
                     a[f"L2_attn_b{n}"].rearrange("(o h d) -> o h d", o=1, h=HEADS4))
            load("heads_in", uv_rows[D:D + 1, 0, :], a["L2_attn_bq"].unsqueeze(0))
            for i, n in ((0, "u"), (1, "v")):
                load("heads_in", wt[D:D + 1, i, :].rearrange("o (h d) -> o h d", h=HEADS4)[:, :, 0:HD],
                     a[f"L2_attn_{n}_bias"].rearrange("o h a d -> o (h a) d"))
            load("heads_in", bo2[:, :], a["L2_attn_bo"].unsqueeze(0))

            load("tree_in", w1s_nat[:, 0, :], a["L2_ffn_w1s"][0:P, :])
            load("tree_in", w1s_nat[0:NODES - P, 1, :], a["L2_ffn_w1s"][P:NODES, :])
            load("tree_in", w1s_t[D:D + 1, 0:NODES], a["L2_ffn_b1s"].unsqueeze(0))
            load("tree_in", b2s[:, 0, :], a["L2_ffn_b2s"][0:P, :])
            load("tree_in", b2s[0:NODES - P, 1, :], a["L2_ffn_b2s"][P:NODES, :])

            rows = (NE * HID3) // P
            for i, n in enumerate(("w1", "w3")):
                flat = a[f"L3_ffn_{n}"].rearrange("e h c -> (e h) c")
                load("moe3_in", w13_nat[:, i, 0:rows, :], flat[0:rows * P, :].rearrange("(k p) c -> p k c", p=P))
                load("moe3_in", w13_nat[0:NE * HID3 - rows * P, i, rows, :], flat[rows * P:NE * HID3, :])
            load("moe3_in", w2e_nat[:, :, :], a["L3_ffn_w2"].rearrange("(k e) c h -> (e c) k h", e=2))
            def load_expert(i, s):
                e = i * 2 + s
                if not first_round(i):
                    sp.wait_ge(sem("f1_down"), e - 1)
                sp.dma_start(f1_w1[:, s, :], a["L1_ffn_W1"][ds(e, 1), :, :].rearrange("e d h -> (e d) h"))\
                  .then_inc(sem(f"f1_w_in{s}"), 16)
                sp.dma_start(f1_w2[:, s, :, :],
                             a["L1_ffn_W2"][ds(e, 1), :, :].rearrange("e (c k) d -> k (e c) d", c=2))\
                  .then_inc(sem(f"f1_w_in{s}"), 16)

            over_experts(sp, load_expert)

            sp.wait_ge(sem("h8_ready"), 1)
            sp.dma_start(out.rearrange("(q g) n d -> (g n) q d", q=Q), outb[:, :, :]).then_inc(sem("out_done"), 16)
            sp.wait_ge(sem("out_done"), 16)

        @block.gpsimd
        def _(pool):
            made = [0]

            def link(ins):
                made[0] += 1
                ins.then_inc(sem("pool_step"), 1)
                pool.wait_ge(sem("pool_step"), made[0])

            pool.memset(wo_pad[:, :, :], 0.0).then_inc(sem("pads_zeroed"), 1)
            pool.memset(wt[:, :, :], 0.0).then_inc(sem("pads_zeroed"), 1)
            pool.memset(wt_v3[:, :], 0.0).then_inc(sem("pads_zeroed"), 1)
            pool.memset(ones_row[:, :], 1.0).then_inc(sem("ones_ready"), 1)
            link(pool.memset(ident[:, :], 0.0))
            pool.affine_select(out=ident[:, :], in_=ident[:, :], compare_op=ALU.not_equal, fill=1.0, base=0,
                               pattern=[[-1, P]], channel_multiplier=1).then_inc(sem("ident_ready"), 1)
            link(pool.memset(same[:, :], 1.0))
            link(pool.affine_select(out=same[:, :], in_=same[:, :], compare_op=ALU.is_ge, fill=0.0, base=0,
                                    pattern=[[-SEQ, GRP]], channel_multiplier=1))
            link(pool.affine_select(out=same[:, :], in_=same[:, :], compare_op=ALU.is_ge, fill=0.0,
                                    base=SEQ - 1, pattern=[[SEQ, GRP]], channel_multiplier=-1))
            pool.tensor_copy(same_tok[:, :].rearrange("p (g j) -> p g j", g=GRP), bc(same[:, :], 2, SEQ))\
                .then_inc(sem("same_ready"), 1)
            pool.wait_ge(sem("same_ready"), 1)
            pool.affine_select(out=same_lt[:, :], in_=same_tok[:, :], compare_op=ALU.is_gt, fill=0.0, base=0,
                               pattern=[[-1, P]], channel_multiplier=1).then_inc(sem("same_lt_ready"), 1)
            link(pool.memset(lower8[:, :, :], 1.0))
            pool.affine_select(out=lower8[:, :, :], in_=lower8[:, :, :], compare_op=ALU.is_gt, fill=0.0, base=0,
                               pattern=[[1, NE], [-1, NE]], channel_multiplier=0)\
                .then_inc(sem("lower8_ready"), 1)
            pool.memset(pos_bd[:, :, :], 0.0).then_inc(sem("pos_bd_zeroed"), 1)
            pool.memset(e3_slot[:, :, :], 0.0).then_inc(sem("e3_slot_zeroed"), 1)
            pool.memset(fn[:, :, D:D + 1], 1.0).then_inc(sem("fn_ones"), 1)
            pool.wait_ge(sem("tok_mm"), 1)
            for q in range(Q):
                pool.memset(tacc[:, q, :], 0.0).then_inc(sem("tacc_step"), 1)

            def add_picked(i, level, n):
                for q in range(Q):
                    unit = (i + n) * Q + q
                    pool.wait_ge(sem("picked"), unit + 1)
                    pool.wait_ge(sem("tacc_step"), unit + 1)
                    pool.tensor_tensor(tacc[:, q, :], tacc[:, q, :], picked[:, q % 2, :], ALU.add)\
                        .then_inc(sem("tacc_step"), 1)

            over_chunks(pool, add_picked)

            pool.wait_ge(sem("w13_t_ready"), 6)
            pool.wait_ge(sem("e3_slot_zeroed"), 1)

            def fill_slot(i, s):
                e = i * 2 + s
                if not first_round(i):
                    pool.wait_ge(sem("f3_up"), e * 3 - 3)
                for j in range(2):
                    pool.tensor_copy(e3_slot[:, s, j * P:(j + 1) * P], w13_t[:, j, ds(e * HID3, P)])\
                        .then_inc(sem(f"e3_slot_in{s}"), 1)
                    pool.tensor_copy(e3_slot[:, s, 2 * P + j * D:2 * P + j * D + TAIL],
                                     w13_t[:, j, ds(e * HID3 + P, TAIL)]).then_inc(sem(f"e3_slot_in{s}"), 1)

            over_experts(pool, fill_slot)

        @block.scalar
        def _(act):
            def evac(dst, src, wait, value, done, func=ACT.Copy, **kw):
                act.wait_ge(*nth(wait, value))
                return act.activation(dst, src, func, **kw).then_inc(sem(done), 1)

            evac(qt0[:, :], bank[0][0:D, :], "tok_mm", 1, "h0t_ready", ACT.Gelu)
            evac(hs[0][:, :, :], tiles(5), "h0_tr", 1, "h0_ready")
            for side in range(2):
                act.dma_start(w2s[side * D:(side + 1) * D, :, :],
                              a["L2_ffn_w2s"][1:NODES, :, :].rearrange("(m s) d o -> s d m o", s=2)[side])\
                   .then_inc(sem("w2s_in"), 16)
            act.dma_start(w2root[:, :], a["L2_ffn_w2s"][0, :, :]).then_inc(sem("w2s_in"), 16)
            evac(cols128[:, :], bank[1][:, 0:2 + 2 * NE], "rows_mm", 1, "cols_ready")
            evac(cols64[:, :], bank[1][0:D, 64:64 + 2 * NE + 4], "rows_mm", 1, "cols_ready")
            evac(xt[0][0:D, :], bank[2][0:D, :], "x1_tr", 1, "x1t_ready")
            evac(qt0[:, :], bank[3][0:D, :], "q0_mm", 1, "qt0_ready")
            evac(att0[:, :, :], tiles(4, P), "s0_mm", 1, "sig_ready", ACT.Sigmoid)
            act.wait_ge(sem("heads_tr"), 1)
            act.wait_ge(sem("pads_zeroed"), 3)
            hv = lambda ap: ap.rearrange("p (h d) -> p h d", h=HEADS4)
            tr = lambda i: bank[6][0:D, i * D:(i + 1) * D].rearrange("p (h d) -> p h d", d=HD)
            for slot, i in ((0, 0), (1, 0), (2, 1), (3, 2), (4, 3), (5, 4)):
                act.activation(hv(wt[0:D, slot, :])[:, :, 0:HD], tr(i), ACT.Copy).then_inc(sem("heads_w"), 1)
            half = HD // 2
            act.activation(hv(wt[0:D, 6, :])[:, :, 0:half], tr(4)[:, :, half:HD], ACT.Copy, scale=-1.0)\
                .then_inc(sem("heads_w"), 1)
            act.activation(hv(wt[0:D, 6, :])[:, :, half:HD], tr(4)[:, :, 0:half], ACT.Copy)\
                .then_inc(sem("heads_w"), 1)
            for rep in range(2):
                two = lambda ap: ap.rearrange("p (k r d) -> p k r d", k=2, r=2)[:, :, rep, :]
                k3, v3 = (bank[6][0:D, i * D:i * D + 32].rearrange("p (k d) -> p k d", k=2) for i in (5, 6))
                act.activation(two(wt[0:D, 7, :])[:, :, 0:HD], k3, ACT.Copy).then_inc(sem("heads_w"), 1)
                act.activation(two(wt[0:D, 8, :])[:, :, 0:half], k3[:, :, half:HD], ACT.Copy, scale=-1.0)\
                    .then_inc(sem("heads_w"), 1)
                act.activation(two(wt[0:D, 8, :])[:, :, half:HD], k3[:, :, 0:half], ACT.Copy)\
                    .then_inc(sem("heads_w"), 1)
                act.activation(two(wt_v3[0:D, :])[:, :, 0:HD], v3, ACT.Copy).then_inc(sem("heads_w"), 1)
            act.activation(router_t[:, :], bank[6][0:D, 7 * D:7 * D + NE], ACT.Copy).then_inc(sem("heads_w"), 1)
            act.activation(wo_t[:, :, :], bank[7][:, 0:2 * D].rearrange("p (i o) -> p i o", i=2), ACT.Copy)\
                .then_inc(sem("heads_w"), 1)

            evac(xt[1][0:D, :], bank[2][0:D, :], "x2_tr", 1, "x2t_ready")
            for c in range(2):
                evac(ht[:, 0, c, :], bank[3 + c][:, :], "f0_mm", c + 1, "f0_ready", ACT.Gelu_apprx_tanh,
                     bias=cols128[:, c:c + 1])

            evac(xt[2][0:D, :], bank[2][0:D, :], "x3_tr", 1, "x3t_ready")
            for c in range(4):
                evac(qt1[:, c, :], bank[c][:, :], "q1_mm", c + 1, "qt1_ready")
            for q in range(Q):
                evac(v1[:, q, :], bank[q][:, :], "v1_mm", q + 1, "v1_ready")
            evac(cexp[:, :, :], comp[:, :, :], "a1_shifted", 1, "a1_exp", ACT.Exp, scale=1.0 / 8.0)
            for b in range(8):
                if b >= 2:
                    act.wait_ge(sem("a1_av"), b - 1)
                evac(att_t[:, b % 2, :], bank[4 + b % 4][:, :], "a1_tr", b + 1, "a1_att_t")
            for c in range(4):
                evac(out_t[:, c, :], bank[c][:, :], "a1_av", 8, "a1_out")

            evac(xt[3][0:D, :], bank[2][0:D, :], "x4_tr", 1, "x4t_ready")
            evac(small[:, 0, 0:Q * NE].rearrange("p (q e) -> p q e", q=Q),
                 small[:, 1, 0:Q * NE].rearrange("p (q e) -> p q e", q=Q), "r1_shifted", 1, "r1_exp", ACT.Exp)
            evac(xt[4][0:D, :], bank[1][0:D, :], "x4n_tr", 1, "x4nt_ready")

            def gelu1(i, s):
                e = i * 2 + s
                if not first_round(i):
                    act.wait_ge(sem("f1_down"), e - 1)
                for c in range(2):
                    evac(ht[:, s, c, :], bank[4 + 2 * s + c][:, :], "f1_up", e * 2 + (c + 1), "f1_ht",
                         ACT.Gelu, bias=cols128[:, ds(e * 2 + (2 + c), 1)])

            over_experts(act, gelu1)
            evac(gates_t[:, :], bank[3][0:NE, :], "g1_tr", 1, "g1t_ready")

            for c in range(3):
                evac(qk4[:, c, :], bank[3 + c][:, :], "qk2_mm", c + 1, "qk2_ready")
            evac(v4[:, :, :], tiles(6, P), "qk2_mm", 4, "qk2_ready")
            act.wait_ge(sem("pos_mm"), 1)
            act.wait_ge(sem("pos_bd_zeroed"), 1)
            for h in range(HEADS4):
                mine = slice(h * HPAD, h * HPAD + HD)
                act.activation(pos_bd[mine, h, :], bank[7][mine, 0:2 * SEQ], ACT.Copy)\
                    .then_inc(sem("pos_bd_ready"), 1)

            def attention4(name):
                evac(cexp[:, 0:16, :], comp[:, 0:16, :], f"{name}_shifted", 1, f"{name}_exp", ACT.Exp, scale=0.25)
                for q in range(Q):
                    if q >= 2:
                        act.wait_ge(sem(f"{name}_av"), q - 1)
                    evac(att_t[:, q % 2, :], bank[4 + q % 2][:, :], f"{name}_tr", q + 1, f"{name}_att_t")
                evac(out_t[:, 0, :], bank[6][:, :], f"{name}_av", 4, f"{name}_out")

            attention4("a2")

            evac(w1s_t[0:D, 0:NODES], bank[3][0:D, 0:NODES], "w1s_tr", 1, "w1s_ready")
            evac(xt[6][0:D, :], bank[2][0:D, :], "x6_tr", 1, "x6t_ready")
            for c in range(2):
                evac(right[:, 2 * c:2 * c + 2, 0:NODES],
                     bank[c][:, :].rearrange("p (q n) -> p q n", q=2)[:, :, 0:NODES], "tree_choice", c + 1,
                     "tree_abs", ACT.Abs)
            for c in range(2):
                evac(pathw[:, 2 * c:2 * c + 2, 0:NODES], right[:, 2 * c:2 * c + 2, 0:NODES], "tree_abs", c + 1,
                     "tree_gelu", ACT.Gelu)
            for lv in range(1, 8):
                evac(xsplit_t[:, lv - 1, :], bank[4 + lv % 2][:, :], "split_tr", lv, "split_t")
            for c, n in ((0, P), (1, NODES - P)):
                evac(pathw_t[0:n, c, :], bank[4 + c][0:n, :], "pathw_tr", c + 1, "pathw_t")
            for j in range(2):
                for g in range(3):
                    n = min(512, NE * HID3 - 512 * g)
                    evac(w13_t[:, j, g * 512:g * 512 + n], bank[4 + g][0:D, 0:n], "w13_tr", 3 * j + g + 1,
                         "w13_t_ready")
            for c, n in ((0, P), (1, TAIL)):
                evac(w2e_t[0:n, c, :], bank[4 + c][0:n, :], "w2e_tr", c + 1, "w2e_t_ready")

            evac(xt[7][0:D, :], bank[2][0:D, :], "f7_tr", 1, "f7t_ready")
            for q in range(Q):
                evac(esim[:, q, :], bank[3 + q][:, :], "sim_mm", q + 1, "sim_exp", ACT.Exp)

            evac(v4[:, :, :], tiles(7, P), "qk3_mm", 5, "v3_ready")
            attention4("a3")
            evac(small[:, 0, 0:Q * NE].rearrange("p (q e) -> p q e", q=Q),
                 small[:, 1, 0:Q * NE].rearrange("p (q e) -> p q e", q=Q), "r3_shifted", 1, "r3_exp", ACT.Exp)

            def silu3(i, s):
                e = i * 2 + s
                if not first_round(i):
                    act.wait_ge(sem("f3_ht"), e * 2 - 2)
                evac(silu[:, s, 0, :], bank[3 * s][:, :], "f3_up", e * 3 + 1, "f3_silu", ACT.Silu)
                evac(silu[0:TAIL, s, 1, :], bank[3 * s + 2][0:TAIL, :], "f3_up", e * 3 + 3, "f3_silu", ACT.Silu)

            over_experts(act, silu3)

        @block.vector
        def _(dve):
            made = [0]

            def link(ins):
                made[0] += 1
                ins.then_inc(sem("dve_step"), 1)
                dve.wait_ge(sem("dve_step"), made[0])

            def rsqrt(v):
                y, t = st[:, 5, :], st[:, 6, :]
                link(dve.tensor_scalar(t.bitcast(U32), v.bitcast(U32), 1, None, ALU.logical_shift_right))
                link(dve.tensor_scalar(y.bitcast(I32), t.bitcast(I32), -1.0, RSQRT_MAGIC, ALU.mult, ALU.add))
                for _ in range(3):
                    link(dve.scalar_tensor_tensor(out=t, in0=y, scalar=-0.5, in1=v, op0=ALU.mult, op1=ALU.mult))
                    link(dve.tensor_tensor(t, t, y, ALU.mult))
                    link(dve.scalar_tensor_tensor(out=y, in0=t, scalar=1.5, in1=y, op0=ALU.add, op1=ALU.mult))
                return y

            def layernorm(src, dst, done):
                link(dve.reduce_sum(st[:, 0, :], src, axis=X))
                link(dve.tensor_scalar(st[:, 1, :], st[:, 0, :], -1.0 / D, None, ALU.mult))
                link(dve.tensor_tensor(xc[:, :, :], src, bc(st[:, 1, :], 2, D), ALU.add))
                link(dve.tensor_tensor(sq[:, :, :], xc[:, :, :], xc[:, :, :], ALU.mult))
                link(dve.reduce_sum(st[:, 2, :], sq[:, :, :], axis=X))
                link(dve.tensor_scalar(st[:, 3, :], st[:, 2, :], 1.0 / D, 1e-5, ALU.mult, ALU.add))
                r = rsqrt(st[:, 3, :])
                dve.tensor_tensor(dst, xc[:, :, :], bc(r, 2, D), ALU.mult).then_inc(sem(done), 1)
                dve.wait_ge(*nth(done))

            def scaled_by_rms(src, dst, scale, shift, least, done):
                link(dve.tensor_tensor(sq[:, :, :], src, src, ALU.mult))
                link(dve.reduce_sum(st[:, 2, :], sq[:, :, :], axis=X))
                if shift:
                    link(dve.tensor_scalar(st[:, 3, :], st[:, 2, :], scale, shift, ALU.mult, ALU.add))
                else:
                    link(dve.tensor_scalar(st[:, 3, :], st[:, 2, :], least, None, ALU.max))
                r = rsqrt(st[:, 3, :])
                dve.tensor_tensor(dst, src, bc(r, 2, D), ALU.mult).then_inc(sem(done), 1)
                dve.wait_ge(*nth(done))

            for i in range(3):
                dve.memset(xt[i][D:D + 1, :], 1.0).then_inc(sem("bias_ones"), 1)
            dve.wait_ge(sem("ident_ready"), 1)
            dve.wait_ge(sem("same_lt_ready"), 1)
            by_pos = lambda m: m[:, :].rearrange("p (g j) -> p j g", g=GRP)
            link(dve.reduce_sum(pos1h[:, :], by_pos(ident), axis=X))
            link(dve.reduce_sum(before[:, :], by_pos(same_lt), axis=X))
            link(dve.tensor_scalar(not_first[:, :], pos1h[:, 0:1], -1.0, 1.0, ALU.mult, ALU.add))
            link(dve.tensor_scalar(strict_bias[:, :], pos1h[:, :], pos1h[:, 0:1], None, ALU.mult))
            link(dve.tensor_tensor(strict_bias[:, :], strict_bias[:, :], before[:, :], ALU.add))
            link(dve.tensor_scalar(strict_bias[:, :], strict_bias[:, :], BIG, -BIG, ALU.mult, ALU.add))
            link(dve.tensor_tensor(causal_bias[:, :], pos1h[:, :], before[:, :], ALU.add))
            link(dve.tensor_scalar(causal_bias[:, :], causal_bias[:, :], BIG, -BIG, ALU.mult, ALU.add))

            dve.wait_ge(sem("h0_ready"), 1)
            layernorm(hs[0][:, :, :], xs[0][:, :, :], "x1_ready")
            dve.wait_ge(sem("sig_ready"), 1)
            dve.tensor_tensor(att0[:, :, :], att0[:, :, :], bc(same_tok[:, :], 1, Q), ALU.mult)\
                .then_inc(sem("att0_ready"), 1)
            dve.wait_ge(sem("a0_mm"), 1)
            link(dve.tensor_tensor(hs[1][:, :, :], hs[0][:, :, :], tiles(5), ALU.add))
            layernorm(hs[1][:, :, :], xs[1][:, :, :], "x2_ready")

            sv = lambda i, n=SEQ: small[:, i, 0:Q * n].rearrange("p (q j) -> p q j", q=Q)
            dve.wait_ge(sem("wr_mm"), 1)
            link(dve.tensor_copy(st[:, 0, :], bank[5][:, 0:Q]))
            dve.tensor_tensor(sv(0), bc(pos1h[:, :], 1, Q), bc(st[:, 0, :], 2, SEQ), ALU.mult)\
                .then_inc(sem("wr_spread"), 1)
            dve.wait_ge(sem("wr_gather_mm"), 1)
            link(dve.tensor_copy(sv(1), bank[6][:, 0:Q * SEQ].rearrange("p (q j) -> p q j", q=Q)))
            link(dve.tensor_tensor(sv(2), sv(1), bc(pos1h[:, :], 1, Q), ALU.mult))
            link(dve.reduce_sum(st[:, 1, :], sv(2), axis=X))
            link(dve.tensor_tensor(sv(3), sv(1), bc(st[:, 1, :], 2, SEQ), ALU.is_gt))
            link(dve.tensor_tensor(sv(4), sv(1), bc(st[:, 1, :], 2, SEQ), ALU.is_equal))
            link(dve.tensor_tensor(sv(4), sv(4), bc(before[:, :], 1, Q), ALU.mult))
            link(dve.tensor_tensor(sv(3), sv(3), sv(4), ALU.add))
            link(dve.reduce_sum(st[:, 2, :], sv(3), axis=X))
            kept = max(1, SEQ // 2) - 1
            link(dve.scalar_tensor_tensor(out=st[:, 4, :], in0=st[:, 2, :], scalar=kept - 0.5, in1=st[:, 1, :],
                                          op0=ALU.is_lt, op1=ALU.mult))
            link(dve.tensor_tensor(hs[2][:, :, :], hs[1][:, :, :], xs[1][:, :, :], ALU.add))
            dve.wait_ge(sem("f0_down"), 1)
            link(dve.tensor_tensor(xc[:, :, :], tiles(7), bc(st[:, 4, :], 2, D), ALU.mult))
            link(dve.tensor_tensor(hs[2][:, :, :], hs[2][:, :, :], xc[:, :, :], ALU.add))
            layernorm(hs[2][:, :, :], xs[2][:, :, :], "x3_ready")

            def compact(n, b, name):
                dve.wait_ge(sem(f"{name}_mm"), n + 1)
                link(dve.tensor_tensor(masked[:, n % 2, :].rearrange("p (k g j) -> p k g j", k=4, g=GRP),
                                       bank[b][:, :].rearrange("p (k g j) -> p k g j", k=4, g=GRP),
                                       bc(bc(same[:, :], 2, SEQ), 1, 4), ALU.mult))
                dve.reduce_sum(comp[:, 4 * n:4 * n + 4, :],
                               masked[:, n % 2, :].rearrange("p (k g j) -> p k j g", k=4, g=GRP), axis=X)\
                    .then_inc(sem(f"{name}_comp"), 1)

            def softmax(nb, name, bias, extra=None, zero_first=False):
                c, e = comp[:, 0:nb, :], cexp[:, 0:nb, :]
                mx, sm = small[:, 2, 0:nb], small[:, 3, 0:nb]
                if extra is not None:
                    link(dve.tensor_tensor(c, c, extra, ALU.add))
                if bias is not None:
                    link(dve.tensor_tensor(c, c, bc(bias, 1, nb), ALU.add))
                link(dve.reduce_max(mx, c, axis=X))
                dve.tensor_tensor(c, c, bc(mx, 2, SEQ), ALU.subtract).then_inc(sem(f"{name}_shifted"), 1)
                dve.wait_ge(sem(f"{name}_exp"), 1)
                link(dve.reduce_sum(sm, e, axis=X))
                link(dve.reciprocal(mx, sm))
                if zero_first:
                    link(dve.tensor_scalar(mx, mx, not_first[:, :], None, ALU.mult))
                link(dve.tensor_tensor(c, e, bc(mx, 2, SEQ), ALU.mult))

            def spread(n, name):
                if n >= 2:
                    dve.wait_ge(sem(f"{name}_tr"), n - 1)
                dve.tensor_tensor(wide[:, n % 2, :].rearrange("p (k g j) -> p k g j", k=4, g=GRP),
                                  bc(comp[:, 4 * n:4 * n + 4, :], 2, GRP),
                                  bc(bc(same[:, :], 2, SEQ), 1, 4), ALU.mult).then_inc(sem(f"{name}_wide"), 1)

            dve.wait_ge(sem("heads_in"), W["heads_in"])
            for i in range(2):
                row = wt[D:D + 1, i, :].rearrange("o (h d) -> o h d", h=HEADS4)[:, :, 0:HD]
                dve.tensor_tensor(row, row, uv_rows[D:D + 1, 0, :].rearrange("o (h d) -> o h d", h=HEADS4), ALU.add)\
                    .then_inc(sem("heads_bias"), 1)

            for c in range(4):
                dve.wait_ge(sem("k1_mm"), c + 1)
                dve.tensor_copy(kt1[:, c, :], bank[4 + c][:, :]).then_inc(sem("kt1_ready"), 1)
            for n in range(8):
                compact(n, (4 + n) % 8, "s1")
            dve.wait_ge(sem("s1_comp"), 8)
            softmax(32, "a1", strict_bias[:, :], zero_first=True)
            for n in range(8):
                spread(n, "a1")
            dve.wait_ge(sem("a1_down"), 1)
            link(dve.tensor_tensor(hs[3][:, :, :], hs[2][:, :, :], tiles(4), ALU.add))

            def route(name, p_in, g, eps):
                probs, lg = small[:, 4, 0:Q * NE].rearrange("p (q e) -> p q e", q=Q), sv(1)
                mx, sm = small[:, 2, 0:Q], small[:, 3, 0:Q]
                link(dve.reduce_max(mx, p_in, axis=X))
                dve.tensor_tensor(lg, p_in, bc(mx, 2, NE), ALU.subtract).then_inc(sem(f"{name}_shifted"), 1)
                dve.wait_ge(sem(f"{name}_exp"), 1)
                link(dve.reduce_sum(sm, sv(0), axis=X))
                link(dve.reciprocal(mx, sm))
                link(dve.tensor_tensor(probs, sv(0), bc(mx, 2, NE), ALU.mult))
                cmp = [ranks[:, i, :].rearrange("p (q e f) -> p q e f", q=Q, e=NE) for i in range(2)]
                other, own = bc(probs, 2, NE), bc(probs, 3, NE)
                link(dve.tensor_tensor(cmp[0], other, own, ALU.is_gt))
                link(dve.tensor_tensor(cmp[1], other, own, ALU.is_equal))
                link(dve.tensor_tensor(cmp[1], cmp[1], bc(lower8[:, :, :], 1, Q), ALU.mult))
                link(dve.tensor_tensor(cmp[0], cmp[0], cmp[1], ALU.add))
                link(dve.reduce_sum(sv(5), cmp[0], axis=X))
                link(dve.scalar_tensor_tensor(out=sv(6), in0=sv(5), scalar=1.5, in1=probs,
                                              op0=ALU.is_lt, op1=ALU.mult))
                link(dve.reduce_sum(sm, sv(6), axis=X))
                if eps:
                    link(dve.tensor_scalar(sm, sm, eps, None, ALU.add))
                link(dve.reciprocal(mx, sm))
                dve.tensor_tensor(g, sv(6), bc(mx, 2, NE), ALU.mult).then_inc(sem(f"{name}_gates"), 1)

            layernorm(hs[3][:, :, :], xs[3][:, :, :], "x4_ready")
            layernorm(xs[3][:, :, :], inner[:, :, :], "x4n_ready")
            dve.wait_ge(sem("lower8_ready"), 1)
            dve.wait_ge(sem("r1_mm"), 1)
            route("r1", bank[3][:, 0:Q * NE].rearrange("p (q e) -> p q e", q=Q), gates[:, 0, :, :], 0.0)
            dve.wait_ge(sem("r1_gates"), 1)
            dve.wait_ge(sem("cols_ready"), 2)
            dve.wait_ge(*nth("x4nt_ready"))
            link(dve.tensor_copy(yacc[:, :, :], hs[3][:, :, :]))

            def combine(e, s, g, b, name):
                dve.wait_ge(sem(f"{name}_down"), e + 1)
                dve.tensor_tensor(ytmp[:, s, :, :], tiles(b), gates[:, g, :, ds(e, 1)].broadcast_to((P, Q, D)),
                                  ALU.mult).then_inc(sem(f"{name}_gated"), 1)
                dve.wait_ge(sem(f"{name}_gated"), e + 1)
                if not (isinstance(e, int) and e == 0):
                    dve.wait_ge(sem(f"{name}_acc"), e)
                dve.tensor_tensor(yacc[:, :, :], yacc[:, :, :], ytmp[:, s, :, :], ALU.add)\
                    .then_inc(sem(f"{name}_acc"), 1)

            def expert1(i, s):
                e = i * 2 + s
                if not first_round(i):
                    dve.wait_ge(sem("f1_up"), e * 2 - 2)
                dve.tensor_scalar(xe[:, s, :], xt[4][0:D, :], cols64[:, ds(e, 1)], cols64[:, ds(e + NE, 1)],
                                  ALU.mult, ALU.add).then_inc(sem("f1_xe"), 1)
                if not first_round(i) or s:
                    combine(e - 1, 1 - s, 0, 2 - s, "f1")

            over_experts(dve, expert1)
            combine(NE - 1, 1, 0, 2, "f1")
            dve.wait_ge(sem("f1_acc"), NE)
            dve.wait_ge(sem("b1_mm"), 1)
            link(dve.tensor_tensor(hs[4][:, :, :], yacc[:, :, :], tiles(0), ALU.add))

            layernorm(hs[4][:, :, :], xs[4][:, :, :], "x5_ready")
            layernorm(xs[4][:, :, :], inner[:, :, :], "x5n_ready")
            dve.wait_ge(*nth("x5n_tr"))
            dve.tensor_scalar(xt[5][0:D, :], bank[2][0:D, :], cols64[:, 2 * NE:2 * NE + 1],
                              cols64[:, 2 * NE + 1:2 * NE + 2], ALU.mult, ALU.add).then_inc(sem("x5nt_ready"), 1)
            dve.wait_ge(sem("p2_mm"), 1)
            pview = bank[0][:, 0:Q * HEADS4 * 2 * SEQ].rearrange("p (b r) -> p b r", r=2 * SEQ)
            for i in range(SEQ):
                off = SEQ - 1 - i
                if i == 0:
                    link(dve.tensor_scalar(posadd[:, :, :], pview[:, :, off:off + SEQ], pos1h[:, 0:1], None, ALU.mult))
                else:
                    link(dve.scalar_tensor_tensor(out=posadd[:, :, :], in0=pview[:, :, off:off + SEQ],
                                                  scalar=pos1h[:, i:i + 1], in1=posadd[:, :, :],
                                                  op0=ALU.mult, op1=ALU.add))

            def attention4(name, bias, extra):
                for q in range(Q):
                    compact(q, 1 + q, f"{name}_s")
                dve.wait_ge(sem(f"{name}_s_comp"), 4)
                softmax(16, name, bias, extra)
                for q in range(Q):
                    spread(q, name)

            attention4("a2", None, posadd[:, :, :])
            dve.wait_ge(sem("a2_down"), 1)
            link(dve.tensor_tensor(hs[5][:, :, :], hs[4][:, :, :], tiles(7), ALU.add))

            layernorm(hs[5][:, :, :], xs[5][:, :, :], "x6_ready")
            dve.wait_ge(sem("tree_mm"), 1)
            lg = [bank[b][:, :].rearrange("p (q n) -> p q n", q=2) for b in (0, 1)]
            for c in range(2):
                dve.tensor_scalar(onehot[:, 2 * c:2 * c + 2, 0:NODES], lg[c][:, :, 0:NODES], 0.0, None, ALU.is_gt)\
                    .then_inc(sem("tree_choice"), 1)
            dve.wait_ge(sem("tree_gelu"), 2)
            dve.wait_ge(sem("tree_choice"), 2)
            link(dve.tensor_copy(right[:, :, 0:PARENTS], onehot[:, :, 0:PARENTS]))
            link(dve.memset(onehot[:, :, 0:1], 1.0))
            for lv in range(7):
                n0, n1 = 2 ** lv - 1, 2 ** (lv + 1) - 1
                here = onehot[:, :, n0:n1]
                kids = onehot[:, :, 2 * n0 + 1:2 * n1 + 1].rearrange("p q (m s) -> p q m s", s=2)
                link(dve.tensor_tensor(kids[:, :, :, 1], here, right[:, :, n0:n1], ALU.mult))
                link(dve.tensor_tensor(kids[:, :, :, 0], here, kids[:, :, :, 1], ALU.subtract))
                link(dve.reduce_sum(went_right[:, lv, :], kids[:, :, :, 1], axis=X))
                s = lv % 2
                if lv >= 2:
                    dve.wait_ge(sem("split_tr"), lv - 1)
                link(dve.tensor_tensor(xsplit[:, s, :, 1, :], xs[5][:, :, :], bc(went_right[:, lv, :], 2, D), ALU.mult))
                dve.tensor_tensor(xsplit[:, s, :, 0, :], xs[5][:, :, :], xsplit[:, s, :, 1, :], ALU.subtract)\
                    .then_inc(sem("split_ready"), 1)
            dve.tensor_tensor(pathw[:, :, 0:NODES], pathw[:, :, 0:NODES], onehot[:, :, 0:NODES], ALU.mult)\
                .then_inc(sem("pathw_ready"), 1)
            dve.wait_ge(sem("pathw_ready"), 1)
            kids = pathw[:, :, 1:NODES].rearrange("p q (m s) -> p q m s", s=2)
            link(dve.tensor_tensor(pairw[:, :, 1:P], kids[:, :, :, 0], kids[:, :, :, 1], ALU.add))
            link(dve.tensor_copy(pairw[:, :, 0:1], pathw[:, :, 0:1]))

            def pick(i, level, n):
                first = 2 ** level if level is not None else 0
                for q in range(Q):
                    unit = (i + n) * Q + q
                    dve.wait_ge(sem("tree_y"), unit + 1)
                    dve.wait_ge(sem("tacc_step"), unit + (Q - 1))
                    dve.tensor_tensor(picked[:, q % 2, :].rearrange("p (m o) -> p m o", m=8),
                                      bank[4 + q][:, :].rearrange("p (m o) -> p m o", m=8),
                                      bc(pairw[:, q, ds(i * 8 + first, 8)], 2, D), ALU.mult)\
                        .then_inc(sem("picked"), 1)

            over_chunks(dve, pick)
            dve.wait_ge(sem("tacc_step"), Q + Q * sum(count for _, count in CHUNKS))
            link(dve.reduce_sum(yacc[:, :, :], tacc[:, :, :].rearrange("p q (m o) -> p q o m", m=8), axis=X))
            link(dve.tensor_tensor(yacc[:, :, :], yacc[:, :, :], hs[5][:, :, :], ALU.add))
            dve.wait_ge(sem("tree_b2"), 1)
            link(dve.tensor_tensor(hs[6][:, :, :], yacc[:, :, :], tiles(3), ALU.add))

            layernorm(hs[6][:, :, :], xs[6][:, :, :], "x7_ready")
            dve.wait_ge(sem("fn_ones"), 1)
            scaled_by_rms(xs[6][:, :, :], fn[:, :, 0:D], 1.0, 0.0, 1e-24, "f7_ready")
            dve.wait_ge(sem("sim_av"), 1)
            sim = bank[7][:, 0:Q * (D + 1)].rearrange("p (q d) -> p q d", q=Q)
            link(dve.reciprocal(st[:, 0, :], sim[:, :, D]))
            link(dve.tensor_scalar(st[:, 0, :], st[:, 0, :], 1.0 - 0.8, None, ALU.mult))
            link(dve.tensor_tensor(inner[:, :, :], sim[:, :, 0:D], bc(st[:, 0, :], 2, D), ALU.mult))
            link(dve.scalar_tensor_tensor(out=inner[:, :, :], in0=fn[:, :, 0:D], scalar=0.8, in1=inner[:, :, :],
                                          op0=ALU.mult, op1=ALU.add))
            scaled_by_rms(inner[:, :, :], xc[:, :, :], 1.0, 0.0, 1e-24, "c7_ready")
            link(dve.tensor_tensor(hs[7][:, :, :], hs[6][:, :, :], xc[:, :, :], ALU.add))

            layernorm(hs[7][:, :, :], xs[7][:, :, :], "x8_ready")
            scaled_by_rms(xs[7][:, :, :], inner[:, :, :], 1.0 / D, 1e-6, 0.0, "x8n_ready")
            dve.wait_ge(*nth("x8n_tr"))
            dve.tensor_scalar(xt[8][0:D, :], bank[2][0:D, :], cols64[:, 2 * NE + 2:2 * NE + 3], None, ALU.mult)\
                .then_inc(sem("x8nt_ready"), 1)
            by8 = lambda ap: ap.rearrange("p (g j) -> p g j", j=SEQ)
            for i in range(2):
                dve.wait_ge(sem("qk3_mm"), 2 * i + 2)
                if i:
                    dve.wait_ge(sem("qk3_ready"), 1)
                link(dve.tensor_tensor(by8(qk4[:, 2, :]), by8(bank[3 + 2 * i][:, :]), bc(rope[:, 0, :], 1, N_IMG), ALU.mult))
                link(dve.tensor_tensor(by8(qk4[:, 3, :]), by8(bank[4 + 2 * i][:, :]), bc(rope[:, 1, :], 1, N_IMG), ALU.mult))
                dve.tensor_tensor(qk4[:, i, :], qk4[:, 2, :], qk4[:, 3, :], ALU.add).then_inc(sem("qk3_ready"), 1)
            attention4("a3", causal_bias[:, :], None)
            dve.wait_ge(sem("a3_down"), 1)
            link(dve.tensor_tensor(yacc[:, :, :], xs[7][:, :, :], tiles(7), ALU.add))
            scaled_by_rms(yacc[:, :, :], inner[:, :, :], 1.0 / D, 1e-6, 0.0, "x9n_ready")
            link(dve.tensor_tensor(yacc[:, :, :], yacc[:, :, :], hs[7][:, :, :], ALU.add))
            dve.wait_ge(*nth("x9n_tr"))
            dve.tensor_scalar(xt[9][0:D, :], bank[2][0:D, :], cols64[:, 2 * NE + 3:2 * NE + 4], None, ALU.mult)\
                .then_inc(sem("x9nt_ready"), 1)
            dve.wait_ge(sem("r3_mm"), 1)
            route("r3", bank[7][:, 0:Q * NE].rearrange("p (q e) -> p q e", q=Q), gates[:, 1, :, :], 1e-9)
            dve.wait_ge(sem("r3_gates"), 1)

            def expert3(i, s):
                e = i * 2 + s
                if not first_round(i):
                    dve.wait_ge(sem("f3_down"), e - 1)
                dve.wait_ge(sem("f3_up"), e * 3 + 2)
                dve.wait_ge(sem("f3_silu"), e * 2 + 1)
                dve.tensor_tensor(ht[:, s, 0, :], silu[:, s, 0, :], bank[3 * s + 1][:, :], ALU.mult)\
                    .then_inc(sem("f3_ht"), 1)
                dve.wait_ge(sem("f3_silu"), e * 2 + 2)
                dve.tensor_tensor(ht[0:TAIL, s, 1, :], silu[0:TAIL, s, 1, :], bank[3 * s + 2][D:D + TAIL, :], ALU.mult)\
                    .then_inc(sem("f3_ht"), 1)
                if not first_round(i) or s:
                    combine(e - 1, 1 - s, 1, 7 - s, "f3")

            over_experts(dve, expert3)
            combine(NE - 1, 1, 1, 7, "f3")
            dve.wait_ge(sem("f3_acc"), NE)
            dve.tensor_copy(outb[:, :, :], yacc[:, :, :]).then_inc(sem("h8_ready"), 1)

        @block.tensor
        def _(pe):
            def loaded(name):
                pe.wait_ge(sem(name), W[name])

            def to_features(src, b, wait, done):
                pe.wait_ge(*nth(wait))
                for q in range(Q):
                    last = pe.transpose(bank[b][0:D, q * P:(q + 1) * P], src[:, q, :], ident[:, :])
                last.then_inc(sem(done), 1)

            tok = lambda q: slice(q * P, (q + 1) * P)

            loaded("tok_w_in")
            pe.wait_ge(sem("ones_ready"), 1)
            pe.wait_ge(sem("bias_ones"), 3)
            for q in range(Q):
                loaded(f"img_in{q}")
                for c in range(0, PATCH_W, 2):
                    k = P if c + 1 < PATCH_W else PATCH_H
                    span = slice(c, c + PATCH_STEP * (SEQ - 1) + 1, PATCH_STEP)
                    pe.matmul(bank[0][0:D, tok(q)], tok_w[0:k, c, :], imgs[0:k, q * GRP:(q + 1) * GRP, span],
                              start=(c == 0), stop=False)
                last = pe.matmul(bank[0][0:D, tok(q)], tok_b[:, :], ones_row[0:1, :], start=False, stop=True)
            last.then_inc(sem("tok_mm"), 1)
            pe.wait_ge(sem("ident_ready"), 1)
            loaded("rows_in")
            pe.transpose(bank[1][:, 0:2 + 2 * NE], rows128[:, :], ident[0:2 + 2 * NE, 0:2 + 2 * NE])
            pe.transpose(bank[1][0:D, 64:64 + 2 * NE + 4], rows64[:, :], ident[0:2 * NE + 4, 0:2 * NE + 4])\
                .then_inc(sem("rows_mm"), 1)
            pe.wait_ge(sem("h0t_ready"), 1)
            for q in range(Q):
                last = pe.transpose(tiles(5)[:, q, :], qt0[:, tok(q)], ident[0:D, 0:D])
            last.then_inc(sem("h0_tr"), 1)

            to_features(xs[0], 2, "x1_ready", "x1_tr")
            loaded("l0_in")
            pe.wait_ge(*nth("x1t_ready"))
            pe.matmul(bank[3][0:D, :], a0_w[:, :], xt[0][0:D, :], start=True, stop=True).then_inc(sem("q0_mm"), 1)
            pe.wait_ge(sem("qt0_ready"), 1)
            for q in range(Q):
                last = pe.matmul(bank[4][:, tok(q)], xt[0][0:D, tok(q)], qt0[:, tok(q)], start=True, stop=True)
            last.then_inc(sem("s0_mm"), 1)
            pe.wait_ge(sem("att0_ready"), 1)
            for q in range(Q):
                last = pe.matmul(tiles(5)[:, q, :], att0[:, q, :], xs[0][:, q, :], start=True, stop=True)
            last.then_inc(sem("a0_mm"), 1)

            loaded("heads_in")
            for i, r in enumerate((D, D, D, D, D, D // 2, D // 2, NE)):
                pe.transpose(bank[6][0:D, i * D:i * D + r], wnat[0:r, i, :], ident[0:r, 0:r])
            for i in range(2):
                last = pe.transpose(bank[7][:, i * D:(i + 1) * D], wo_pad[:, i, :], ident[0:D, 0:D])
            last.then_inc(sem("heads_tr"), 1)

            to_features(xs[1], 2, "x2_ready", "x2_tr")
            pe.wait_ge(*nth("x2t_ready"))
            for q in range(Q):
                last = pe.matmul(bank[5][:, q:q + 1], xt[1][:, tok(q)], f0_wr[:, :], start=True, stop=True)
            last.then_inc(sem("wr_mm"), 1)
            for c in range(2):
                pe.matmul(bank[3 + c][:, :], f0_w1[:, c * P:(c + 1) * P], xt[1][0:D, :], start=True, stop=True)\
                    .then_inc(sem("f0_mm"), 1)
            pe.wait_ge(sem("heads_w"), 18)
            pe.wait_ge(sem("wr_spread"), 1)
            pe.matmul(bank[6][:, 0:Q * SEQ], same_tok[:, :], small[:, 0, 0:Q * SEQ], start=True, stop=True)\
                .then_inc(sem("wr_gather_mm"), 1)
            pe.wait_ge(sem("f0_ready"), 2)
            for q in range(Q):
                for c in range(2):
                    pe.matmul(tiles(7)[:, q, :], ht[:, 0, c, tok(q)], f0_w2[:, c, :], start=(c == 0), stop=False)
                last = pe.matmul(tiles(7)[:, q, :], ones_row[0:1, :], f0_b2[:, :], start=False, stop=True)
            last.then_inc(sem("f0_down"), 1)

            to_features(xs[2], 2, "x3_ready", "x3_tr")
            loaded("l1_in")
            pe.wait_ge(*nth("x3t_ready"))
            for c in range(4):
                pe.matmul(bank[c][:, :], a1_w[:, 0, c * P:(c + 1) * P], xt[2][:, :], start=True, stop=True)\
                    .then_inc(sem("q1_mm"), 1)
            for c in range(4):
                pe.matmul(bank[4 + c][:, :], a1_w[:, 1, c * P:(c + 1) * P], xt[2][:, :], start=True, stop=True)\
                    .then_inc(sem("k1_mm"), 1)
            for q in range(Q):
                pe.wait_ge(sem("qt1_ready"), q + 1)
                pe.matmul(bank[q][:, :], xt[2][:, tok(q)], a1_w[:, 2, :], start=True, stop=True)\
                    .then_inc(sem("v1_mm"), 1)
            pe.wait_ge(sem("kt1_ready"), 4)
            for n in range(8):
                q, half = n // 2, n % 2
                part = slice(half * D, (half + 1) * D)
                if n >= 4:
                    pe.wait_ge(sem("v1_ready"), n - 3)
                for k in range(4):
                    h = 2 * k + half
                    last = pe.matmul(bank[(4 + n) % 8][:, k * P:(k + 1) * P], qt1[part, h // 2, tok(q)],
                                     kt1[part, h // 2, tok(q)], start=True, stop=True)
                last.then_inc(sem("s1_mm"), 1)
            for n in range(9):
                if n < 8:
                    pe.wait_ge(sem("a1_wide"), n + 1)
                    if n >= 4:
                        pe.wait_ge(sem("a1_att_t"), n - 3)
                    for k in range(4):
                        last = pe.transpose(bank[4 + n % 4][:, k * P:(k + 1) * P], wide[:, n % 2, k * P:(k + 1) * P],
                                            ident[:, :])
                    last.then_inc(sem("a1_tr"), 1)
                if n >= 1:
                    m = n - 1
                    q, half = m // 2, m % 2
                    part = slice(half * D, (half + 1) * D)
                    pe.wait_ge(sem("a1_att_t"), m + 1)
                    for k in range(4):
                        h = 2 * k + half
                        last = pe.matmul(bank[h // 2][part, tok(q)], v1[:, q, h * D:(h + 1) * D],
                                         att_t[:, m % 2, k * P:(k + 1) * P], start=True, stop=True)
                    last.then_inc(sem("a1_av"), 1)
            pe.wait_ge(sem("a1_out"), 4)
            for q in range(Q):
                for c in range(4):
                    pe.matmul(tiles(4)[:, q, :], out_t[:, c, tok(q)], a1_wu[:, c, :], start=(c == 0), stop=False)
                last = pe.matmul(tiles(4)[:, q, :], ones_row[0:1, :], a1_bu[:, :], start=False, stop=True)
            last.then_inc(sem("a1_down"), 1)

            to_features(xs[3], 2, "x4_ready", "x4_tr")
            pe.wait_ge(*nth("x4t_ready"))
            for q in range(Q):
                last = pe.matmul(bank[3][:, q * NE:(q + 1) * NE], xt[3][:, tok(q)], f1_wr[:, :], start=True, stop=True)
            last.then_inc(sem("r1_mm"), 1)
            to_features(inner, 1, "x4n_ready", "x4n_tr")

            def down1(e, s):
                pe.wait_ge(sem("f1_ht"), e * 2 + 2)
                if not isinstance(e, int) or e >= 2:
                    pe.wait_ge(sem("f1_gated"), e - 1)
                for q in range(Q):
                    for c in range(2):
                        last = pe.matmul(tiles(1 + s)[:, q, :], ht[:, s, c, tok(q)], f1_w2[:, s, c, :],
                                         start=(c == 0), stop=(c == 1))
                last.then_inc(sem("f1_down"), 1)

            def expert1(i, s):
                e = i * 2 + s
                pe.wait_ge(sem(f"f1_w_in{s}"), i * 32 + 32)
                pe.wait_ge(sem("f1_xe"), e + 1)
                if not first_round(i):
                    pe.wait_ge(sem("f1_ht"), e * 2 - 2)
                for c in range(2):
                    pe.matmul(bank[4 + 2 * s + c][:, :], f1_w1[:, s, c * P:(c + 1) * P], xe[:, s, :],
                              start=True, stop=True).then_inc(sem("f1_up"), 1)
                if not first_round(i) or s:
                    down1(e - 1, 1 - s)

            over_experts(pe, expert1)
            down1(NE - 1, 1)
            pe.wait_ge(sem("r1_gates"), 1)
            for q in range(Q):
                last = pe.transpose(bank[3][0:NE, tok(q)], gates[:, 0, q, :], ident[:, :])
            last.then_inc(sem("g1_tr"), 1)
            pe.wait_ge(sem("g1t_ready"), 1)
            for q in range(Q):
                last = pe.matmul(tiles(0)[:, q, :], gates_t[:, tok(q)], f1_b2[:, :], start=True, stop=True)
            last.then_inc(sem("b1_mm"), 1)

            pe.wait_ge(sem("heads_bias"), 2)
            pe.matmul(bank[7][:, 0:2 * SEQ], wt[:, 4, :], rel[:, :], start=True, stop=True).then_inc(sem("pos_mm"), 1)
            to_features(inner, 2, "x5n_ready", "x5n_tr")
            pe.wait_ge(*nth("x5nt_ready"))
            for c in range(3):
                pe.matmul(bank[3 + c][:, :], wt[:, c, :], xt[5][:, :], start=True, stop=True)\
                    .then_inc(sem("qk2_mm"), 1)
            for q in range(Q):
                last = pe.matmul(bank[6][:, tok(q)], xt[5][:, tok(q)], wt[:, 3, :], start=True, stop=True)
            last.then_inc(sem("qk2_mm"), 1)
            pe.wait_ge(sem("qk2_ready"), 4)
            pe.wait_ge(sem("pos_bd_ready"), 4)
            for q in range(Q):
                last = pe.matmul(bank[0][:, 0:Q * HEADS4 * 2 * SEQ].rearrange("p (h q r) -> p h q r", h=HEADS4, q=Q)
                                 [:, :, q, :], qk4[:, 1, tok(q)], pos_bd[:, :, :], start=True, stop=True)
            last.then_inc(sem("p2_mm"), 1)

            def attention4(name, qi, ki, out_w, bias):
                for h in range(HEADS4):
                    part = slice(h * HPAD, (h + 1) * HPAD)
                    for q in range(Q):
                        last = pe.matmul(bank[1 + h][:, tok(q)], qk4[part, qi, tok(q)],
                                         qk4[part, ki, tok(q)], start=True, stop=True)
                    last.then_inc(sem(f"{name}_s_mm"), 1)
                for n in range(HEADS4 + 1):
                    if n < HEADS4:
                        pe.wait_ge(sem(f"{name}_wide"), n + 1)
                        if n >= 2:
                            pe.wait_ge(sem(f"{name}_att_t"), n - 1)
                        for k in range(4):
                            last = pe.transpose(bank[4 + n % 2][:, k * P:(k + 1) * P],
                                                wide[:, n % 2, k * P:(k + 1) * P], ident[:, :])
                        last.then_inc(sem(f"{name}_tr"), 1)
                    if n >= 1:
                        h = n - 1
                        part = slice(h * HPAD, (h + 1) * HPAD)
                        pe.wait_ge(sem(f"{name}_att_t"), h + 1)
                        for q in range(Q):
                            last = pe.matmul(bank[6][part, tok(q)], v4[:, q, part], att_t[:, h % 2, tok(q)],
                                             start=True, stop=True)
                        last.then_inc(sem(f"{name}_av"), 1)
                pe.wait_ge(sem(f"{name}_out"), 1)
                for q in range(Q):
                    last = pe.matmul(tiles(7)[:, q, :], out_t[:, 0, tok(q)], wo_t[:, out_w, :], start=True,
                                     stop=bias is None)
                    if bias is not None:
                        last = pe.matmul(tiles(7)[:, q, :], ones_row[0:1, :], bias, start=False, stop=True)
                last.then_inc(sem(f"{name}_down"), 1)

            attention4("a2", 0, 2, 0, bo2[:, :])

            loaded("tree_in")
            for c, n in ((0, P), (1, NODES - P)):
                last = pe.transpose(bank[3][0:D, c * P:c * P + n], w1s_nat[0:n, c, :], ident[0:n, 0:n])
            last.then_inc(sem("w1s_tr"), 1)
            to_features(xs[5], 2, "x6_ready", "x6_tr")
            pe.wait_ge(*nth("x6t_ready"))
            pe.wait_ge(sem("w1s_ready"), 1)
            for q in range(Q):
                last = pe.matmul(bank[q // 2][:, (q % 2) * 256:(q % 2) * 256 + NODES], xt[6][:, tok(q)],
                                 w1s_t[:, 0:NODES], start=True, stop=True)
            last.then_inc(sem("tree_mm"), 1)
            for lv in range(1, 8):
                pe.wait_ge(sem("split_ready"), lv)
                if lv >= 3:
                    pe.wait_ge(sem("split_t"), lv - 2)
                for q in range(Q):
                    last = pe.transpose(bank[4 + lv % 2][:, tok(q)],
                                        xsplit[:, (lv - 1) % 2, q, :, :].rearrange("p s d -> p (s d)"), ident[:, :])
                last.then_inc(sem("split_tr"), 1)
            pe.wait_ge(sem("pathw_ready"), 1)
            pe.wait_ge(sem("split_t"), 7)
            for c, n in ((0, P), (1, NODES - P)):
                for q in range(Q):
                    last = pe.transpose(bank[4 + c][0:n, tok(q)], pathw[:, q, c * P:c * P + n], ident[:, :])
                last.then_inc(sem("pathw_tr"), 1)
            pe.wait_ge(sem("pathw_t"), 2)
            for q in range(Q):
                for c, n in ((0, P), (1, NODES - P)):
                    last = pe.matmul(tiles(3)[:, q, :], pathw_t[0:n, c, tok(q)], b2s[0:n, c, :],
                                     start=(c == 0), stop=(c == 1))
            last.then_inc(sem("tree_b2"), 1)
            pe.wait_ge(sem("w2s_in"), 48)

            def pair_outputs(i, level, n):
                for q in range(Q):
                    if not (first_round(i) and n == 0):
                        pe.wait_ge(sem("picked"), (i + n) * Q + (q - Q + 1))
                    if level is not None:
                        pe.matmul(bank[4 + q][:, :], xsplit_t[:, level, tok(q)],
                                  w2s[:, ds(i * 8 + (2 ** level - 1), 8), :].rearrange("p m o -> p (m o)"),
                                  start=True, stop=True).then_inc(sem("tree_y"), 1)
                    else:
                        pe.matmul(bank[4 + q][:, 0:D], xt[6][0:D, tok(q)], w2root[:, :], start=True, stop=True)
                        for lv in range(3):
                            m0, m1 = 2 ** lv - 1, 2 ** (lv + 1) - 1
                            last = pe.matmul(bank[4 + q][:, D * (1 + m0):D * (1 + m1)], xsplit_t[:, lv, tok(q)],
                                             w2s[:, m0:m1, :].rearrange("p m o -> p (m o)"), start=True, stop=True)
                        last.then_inc(sem("tree_y"), 1)

            over_chunks(pe, pair_outputs)

            loaded("moe3_in")
            pe.wait_ge(sem("picked"), Q * sum(count for _, count in CHUNKS))
            for j in range(2):
                for g in range(3):
                    if j:
                        pe.wait_ge(sem("w13_t_ready"), g + 1)
                    blocks = range(4 * g, min(4 * g + 4, NB13))
                    for k in blocks:
                        r = min(P, NE * HID3 - k * P)
                        last = pe.transpose(bank[4 + g][0:D, (k % 4) * P:(k % 4) * P + r], w13_nat[0:r, j, k, :],
                                            ident[0:r, 0:r])
                    last.then_inc(sem("w13_tr"), 1)
            pe.wait_ge(sem("w13_t_ready"), 6)
            for c, (h0, n) in enumerate(((0, P), (P, TAIL))):
                for k in range(NE // 2):
                    last = pe.transpose(bank[4 + c][0:n, tok(k)], w2e_nat[:, k, h0:h0 + n], ident[:, :])
                last.then_inc(sem("w2e_tr"), 1)

            to_features(fn[:, :, 0:D], 2, "f7_ready", "f7_tr")
            pe.wait_ge(*nth("f7t_ready"))
            pe.wait_ge(sem("w2e_t_ready"), 2)
            for q in range(Q):
                pe.matmul(bank[3 + q][:, :], xt[7][0:D, tok(q)], xt[7][0:D, :], start=True, stop=True)\
                    .then_inc(sem("sim_mm"), 1)
            pe.wait_ge(sem("sim_exp"), 4)
            for q in range(Q):
                for m in range(Q):
                    last = pe.matmul(bank[7][:, q * (D + 1):(q + 1) * (D + 1)], esim[:, m, tok(q)], fn[:, m, :],
                                     start=(m == 0), stop=(m == Q - 1))
            last.then_inc(sem("sim_av"), 1)

            to_features(inner, 2, "x8n_ready", "x8n_tr")
            pe.wait_ge(*nth("x8nt_ready"))
            for c in range(4):
                pe.matmul(bank[3 + c][:, :], wt[0:D, 5 + c, :], xt[8][0:D, :], start=True, stop=True)\
                    .then_inc(sem("qk3_mm"), 1)
            for q in range(Q):
                last = pe.matmul(bank[7][:, tok(q)], xt[8][0:D, tok(q)], wt_v3[0:D, :], start=True, stop=True)
            last.then_inc(sem("qk3_mm"), 1)
            pe.wait_ge(sem("v3_ready"), 1)
            pe.wait_ge(sem("qk3_ready"), 2)
            attention4("a3", 0, 1, 1, None)
            to_features(inner, 2, "x9n_ready", "x9n_tr")
            pe.wait_ge(*nth("x9nt_ready"))
            for q in range(Q):
                last = pe.matmul(bank[7][:, q * NE:(q + 1) * NE], xt[9][0:D, tok(q)], router_t[:, :],
                                 start=True, stop=True)
            last.then_inc(sem("r3_mm"), 1)

            def down3(e, s):
                pe.wait_ge(sem("f3_ht"), e * 2 + 2)
                if not isinstance(e, int) or e >= 2:
                    pe.wait_ge(sem("f3_gated"), e - 1)
                for q in range(Q):
                    pe.matmul(tiles(6 + s)[:, q, :], ht[:, s, 0, tok(q)], w2e_t[:, 0, ds(e * D, D)],
                              start=True, stop=False)
                    last = pe.matmul(tiles(6 + s)[:, q, :], ht[0:TAIL, s, 1, tok(q)],
                                     w2e_t[0:TAIL, 1, ds(e * D, D)], start=False, stop=True)
                last.then_inc(sem("f3_down"), 1)

            def expert3(i, s):
                e = i * 2 + s
                pe.wait_ge(sem(f"e3_slot_in{s}"), i * 4 + 4)
                if not first_round(i):
                    pe.wait_ge(sem("f3_ht"), e * 2 - 2)
                for c in range(3):
                    m = P if c < 2 else D + TAIL
                    pe.matmul(bank[3 * s + c][0:m, :], e3_slot[:, s, c * P:c * P + m], xt[9][0:D, :],
                              start=True, stop=True).then_inc(sem("f3_up"), 1)
                if not first_round(i) or s:
                    down3(e - 1, 1 - s)

            over_experts(pe, expert3)
            down3(NE - 1, 1)


_INS = ["x", "L0_tok_weight", "L0_tok_bias", "L0_attn_q_weight", "L0_ffn_wr", "L0_ffn_br", "L0_ffn_w1",
        "L0_ffn_b1", "L0_ffn_w2", "L0_ffn_b2", "L1_attn_Wq", "L1_attn_bq", "L1_attn_Wk", "L1_attn_bk",
        "L1_attn_Wv", "L1_attn_bv", "L1_attn_Wu", "L1_attn_bu", "L1_ffn_Wr", "L1_ffn_br", "L1_ffn_ln_g",
        "L1_ffn_ln_b", "L1_ffn_W1", "L1_ffn_b1", "L1_ffn_W2", "L1_ffn_b2", "L2_attn_ln_gamma",
        "L2_attn_ln_beta", "L2_attn_Wq", "L2_attn_bq", "L2_attn_Wk", "L2_attn_bk", "L2_attn_Wv", "L2_attn_bv",
        "L2_attn_Wpos", "L2_attn_bpos", "L2_attn_Wo", "L2_attn_bo", "L2_attn_u_bias", "L2_attn_v_bias",
        "L2_ffn_w1s", "L2_ffn_b1s", "L2_ffn_w2s", "L2_ffn_b2s", "L3_ffn_ln1_w", "L3_ffn_ln2_w", "L3_ffn_wq",
        "L3_ffn_wk", "L3_ffn_wv", "L3_ffn_wo", "L3_ffn_router_w", "L3_ffn_w1", "L3_ffn_w2", "L3_ffn_w3"]


def kernel(**inputs):
    import numpy as _np
    import concourse.bacc as _bacc
    from concourse import mybir as _mybir
    from concourse.bass_utils import run_bass_kernel_spmd as _run

    nc = _bacc.Bacc("TRN2", target_bir_lowering=False, num_devices=1)
    arrays, drams = {}, {}
    rope, rel = shape_constants()
    for name, value in [(n, inputs[n]) for n in _INS] + [("rope", rope), ("rel", rel)]:
        value = _np.ascontiguousarray(value)
        arrays[f"in_{name}_dram"] = value
        drams[name] = nc.dram_tensor(f"in_{name}_dram", value.shape, _mybir.dt.from_np(value.dtype),
                                     kind="ExternalInput").ap()
    out = nc.dram_tensor("out_0_dram", (N_IMG, SEQ, D), F32, kind="ExternalOutput").ap()
    vit_tower(nc, drams, drams["rope"], drams["rel"], out)
    r = _run(nc, [arrays], core_ids=[0])
    return r.results[0]["out_0_dram"]
```

```python
import math
from contextlib import ExitStack

import concourse.bass as bass
import numpy as np
from concourse import mybir

P = 128
D = 64
F32 = mybir.dt.float32
BF16 = mybir.dt.bfloat16
I32 = mybir.dt.int32
U32 = mybir.dt.uint32
ALU = mybir.AluOpType
ACT = mybir.ActivationFunctionType
X = mybir.AxisListType.X
ds = bass.ds

N_IMG = 64
IMG_H = IMG_W = 112
PATCH_H, PATCH_W, PATCH_STEP = 64, 25, 12
SEQ = (IMG_W - PATCH_W) // PATCH_STEP + 1
T = N_IMG * SEQ
Q = T // P
GRP = P // SEQ
HEADS4, HD, HPAD = 4, 16, 32
MAX_REL = 30
NE = 8
NODES = 255
PARENTS = NODES // 2
HID3 = int(8 / 3 * D)
TAIL = HID3 - P
RSQRT_MAGIC = 1597463007.0
BIG = 1e30


def shape_constants():
    inv_freq = 1.0 / 10000.0 ** (np.arange(0, HD, 2, dtype=np.float32) / HD)
    freqs = np.outer(np.arange(SEQ, dtype=np.float32), inv_freq)
    emb = np.concatenate([freqs, freqs], axis=-1).astype(np.float32)
    rope = np.zeros((P, 2, SEQ), np.float32)
    for h in range(HEADS4):
        rope[h * HPAD:h * HPAD + HD, 0] = np.cos(emb).T
        rope[h * HPAD:h * HPAD + HD, 1] = np.sin(emb).T
    n = 2 * MAX_REL + 1
    div = np.exp(np.arange(0, D, 2, dtype=np.float32) * np.float32(-math.log(10000.0) / D))
    ang = (np.arange(n, dtype=np.float32)[:, None] * div).astype(np.float32)
    enc = np.stack([np.sin(ang), np.cos(ang)], axis=-1).reshape(n, D).astype(np.float32)
    rel = np.ones((D + 1, 2 * SEQ), np.float32)
    rel[:D, 2 * SEQ - 1] = 0.0
    rel[:D, :2 * SEQ - 1] = enc[MAX_REL - SEQ + 1:MAX_REL + SEQ].T
    return rope, rel


def bc(ap, axis, n):
    ap = ap.unsqueeze(axis)
    shape = list(ap.shape)
    shape[axis] = n
    return ap.broadcast_to(tuple(shape))


def vit_tower(nc, a, rope_dram, rel_dram, out):
    ctx = ExitStack()
    with ctx:
        ctx.enter_context(nc.allow_non_contiguous_dma("weights in layouts of their own"))
        sems = {}
        STEPS = {
            "normed": ("x1_ready", "x2_ready", "x3_ready", "x4_ready", "x4n_ready", "x5n_ready",
                       "x6_ready", "f7_ready", "c7_ready", "x8n_ready", "x8_ready", "x9n_ready"),
            "features_tr": ("x1_tr", "x2_tr", "x3_tr", "x4_tr", "x4n_tr", "x5n_tr", "x6_tr", "f7_tr", "x8n_tr",
                            "x9n_tr"),
            "features_by_act": ("x1t_ready", "x2t_ready", "x3t_ready", "x4t_ready", "x4nt_ready", "x6t_ready",
                                "f7t_ready"),
            "features_by_dve": ("x5nt_ready", "x8nt_ready", "x9nt_ready"),
            "variance": ("x1_var", "x2_var", "x3_var", "x4_var", "x5_var", "x6_var", "f7_var", "c7_var",
                         "x8_var", "x9_var"),
        }
        ROOTS = (("x1", 1), ("x2", 1), ("x3", 1), ("x4", 2), ("x5", 1), ("x6", 1), ("f7", 1), ("c7", 1), ("x8", 2),
                 ("x9", 1))
        STEP = {name: (counter, n) for counter, names in STEPS.items() for n, name in enumerate(names)}

        def nth(name, value=1):
            return sem(name), value + (STEP[name][1] if name in STEP else 0)

        def sem(name):
            name = STEP[name][0] if name in STEP else name
            if name not in sems:
                sems[name] = ctx.enter_context(nc.semaphore(name))
            return sems[name]

        def sb(name, shape, dt=F32):
            return ctx.enter_context(nc.sbuf_tensor(name, shape, dt))

        bank = [ctx.enter_context(nc.psum_tensor(f"bank{i}", [P, 512], F32)) for i in range(8)]

        def tiles(b, n=D):
            return bank[b][:, 0:Q * n].rearrange("p (q n) -> p q n", q=Q)

        def views(region, *shapes):
            at = 0
            for shape in shapes:
                n = int(np.prod(shape))
                names = " ".join("abc"[:len(shape)])
                yield region[:, at:at + n].rearrange(f"p ({names}) -> p {names}", **dict(zip("abc", shape)))
                at += n

        region_a = sb("region_a", [P, N_IMG * IMG_W])
        region_b = sb("region_b", [P, (4 + 8 + 4) * T])
        region_c = sb("region_c", [P, PATCH_W * D])
        imgs, = views(region_a, (N_IMG, IMG_W))
        pathw, onehot, right, esim, silu = views(region_a, (Q, 256), (Q, 256), (Q, 256), (Q, T), (4, T))
        out_t = silu
        silu = silu.rearrange("p (s c) t -> p s c t", s=2)
        qt0 = region_b[0:D, 12 * T:13 * T]
        att0 = region_b[:, 13 * T:14 * T].rearrange("p (q n) -> p q n", q=Q)
        key_pads, qt1, v1 = views(region_b, (8, T), (4, T), (Q, 512))
        _, qk4, v4 = views(region_b, (8, T), (4, T), (Q, P))
        z_t, zbuf, pathw_t = views(region_b, (2, T), (2, Q * 2 * D), (2, T))
        zbuf = zbuf.rearrange("p b (q s d) -> p b q s d", q=Q, s=2)
        tok_w, = views(region_c, (PATCH_W, D))
        wide, ranks = views(region_c, (2, 512), (2, Q * NE * NE))
        padded = sb("padded", [P, 64 + 8 + 256 + 3 * 512 + NE + 9 * P + P + NE + 256 + 6 * P + 512 + 2 * SEQ])
        (a0_w, f0_wr, f0_w1, a1_w, f1_wr, wt, wt_v3, router_t, w1s_t, e3_slot, f1_slot, rel) = views(
            padded, (D,), (8,), (256,), (3, 512), (NE,), (9, P), (P,), (NE,), (256,), (2, 3 * P), (2, 256),
            (2 * SEQ,))
        ident = sb("ident", [P, P])
        same = sb("same", [P, GRP])
        same_tok = sb("same_tok", [P, P])
        same_lt = sb("same_lt", [P, P])
        pos1h = sb("pos1h", [P, SEQ])
        before = sb("before", [P, SEQ])
        strict_bias = sb("strict_bias", [P, SEQ])
        causal_bias = sb("causal_bias", [P, SEQ])
        not_first = sb("not_first", [P, 1])
        lower8 = sb("lower8", [P, NE, NE])
        ones_row = sb("ones_row", [P, P])
        rope = sb("rope", [P, 2, SEQ])
        tok_b = sb("tok_b", [1, D])
        f0_w2 = sb("f0_w2", [P, 2, D])
        f0_b2 = sb("f0_b2", [1, D])
        rows128 = sb("rows128", [2 + 2 * NE, P])
        cols128 = sb("cols128", [P, 2 + 2 * NE])
        rows64 = sb("rows64", [2 * NE + 4, D])
        cols64 = sb("cols64", [D, 2 * NE + 4])
        a1_wu = sb("a1_wu", [P, 4, D])
        a1_bu = sb("a1_bu", [1, D])
        f1_w1 = sb("f1_w1", [D, NE, 256])
        f1_w2 = sb("f1_w2", [P, NE, 2, D])
        f1_bias = sb("f1_bias", [P, 2 * NE])
        f1_b2 = sb("f1_b2", [NE, D])
        wnat = sb("wnat", [D, 8, D])
        wo_pad = sb("wo_pad", [D, 2, P])
        uv_rows = sb("uv_rows", [D + 1, 2, D])
        wo_t = sb("wo_t", [P, 2, D])
        bo2 = sb("bo2", [1, D])
        w1s_nat = sb("w1s_nat", [P, 2, D])
        b2s = sb("b2s", [P, 2, D])
        w2s = sb("w2s", [P, PARENTS, D])
        w2low = sb("w2low", [P, 2, 8, D])
        NB13 = -(-NE * HID3 // P)
        w13_nat = sb("w13_nat", [P, 2, NB13, D])
        w13_t = sb("w13_t", [D, 2, NB13 * P])
        w2e_nat = sb("w2e_nat", [P, NE // 2, HID3])
        w2e_t = sb("w2e_t", [P, 2, NE * D])
        hs = [sb(f"h{i}", [P, Q, D]) for i in range(2)] * 4
        xs = [sb(f"x{i}", [P, Q, D]) for i in range(2)] * 4
        xc = sb("xc", [P, Q, D])
        sq = sb("sq", [P, Q, D])
        st = sb("st", [P, 8, Q])
        xt = [sb(f"xt{i}", [P, T]) for i in range(3)]
        xt = [xt[i % 3] for i in range(10)]
        ft = sb("ft", [P, T])
        bst = sb("bst", [P, Q, 6])
        mv = sb("mv", [P, Q, 2])
        var2 = sb("var2", [P, 2, Q])
        rs = sb("rs", [P, 2, Q])
        rs_t = sb("rs_t", [P, 2, Q])
        half_neg = sb("half_neg", [P, 2, Q])
        ident_b = sb("ident_b", [P, P], BF16)
        other_b = sb("other_b", [P, P], BF16)
        upath = sb("upath", [P, Q, 18, 2])
        inner = sb("inner", [P, Q, D])
        small = sb("small", [P, 8, Q * NE])
        ht = sb("ht", [P, 2, 2, T])
        comp = sb("comp", [P, 32, SEQ])
        cexp = sb("cexp", [P, 32, SEQ])
        att_t = sb("att_t", [P, 2, 512])
        gates = sb("gates", [P, 2, Q, NE])
        gates_t = sb("gates_t", [NE, T])
        yacc = sb("yacc", [P, Q, D])
        ytmp = sb("ytmp", [P, 2, Q, D])
        posadd = sb("posadd", [P, Q * HEADS4, SEQ])
        pos_bd = sb("pos_bd", [P, HEADS4, 2 * SEQ])
        fn = sb("fn", [P, Q, D + 1])

        block = ctx.enter_context(nc.Block())
        def first_round(i):
            return isinstance(i, int) and i == 0

        def over_pairs(eng, step, rounds):
            step(0, 0)
            step(0, 1)
            with eng.Fori(1, rounds) as i:
                step(i, 0)
                step(i, 1)

        def over_experts(eng, step):
            over_pairs(eng, step, NE // 2)

        CHUNKS = 17
        FIRST_CHUNK = {7: 0, 6: 8, 5: 12, 4: 14}

        W = {}

        @block.sync
        def _(sp):
            def load(name, dst, src):
                W[name] = W.get(name, 0) + 16
                sp.dma_start(dst, src).then_inc(sem(name), 16)

            patch_rows = a["x"][:, 0, 0:PATCH_H, :].rearrange("b r w -> r b w")
            tw = a["L0_tok_weight"].rearrange("(r c) d -> r c d", c=PATCH_W)
            load("tok_w_in", tok_w[0:PATCH_H, :, :], tw)
            load("tok_w_in", tok_w[PATCH_H:P, 0:PATCH_W - 1, :], tw[:, 1:PATCH_W, :])
            load("tok_w_in", tok_b[:, :], a["L0_tok_bias"].unsqueeze(0))
            for q in range(Q):
                mine = slice(q * GRP, (q + 1) * GRP)
                load(f"img_in{q}", imgs[0:PATCH_H, mine, :], patch_rows[:, mine, :])
            sp.wait_ge(sem("padded_zeroed"), 1)
            load("l0_in", a0_w[0:D, :], a["L0_attn_q_weight"])
            load("l0_in", f0_wr[0:D, 0:1], a["L0_ffn_wr"])
            load("l0_in", f0_wr[D:D + 1, 0:1], a["L0_ffn_br"].unsqueeze(0))
            load("l0_in", f0_w1[0:D, :], a["L0_ffn_w1"])
            load("l0_in", f0_w2[:, :, :], a["L0_ffn_w2"].rearrange("(c k) d -> k c d", c=2))
            load("l0_in", f0_b2[:, :], a["L0_ffn_b2"].unsqueeze(0))
            load("rows_in", rows128[0:2, :], a["L0_ffn_b1"].rearrange("(c k) -> c k", c=2))
            load("rows_in", rows128[2:2 + 2 * NE, :], a["L1_ffn_b1"].rearrange("e (c k) -> (e c) k", c=2))
            load("rows_in", rows64[0:NE, :], a["L1_ffn_ln_g"])
            load("rows_in", rows64[NE:2 * NE, :], a["L1_ffn_ln_b"])
            for i, n in enumerate(("L2_attn_ln_gamma", "L2_attn_ln_beta", "L3_ffn_ln1_w", "L3_ffn_ln2_w")):
                load("rows_in", rows64[2 * NE + i:2 * NE + i + 1, :], a[n].unsqueeze(0))
            for i, n in enumerate("qkv"):
                load("l1_in", a1_w[0:D, i, :], a[f"L1_attn_W{n}"])
                load("l1_in", a1_w[D:D + 1, i, :], a[f"L1_attn_b{n}"].unsqueeze(0))
            load("l1_in", a1_wu[:, :, :], a["L1_attn_Wu"].rearrange("(c k) d -> k c d", c=4))
            load("l1_in", a1_bu[:, :], a["L1_attn_bu"].unsqueeze(0))
            load("l1_in", f1_wr[0:D, :], a["L1_ffn_Wr"])
            load("l1_in", f1_wr[D:D + 1, :], a["L1_ffn_br"].unsqueeze(0))
            load("l1_in", f1_b2[:, :], a["L1_ffn_b2"])

            load("heads_in", rope[:, :, :], rope_dram)
            load("heads_in", rel[0:D + 1, :], rel_dram)
            for i, n in enumerate(("L2_attn_Wq", "L2_attn_Wk", "L2_attn_Wv", "L2_attn_Wpos")):
                load("heads_in", wnat[:, i, :], a[n])
            for i, (n, r) in enumerate((("L3_ffn_wq", D), ("L3_ffn_wk", D // 2), ("L3_ffn_wv", D // 2),
                                        ("L3_ffn_router_w", NE))):
                load("heads_in", wnat[0:r, 4 + i, :], a[n])
            sp.wait_ge(sem("pads_zeroed"), 1)
            for i, n in enumerate(("L2_attn_Wo", "L3_ffn_wo")):
                load("heads_in", wo_pad[:, i, :].rearrange("o (h d) -> o h d", h=HEADS4)[:, :, 0:HD],
                     a[n].rearrange("o (h d) -> o h d", h=HEADS4))
            for i, n in ((2, "k"), (3, "v"), (4, "pos")):
                load("heads_in", wt[D:D + 1, i, :].rearrange("o (h d) -> o h d", h=HEADS4)[:, :, 0:HD],
                     a[f"L2_attn_b{n}"].rearrange("(o h d) -> o h d", o=1, h=HEADS4))
            load("heads_in", uv_rows[D:D + 1, 0, :], a["L2_attn_bq"].unsqueeze(0))
            for i, n in ((0, "u"), (1, "v")):
                load("heads_in", wt[D:D + 1, i, :].rearrange("o (h d) -> o h d", h=HEADS4)[:, :, 0:HD],
                     a[f"L2_attn_{n}_bias"].rearrange("o h a d -> o (h a) d"))
            load("heads_in", bo2[:, :], a["L2_attn_bo"].unsqueeze(0))

            load("tree_in", w1s_nat[:, 0, :], a["L2_ffn_w1s"][0:P, :])
            load("tree_in", w1s_nat[0:NODES - P, 1, :], a["L2_ffn_w1s"][P:NODES, :])
            load("tree_in", w1s_t[D:D + 1, 0:NODES], a["L2_ffn_b1s"].unsqueeze(0))
            load("tree_in", b2s[:, 0, :], a["L2_ffn_b2s"][0:P, :])
            load("tree_in", b2s[0:NODES - P, 1, :], a["L2_ffn_b2s"][P:NODES, :])

            rows = (NE * HID3) // P
            for i, n in enumerate(("w1", "w3")):
                flat = a[f"L3_ffn_{n}"].rearrange("e h c -> (e h) c")
                load("moe3_in", w13_nat[:, i, 0:rows, :], flat[0:rows * P, :].rearrange("(k p) c -> p k c", p=P))
                load("moe3_in", w13_nat[0:NE * HID3 - rows * P, i, rows, :], flat[rows * P:NE * HID3, :])
            load("moe3_in", w2e_nat[:, :, :], a["L3_ffn_w2"].rearrange("(k e) c h -> (e c) k h", e=2))
            load("f1_in", f1_w1[:, :, :], a["L1_ffn_W1"].rearrange("e d h -> d e h"))
            load("f1_in", f1_w2[:, :, 0, :], a["L1_ffn_W2"][:, 0:P, :].rearrange("e k d -> k e d"))
            load("f1_in", f1_w2[:, :, 1, :], a["L1_ffn_W2"][:, P:2 * P, :].rearrange("e k d -> k e d"))
            for side in range(2):
                load("w2s_in", w2s[side * D:(side + 1) * D, :, :],
                     a["L2_ffn_w2s"][1:NODES, :, :].rearrange("(m s) d o -> s d m o", s=2)[side])
            for lv in range(4):
                chunk, side = (3 - lv) // 2, (3 - lv) % 2
                reps = 2 ** (3 - lv)
                dst = w2low[side * D:(side + 1) * D, chunk, :, :].rearrange("d (n r) o -> d n r o", r=reps)
                for r in range(reps):
                    load("w2s_in", dst[:, :, r, :], a["L2_ffn_w2s"][2 ** lv - 1:2 ** (lv + 1) - 1].rearrange(
                        "n d o -> d n o"))

            sp.wait_ge(sem("f3_acc"), NE)
            sp.dma_start(out.rearrange("(q g) n d -> (g n) q d", q=Q), yacc[:, :, :]).then_inc(sem("out_done"), 16)
            sp.wait_ge(sem("out_done"), 16)

        @block.gpsimd
        def _(pool):
            made = [0]

            def link(ins):
                made[0] += 1
                ins.then_inc(sem("pool_step"), 1)
                pool.wait_ge(sem("pool_step"), made[0])

            pool.memset(padded[:, :], 0.0).then_inc(sem("padded_zeroed"), 1)
            pool.memset(wo_pad[:, :, :], 0.0).then_inc(sem("pads_zeroed"), 1)
            pool.memset(ft[:, :], 0.0).then_inc(sem("ft_zeroed"), 1)
            pool.memset(half_neg[:, :, :], -0.5).then_inc(sem("half_neg_ready"), 1)
            pool.memset(ones_row[:, :], 1.0).then_inc(sem("ones_ready"), 1)
            link(pool.memset(ident[:, :], 0.0))
            pool.affine_select(out=ident[:, :], in_=ident[:, :], compare_op=ALU.not_equal, fill=1.0, base=0,
                               pattern=[[-1, P]], channel_multiplier=1).then_inc(sem("ident_ready"), 1)
            pool.wait_ge(sem("ident_ready"), 1)
            pool.tensor_copy(ident_b[:, :], ident[:, :]).then_inc(sem("masks_b"), 1)
            link(pool.memset(same[:, :], 1.0))
            link(pool.affine_select(out=same[:, :], in_=same[:, :], compare_op=ALU.is_ge, fill=0.0, base=0,
                                    pattern=[[-SEQ, GRP]], channel_multiplier=1))
            link(pool.affine_select(out=same[:, :], in_=same[:, :], compare_op=ALU.is_ge, fill=0.0,
                                    base=SEQ - 1, pattern=[[SEQ, GRP]], channel_multiplier=-1))
            pool.tensor_copy(same_tok[:, :].rearrange("p (g j) -> p g j", g=GRP), bc(same[:, :], 2, SEQ))\
                .then_inc(sem("same_ready"), 1)
            pool.wait_ge(sem("same_ready"), 1)
            pool.tensor_scalar(other_b[:, :], same_tok[:, :], BIG, -BIG, ALU.mult, ALU.add)\
                .then_inc(sem("masks_b"), 1)
            pool.affine_select(out=same_lt[:, :], in_=same_tok[:, :], compare_op=ALU.is_gt, fill=0.0, base=0,
                               pattern=[[-1, P]], channel_multiplier=1).then_inc(sem("same_lt_ready"), 1)
            link(pool.memset(lower8[:, :, :], 1.0))
            pool.affine_select(out=lower8[:, :, :], in_=lower8[:, :, :], compare_op=ALU.is_gt, fill=0.0, base=0,
                               pattern=[[1, NE], [-1, NE]], channel_multiplier=0)\
                .then_inc(sem("lower8_ready"), 1)
            pool.memset(pos_bd[:, :, :], 0.0).then_inc(sem("pos_bd_zeroed"), 1)
            pool.memset(key_pads[:, :, :], 0.0).then_inc(sem("keys_zeroed"), 1)
            pool.memset(fn[:, :, D:D + 1], 1.0).then_inc(sem("fn_ones"), 1)

            def root(name, n):
                pool.wait_ge(*nth(f"{name}_var"))
                if n == 1:
                    pool.wait_ge(sem("half_neg_ready"), 1)
                pool.tensor_tensor(rs[:, 0:n, :], var2[:, 0:n, :], half_neg[:, 0:n, :], ALU.pow)\
                    .then_inc(sem("rooted"), 1)

            for name, n in ROOTS[0:4]:
                root(name, n)
            pool.wait_ge(sem("a1_out"), 4)
            pool.memset(key_pads[:, 0:4, :], 0.0).then_inc(sem("keys_zeroed"), 1)
            for name, n in ROOTS[4:7]:
                root(name, n)
            pool.memset(key_pads[:, 0:4, :], 0.0).then_inc(sem("keys_zeroed"), 1)
            for name, n in ROOTS[7:]:
                root(name, n)

            pool.wait_ge(sem("w13_t_ready"), 6)

            def fill_slot(i, s):
                e = i * 2 + s
                if not first_round(i):
                    pool.wait_ge(sem("f3_up"), e * 3 - 3)
                for j in range(2):
                    pool.tensor_copy(e3_slot[0:D, s, j * P:(j + 1) * P], w13_t[:, j, ds(e * HID3, P)])\
                        .then_inc(sem(f"e3_slot_in{s}"), 1)
                    pool.tensor_copy(e3_slot[0:D, s, 2 * P + j * D:2 * P + j * D + TAIL],
                                     w13_t[:, j, ds(e * HID3 + P, TAIL)]).then_inc(sem(f"e3_slot_in{s}"), 1)

            over_experts(pool, fill_slot)

        @block.scalar
        def _(act):
            def evac(dst, src, wait, value, done, func=ACT.Copy, **kw):
                act.wait_ge(*nth(wait, value))
                return act.activation(dst, src, func, **kw).then_inc(sem(done), 1)

            for q in (0, 2):
                act.wait_ge(sem(f"img_in{q}"), W[f"img_in{q}"])
                act.activation(imgs[PATCH_H:P, q * GRP:(q + 1) * GRP, 0:IMG_W - 1],
                               imgs[0:PATCH_H, q * GRP:(q + 1) * GRP, 1:IMG_W], ACT.Copy)\
                   .then_inc(sem("img_shifted_act"), 1)
            evac(qt0[:, :], bank[0][0:D, :], "tok_mm", 1, "h0t_ready", ACT.Gelu)
            evac(hs[0][:, :, :], tiles(5), "h0_tr", 1, "h0_ready")
            evac(cols128[:, :], bank[1][:, 0:2 + 2 * NE], "rows_mm", 1, "cols_ready")
            evac(cols64[:, :], bank[1][0:D, 64:64 + 2 * NE + 4], "rows_mm", 1, "cols_ready")
            evac(xt[0][0:D, :], bank[2][0:D, :], "x1_tr", 1, "x1t_ready")
            evac(qt0[:, :], bank[3][0:D, :], "q0_mm", 1, "qt0_ready")
            evac(att0[:, :, :], tiles(4, P), "s0_mm", 1, "sig_ready", ACT.Sigmoid)
            act.wait_ge(sem("heads_tr"), 1)
            act.wait_ge(sem("pads_zeroed"), 1)
            hv = lambda ap: ap.rearrange("p (h d) -> p h d", h=HEADS4)
            tr = lambda i: bank[6][0:D, i * D:(i + 1) * D].rearrange("p (h d) -> p h d", d=HD)
            for slot, i in ((0, 0), (1, 0), (2, 1), (3, 2), (4, 3), (5, 4)):
                act.activation(hv(wt[0:D, slot, :])[:, :, 0:HD], tr(i), ACT.Copy).then_inc(sem("heads_w"), 1)
            half = HD // 2
            act.activation(hv(wt[0:D, 6, :])[:, :, 0:half], tr(4)[:, :, half:HD], ACT.Copy, scale=-1.0)\
                .then_inc(sem("heads_w"), 1)
            act.activation(hv(wt[0:D, 6, :])[:, :, half:HD], tr(4)[:, :, 0:half], ACT.Copy)\
                .then_inc(sem("heads_w"), 1)
            for rep in range(2):
                two = lambda ap: ap.rearrange("p (k r d) -> p k r d", k=2, r=2)[:, :, rep, :]
                k3, v3 = (bank[6][0:D, i * D:i * D + 32].rearrange("p (k d) -> p k d", k=2) for i in (5, 6))
                act.activation(two(wt[0:D, 7, :])[:, :, 0:HD], k3, ACT.Copy).then_inc(sem("heads_w"), 1)
                act.activation(two(wt[0:D, 8, :])[:, :, 0:half], k3[:, :, half:HD], ACT.Copy, scale=-1.0)\
                    .then_inc(sem("heads_w"), 1)
                act.activation(two(wt[0:D, 8, :])[:, :, half:HD], k3[:, :, 0:half], ACT.Copy)\
                    .then_inc(sem("heads_w"), 1)
                act.activation(two(wt_v3[0:D, :])[:, :, 0:HD], v3, ACT.Copy).then_inc(sem("heads_w"), 1)
            act.activation(router_t[0:D, :], bank[6][0:D, 7 * D:7 * D + NE], ACT.Copy).then_inc(sem("heads_w"), 1)
            act.activation(wo_t[:, :, :], bank[7][:, 0:2 * D].rearrange("p (i o) -> p i o", i=2), ACT.Copy)\
                .then_inc(sem("heads_w"), 1)

            evac(xt[1][0:D, :], bank[2][0:D, :], "x2_tr", 1, "x2t_ready")
            for c in range(2):
                evac(ht[:, 0, c, :], bank[3 + c][:, :], "f0_mm", c + 1, "f0_ready", ACT.Gelu_apprx_tanh,
                     bias=cols128[:, c:c + 1])

            evac(xt[2][0:D, :], bank[2][0:D, :], "x3_tr", 1, "x3t_ready")
            act.wait_ge(sem("keys_zeroed"), 1)
            for c in range(4):
                evac(qt1[:, c, :], bank[c % 2][:, :], "q1_mm", c + 1, "qt1_ready")
                evac(key_pads[D:P, 2 * c + 1, :], bank[2 + c % 2][D:P, :], "k1_mm", c + 1, "k1_odd")
            for q in range(Q):
                evac(v1[:, q, :], bank[6 + q % 2][:, :], "v1_mm", q + 1, "v1_ready")
            evac(cexp[:, :, :], comp[:, :, :], "a1_shifted", 1, "a1_exp", ACT.Exp, scale=1.0 / 8.0)
            for b in range(8):
                if b >= 2:
                    act.wait_ge(sem("a1_av"), b - 1)
                evac(att_t[:, b % 2, :], bank[4 + b % 4][:, :], "a1_tr", b + 1, "a1_att_t")
            for c in range(4):
                evac(out_t[:, c, :], bank[c][:, :], "a1_av", 2 * c + 2, "a1_out")
            for j in range(2):
                for g in range(3):
                    n = min(512, NE * HID3 - 512 * g)
                    evac(w13_t[:, j, g * 512:g * 512 + n], bank[5 + g][0:D, 0:n], "w13_tr", 3 * j + g + 1,
                         "w13_t_ready")
            for c, n in ((0, P), (1, TAIL)):
                evac(w2e_t[0:n, c, :], bank[5 + c][0:n, :], "w2e_tr", c + 1, "w2e_t_ready")

            evac(xt[3][0:D, :], bank[2][0:D, :], "x4_tr", 1, "x4t_ready")
            evac(small[:, 0, 0:Q * NE].rearrange("p (q e) -> p q e", q=Q),
                 small[:, 1, 0:Q * NE].rearrange("p (q e) -> p q e", q=Q), "r1_shifted", 1, "r1_exp", ACT.Exp)
            evac(xt[4][0:D, :], bank[1][0:D, :], "x4n_tr", 1, "x4nt_ready")

            def gelu1(i, s):
                e = i * 2 + s
                if not first_round(i):
                    act.wait_ge(sem("f1_down"), e - 1)
                for c in range(2):
                    evac(ht[:, s, c, :], bank[4 + 2 * s + c][:, :], "f1_up", e * 2 + (c + 1), "f1_ht",
                         ACT.Gelu, bias=f1_bias[:, ds(e * 2 + c, 1)])

            act.wait_ge(sem("f1_bias_ready"), 1)
            over_experts(act, gelu1)
            evac(gates_t[:, :], bank[3][0:NE, :], "g1_tr", 1, "g1t_ready")

            for c in range(2):
                evac(qk4[:, c, :], bank[3 + c][:, :], "qk2_mm", c + 1, "qk2_ready")
            act.wait_ge(sem("keys_zeroed"), 2)
            for h in (2, 3):
                mine = slice(h * HPAD, (h + 1) * HPAD)
                evac(key_pads[mine, h, :], bank[5][mine, :], "qk2_mm", 3, "qk2_ready")
            evac(v4[:, :, :], tiles(6, P), "qk2_mm", 4, "qk2_ready")
            act.wait_ge(sem("pos_mm"), 1)
            act.wait_ge(sem("pos_bd_zeroed"), 1)
            for h in range(HEADS4):
                mine = slice(h * HPAD, h * HPAD + HD)
                act.activation(pos_bd[mine, h, :], bank[7][mine, 0:2 * SEQ], ACT.Copy)\
                    .then_inc(sem("pos_bd_ready"), 1)

            def attention4(name):
                evac(cexp[:, 0:16, :], comp[:, 0:16, :], f"{name}_shifted", 1, f"{name}_exp", ACT.Exp, scale=0.25)
                for q in range(Q):
                    if q >= 2:
                        act.wait_ge(sem(f"{name}_av"), q - 1)
                    evac(att_t[:, q % 2, :], bank[4 + q % 2][:, :], f"{name}_tr", q + 1, f"{name}_att_t")
                evac(out_t[:, 0, :], bank[6][:, :], f"{name}_av", 4, f"{name}_out")

            attention4("a2")

            evac(w1s_t[0:D, 0:NODES], bank[3][0:D, 0:NODES], "w1s_tr", 1, "w1s_ready")
            evac(xt[6][0:D, :], bank[2][0:D, :], "x6_tr", 1, "x6t_ready")
            for c in range(2):
                evac(right[:, 2 * c:2 * c + 2, 0:NODES],
                     bank[c][:, :].rearrange("p (q n) -> p q n", q=2)[:, :, 0:NODES], "tree_choice", c + 1,
                     "tree_abs", ACT.Abs)
            for c in range(2):
                evac(pathw[:, 2 * c:2 * c + 2, 0:NODES], right[:, 2 * c:2 * c + 2, 0:NODES], "tree_abs", c + 1,
                     "tree_gelu", ACT.Gelu)
            for c, n in ((0, P), (1, NODES - P)):
                evac(pathw_t[0:n, c, :], bank[4 + c][0:n, :], "pathw_tr", c + 1, "pathw_t")

            def copy_z_round(i, s):
                k = i * 2 + s
                if not first_round(i):
                    act.wait_ge(sem("tree_main"), k - 1)
                evac(z_t[:, s, :], bank[s][:, :], "z_tr", k + 1, "z_t_ready")

            over_pairs(act, copy_z_round, CHUNKS // 2)
            act.wait_ge(sem("tree_main"), CHUNKS - 2)
            evac(z_t[:, 0, :], bank[0][:, :], "z_tr", CHUNKS, "z_t_ready")

            act.wait_ge(sem("ft_zeroed"), 1)
            evac(ft[0:D, :], bank[2][0:D, :], "f7_tr", 1, "f7t_ready")
            for q in range(Q):
                evac(esim[:, q, :], bank[3 + q][:, :], "sim_mm", q + 1, "sim_exp", ACT.Exp)

            evac(v4[:, :, :], tiles(7, P), "qk3_mm", 5, "v3_ready")
            attention4("a3")
            evac(small[:, 0, 0:Q * NE].rearrange("p (q e) -> p q e", q=Q),
                 small[:, 1, 0:Q * NE].rearrange("p (q e) -> p q e", q=Q), "r3_shifted", 1, "r3_exp", ACT.Exp)

            def silu3(i, s):
                e = i * 2 + s
                if not first_round(i):
                    act.wait_ge(sem("f3_ht"), e * 2 - 2)
                evac(silu[:, s, 0, :], bank[3 * s][:, :], "f3_up", e * 3 + 1, "f3_silu", ACT.Silu)
                evac(silu[0:TAIL, s, 1, :], bank[3 * s + 2][0:TAIL, :], "f3_up", e * 3 + 3, "f3_silu", ACT.Silu)

            over_experts(act, silu3)

        @block.vector
        def _(dve):
            made = [0]

            def link(ins):
                made[0] += 1
                ins.then_inc(sem("dve_step"), 1)
                dve.wait_ge(sem("dve_step"), made[0])

            def rsqrt(n, name):
                dve.wait_ge(sem("rooted"), [r for r, _ in ROOTS].index(name) + 1)
                v, y, t = var2[:, 0:n, :], rs[:, 0:n, :], rs_t[:, 0:n, :]
                link(dve.tensor_tensor(t, y, y, ALU.mult))
                link(dve.scalar_tensor_tensor(out=t, in0=t, scalar=-0.5, in1=v, op0=ALU.mult, op1=ALU.mult))
                link(dve.scalar_tensor_tensor(out=y, in0=t, scalar=1.5, in1=y, op0=ALU.add, op1=ALU.mult))

            def moments(src, name, *rows):
                for q in range(Q):
                    last = dve.bn_stats(bst[:, q, :], src[:, q, :])
                link(last)
                for q in range(Q):
                    last = dve.bn_aggr(mv[:, q, :], bst[:, q, :])
                link(last)
                for i, (a, b) in enumerate(rows):
                    last = dve.tensor_scalar(var2[:, i, :], mv[:, :, 1], a, b, ALU.mult, ALU.add)
                last.then_inc(sem(f"{name}_var"), 1)

            def centred(src, dst, row, done):
                for q in range(Q):
                    last = dve.tensor_scalar(dst[:, q, :], src[:, q, :], mv[:, q, 0:1], rs[:, row, q:q + 1],
                                             ALU.subtract, ALU.mult)
                last.then_inc(sem(done), 1)
                dve.wait_ge(*nth(done))

            EPS = 1e-5

            def layernorm(src, dst, name):
                moments(src, name, (1.0, EPS))
                rsqrt(1, name)
                centred(src, dst, 0, f"{name}_ready")

            def mean_square(src, name, scale, shift, least):
                link(dve.tensor_tensor(sq[:, :, :], src, src, ALU.mult))
                link(dve.reduce_sum(st[:, 2, :], sq[:, :, :], axis=X))
                if shift:
                    last = dve.tensor_scalar(var2[:, 0, :], st[:, 2, :], scale, shift, ALU.mult, ALU.add)
                else:
                    last = dve.tensor_scalar(var2[:, 0, :], st[:, 2, :], least, None, ALU.max)
                last.then_inc(sem(f"{name}_var"), 1)

            def scaled_by_rms(src, dst, scale, shift, least, name, done):
                mean_square(src, name, scale, shift, least)
                rsqrt(1, name)
                dve.tensor_tensor(dst, src, bc(rs[:, 0, :], 2, D), ALU.mult).then_inc(sem(done), 1)
                dve.wait_ge(*nth(done))

            for i in range(3):
                link(dve.memset(xt[i][D:P, :], 0.0))
                dve.memset(xt[i][D:D + 1, :], 1.0).then_inc(sem("bias_ones"), 1)
            for q in (1, 3):
                dve.wait_ge(sem(f"img_in{q}"), W[f"img_in{q}"])
                dve.tensor_copy(imgs[PATCH_H:P, q * GRP:(q + 1) * GRP, 0:IMG_W - 1],
                                imgs[0:PATCH_H, q * GRP:(q + 1) * GRP, 1:IMG_W]).then_inc(sem("img_shifted_dve"), 1)
            dve.wait_ge(sem("ident_ready"), 1)
            dve.wait_ge(sem("same_lt_ready"), 1)
            by_pos = lambda m: m[:, :].rearrange("p (g j) -> p j g", g=GRP)
            link(dve.reduce_sum(pos1h[:, :], by_pos(ident), axis=X))
            link(dve.reduce_sum(before[:, :], by_pos(same_lt), axis=X))
            link(dve.tensor_scalar(not_first[:, :], pos1h[:, 0:1], -1.0, 1.0, ALU.mult, ALU.add))
            link(dve.tensor_scalar(strict_bias[:, :], pos1h[:, :], pos1h[:, 0:1], None, ALU.mult))
            link(dve.tensor_tensor(strict_bias[:, :], strict_bias[:, :], before[:, :], ALU.add))
            link(dve.tensor_scalar(strict_bias[:, :], strict_bias[:, :], BIG, -BIG, ALU.mult, ALU.add))
            link(dve.tensor_tensor(causal_bias[:, :], pos1h[:, :], before[:, :], ALU.add))
            link(dve.tensor_scalar(causal_bias[:, :], causal_bias[:, :], BIG, -BIG, ALU.mult, ALU.add))

            dve.wait_ge(sem("h0_ready"), 1)
            layernorm(hs[0], xs[0], "x1")
            dve.wait_ge(sem("sig_ready"), 1)
            dve.tensor_tensor(att0[:, :, :], att0[:, :, :], bc(same_tok[:, :], 1, Q), ALU.mult)\
                .then_inc(sem("att0_ready"), 1)
            dve.wait_ge(sem("a0_mm"), 1)
            link(dve.tensor_tensor(hs[1][:, :, :], hs[0][:, :, :], tiles(5), ALU.add))
            layernorm(hs[1], xs[1], "x2")

            sv = lambda i, n=SEQ: small[:, i, 0:Q * n].rearrange("p (q j) -> p q j", q=Q)
            dve.wait_ge(sem("wr_mm"), 1)
            link(dve.tensor_copy(st[:, 0, :], bank[5][:, 0:Q]))
            dve.tensor_tensor(sv(0), bc(pos1h[:, :], 1, Q), bc(st[:, 0, :], 2, SEQ), ALU.mult)\
                .then_inc(sem("wr_spread"), 1)
            dve.wait_ge(sem("wr_gather_mm"), 1)
            link(dve.tensor_copy(sv(1), bank[6][:, 0:Q * SEQ].rearrange("p (q j) -> p q j", q=Q)))
            link(dve.tensor_tensor(sv(2), sv(1), bc(pos1h[:, :], 1, Q), ALU.mult))
            link(dve.reduce_sum(st[:, 1, :], sv(2), axis=X))
            link(dve.tensor_tensor(sv(3), sv(1), bc(st[:, 1, :], 2, SEQ), ALU.is_gt))
            link(dve.tensor_tensor(sv(4), sv(1), bc(st[:, 1, :], 2, SEQ), ALU.is_equal))
            link(dve.tensor_tensor(sv(4), sv(4), bc(before[:, :], 1, Q), ALU.mult))
            link(dve.tensor_tensor(sv(3), sv(3), sv(4), ALU.add))
            link(dve.reduce_sum(st[:, 2, :], sv(3), axis=X))
            kept = max(1, SEQ // 2) - 1
            link(dve.scalar_tensor_tensor(out=st[:, 4, :], in0=st[:, 2, :], scalar=kept - 0.5, in1=st[:, 1, :],
                                          op0=ALU.is_lt, op1=ALU.mult))
            link(dve.tensor_tensor(hs[2][:, :, :], hs[1][:, :, :], xs[1][:, :, :], ALU.add))
            dve.wait_ge(sem("f0_down"), 1)
            link(dve.tensor_tensor(xc[:, :, :], tiles(7), bc(st[:, 4, :], 2, D), ALU.mult))
            link(dve.tensor_tensor(hs[2][:, :, :], hs[2][:, :, :], xc[:, :, :], ALU.add))
            layernorm(hs[2], xs[2], "x3")

            def compact(n, b, name):
                dve.wait_ge(sem(f"{name}_mm"), n + 1)
                dve.reduce_max(comp[:, 4 * n:4 * n + 4, :],
                               bank[b][:, :].rearrange("p (k g j) -> p k j g", k=4, g=GRP), axis=X)\
                    .then_inc(sem(f"{name}_comp"), 1)

            def softmax(nb, name, bias, extra=None, zero_first=False):
                c, e = comp[:, 0:nb, :], cexp[:, 0:nb, :]
                mx, sm = small[:, 2, 0:nb], small[:, 3, 0:nb]
                if extra is not None:
                    link(dve.tensor_tensor(c, c, extra, ALU.add))
                if bias is not None:
                    link(dve.tensor_tensor(c, c, bc(bias, 1, nb), ALU.add))
                link(dve.reduce_max(mx, c, axis=X))
                dve.tensor_tensor(c, c, bc(mx, 2, SEQ), ALU.subtract).then_inc(sem(f"{name}_shifted"), 1)
                dve.wait_ge(sem(f"{name}_exp"), 1)
                link(dve.reduce_sum(sm, e, axis=X))
                link(dve.reciprocal(mx, sm))
                if zero_first:
                    link(dve.tensor_scalar(mx, mx, not_first[:, :], None, ALU.mult))
                link(dve.tensor_tensor(c, e, bc(mx, 2, SEQ), ALU.mult))

            def spread(n, name):
                if n >= 2:
                    dve.wait_ge(sem(f"{name}_tr"), n - 1)
                dve.tensor_tensor(wide[:, n % 2, :].rearrange("p (k g j) -> p k g j", k=4, g=GRP),
                                  bc(comp[:, 4 * n:4 * n + 4, :], 2, GRP),
                                  bc(bc(same[:, :], 2, SEQ), 1, 4), ALU.mult).then_inc(sem(f"{name}_wide"), 1)

            dve.wait_ge(sem("heads_in"), W["heads_in"])
            for i in range(2):
                row = wt[D:D + 1, i, :].rearrange("o (h d) -> o h d", h=HEADS4)[:, :, 0:HD]
                dve.tensor_tensor(row, row, uv_rows[D:D + 1, 0, :].rearrange("o (h d) -> o h d", h=HEADS4), ALU.add)\
                    .then_inc(sem("heads_bias"), 1)

            dve.wait_ge(sem("keys_zeroed"), 1)
            for c in range(4):
                dve.wait_ge(sem("k1_mm"), c + 1)
                dve.tensor_copy(key_pads[0:D, 2 * c, :], bank[2 + c % 2][0:D, :]).then_inc(sem("k1_even"), 1)
                if c:
                    compact(2 * c - 2, 4, "s1")
                    compact(2 * c - 1, 5, "s1")
            compact(6, 4, "s1")
            compact(7, 5, "s1")
            dve.wait_ge(sem("s1_comp"), 8)
            softmax(32, "a1", strict_bias[:, :], zero_first=True)
            for n in range(8):
                spread(n, "a1")
            dve.wait_ge(sem("a1_down"), 1)
            link(dve.tensor_tensor(hs[3][:, :, :], hs[2][:, :, :], tiles(4), ALU.add))

            def route(name, p_in, g, eps):
                probs, lg = small[:, 4, 0:Q * NE].rearrange("p (q e) -> p q e", q=Q), sv(1)
                mx, sm = small[:, 2, 0:Q], small[:, 3, 0:Q]
                link(dve.reduce_max(mx, p_in, axis=X))
                dve.tensor_tensor(lg, p_in, bc(mx, 2, NE), ALU.subtract).then_inc(sem(f"{name}_shifted"), 1)
                dve.wait_ge(sem(f"{name}_exp"), 1)
                link(dve.reduce_sum(sm, sv(0), axis=X))
                link(dve.reciprocal(mx, sm))
                link(dve.tensor_tensor(probs, sv(0), bc(mx, 2, NE), ALU.mult))
                cmp = [ranks[:, i, :].rearrange("p (q e f) -> p q e f", q=Q, e=NE) for i in range(2)]
                other, own = bc(probs, 2, NE), bc(probs, 3, NE)
                link(dve.tensor_tensor(cmp[0], other, own, ALU.is_gt))
                link(dve.tensor_tensor(cmp[1], other, own, ALU.is_equal))
                link(dve.tensor_tensor(cmp[1], cmp[1], bc(lower8[:, :, :], 1, Q), ALU.mult))
                link(dve.tensor_tensor(cmp[0], cmp[0], cmp[1], ALU.add))
                link(dve.reduce_sum(sv(5), cmp[0], axis=X))
                link(dve.scalar_tensor_tensor(out=sv(6), in0=sv(5), scalar=1.5, in1=probs,
                                              op0=ALU.is_lt, op1=ALU.mult))
                link(dve.reduce_sum(sm, sv(6), axis=X))
                if eps:
                    link(dve.tensor_scalar(sm, sm, eps, None, ALU.add))
                link(dve.reciprocal(mx, sm))
                dve.tensor_tensor(g, sv(6), bc(mx, 2, NE), ALU.mult).then_inc(sem(f"{name}_gates"), 1)

            moments(hs[3], "x4", (1.0, EPS), (1.0 + EPS, EPS * EPS))
            rsqrt(2, "x4")
            centred(hs[3], xs[3], 0, "x4_ready")
            centred(hs[3], inner, 1, "x4n_ready")
            def scale_weights(i, s):
                e = i * 2 + s
                if not first_round(i):
                    dve.wait_ge(sem("f1_up"), e * 2 - 2)
                dve.tensor_scalar(f1_slot[0:D, s, :], f1_w1[:, ds(e, 1), :].squeeze(1) if not isinstance(e, int)
                                  else f1_w1[:, e, :], cols64[:, ds(e, 1)], None, ALU.mult)\
                    .then_inc(sem("f1_slot_in"), 1)

            dve.wait_ge(sem("cols_ready"), 2)
            dve.wait_ge(sem("f1_in"), W["f1_in"])
            scale_weights(0, 0)
            scale_weights(0, 1)
            dve.wait_ge(sem("f1_shift_mm"), 1)
            dve.tensor_tensor(f1_bias[:, :], bank[0][:, 0:2 * NE], cols128[:, 2:2 + 2 * NE], ALU.add)\
                .then_inc(sem("f1_bias_ready"), 1)
            dve.wait_ge(sem("lower8_ready"), 1)
            dve.wait_ge(sem("r1_mm"), 1)
            route("r1", bank[3][:, 0:Q * NE].rearrange("p (q e) -> p q e", q=Q), gates[:, 0, :, :], 0.0)
            dve.wait_ge(sem("r1_gates"), 1)
            link(dve.tensor_copy(yacc[:, :, :], hs[3][:, :, :]))

            def combine(e, s, g, b, name):
                dve.wait_ge(sem(f"{name}_down"), e + 1)
                dve.tensor_tensor(ytmp[:, s, :, :], tiles(b), gates[:, g, :, ds(e, 1)].broadcast_to((P, Q, D)),
                                  ALU.mult).then_inc(sem(f"{name}_gated"), 1)
                dve.wait_ge(sem(f"{name}_gated"), e + 1)
                if not (isinstance(e, int) and e == 0):
                    dve.wait_ge(sem(f"{name}_acc"), e)
                dve.tensor_tensor(yacc[:, :, :], yacc[:, :, :], ytmp[:, s, :, :], ALU.add)\
                    .then_inc(sem(f"{name}_acc"), 1)

            def expert1(i, s):
                e = i * 2 + s
                if not first_round(i):
                    scale_weights(i, s)
                if not first_round(i) or s:
                    combine(e - 1, 1 - s, 0, 2 - s, "f1")

            over_experts(dve, expert1)
            combine(NE - 1, 1, 0, 2, "f1")
            dve.wait_ge(sem("f1_acc"), NE)
            dve.wait_ge(sem("b1_mm"), 1)
            link(dve.tensor_tensor(hs[4][:, :, :], yacc[:, :, :], tiles(0), ALU.add))

            moments(hs[4], "x5", (1.0 + EPS, EPS * EPS))
            rsqrt(1, "x5")
            centred(hs[4], inner, 0, "x5n_ready")
            dve.wait_ge(*nth("x5n_tr"))
            dve.tensor_scalar(xt[5][0:D, :], bank[2][0:D, :], cols64[:, 2 * NE:2 * NE + 1],
                              cols64[:, 2 * NE + 1:2 * NE + 2], ALU.mult, ALU.add).then_inc(sem("x5nt_ready"), 1)
            dve.wait_ge(sem("keys_zeroed"), 2)
            dve.wait_ge(sem("qk2_mm"), 3)
            for h in (0, 1):
                mine = slice(h * HPAD, (h + 1) * HPAD)
                dve.tensor_copy(key_pads[mine, h, :], bank[5][mine, :]).then_inc(sem("k2_ready"), 1)
            dve.wait_ge(sem("p2_mm"), 1)
            pview = bank[0][:, 0:Q * HEADS4 * 2 * SEQ].rearrange("p (b r) -> p b r", r=2 * SEQ)
            for i in range(SEQ):
                off = SEQ - 1 - i
                if i == 0:
                    link(dve.tensor_scalar(posadd[:, :, :], pview[:, :, off:off + SEQ], pos1h[:, 0:1], None, ALU.mult))
                else:
                    link(dve.scalar_tensor_tensor(out=posadd[:, :, :], in0=pview[:, :, off:off + SEQ],
                                                  scalar=pos1h[:, i:i + 1], in1=posadd[:, :, :],
                                                  op0=ALU.mult, op1=ALU.add))

            def attention4(name, bias, extra):
                for q in range(Q):
                    compact(q, 1 + q, f"{name}_s")
                dve.wait_ge(sem(f"{name}_s_comp"), 4)
                softmax(16, name, bias, extra)
                for q in range(Q):
                    spread(q, name)

            attention4("a2", None, posadd[:, :, :])
            dve.wait_ge(sem("a2_down"), 1)
            link(dve.tensor_tensor(hs[5][:, :, :], hs[4][:, :, :], tiles(7), ALU.add))

            layernorm(hs[5], xs[5], "x6")
            dve.wait_ge(sem("tree_mm"), 1)
            lg = [bank[b][:, :].rearrange("p (q n) -> p q n", q=2) for b in (0, 1)]
            for c in range(2):
                dve.tensor_scalar(onehot[:, 2 * c:2 * c + 2, 0:NODES], lg[c][:, :, 0:NODES], 0.0, None, ALU.is_gt)\
                    .then_inc(sem("tree_choice"), 1)
            dve.wait_ge(sem("tree_gelu"), 2)
            dve.wait_ge(sem("tree_choice"), 2)
            link(dve.tensor_copy(right[:, :, 0:PARENTS], onehot[:, :, 0:PARENTS]))
            link(dve.memset(onehot[:, :, 0:1], 1.0))
            for lv in range(7):
                n0, n1 = 2 ** lv - 1, 2 ** (lv + 1) - 1
                here = onehot[:, :, n0:n1]
                kids = onehot[:, :, 2 * n0 + 1:2 * n1 + 1].rearrange("p q (m s) -> p q m s", s=2)
                link(dve.tensor_tensor(kids[:, :, :, 1], here, right[:, :, n0:n1], ALU.mult))
                link(dve.tensor_tensor(kids[:, :, :, 0], here, kids[:, :, :, 1], ALU.subtract))
            dve.tensor_tensor(pathw[:, :, 0:NODES], pathw[:, :, 0:NODES], onehot[:, :, 0:NODES], ALU.mult)\
                .then_inc(sem("pathw_ready"), 1)
            dve.wait_ge(sem("pathw_ready"), 1)
            for lv in (7, 6, 5, 4):
                n0, low = 2 ** lv - 1, 2 ** (lv - 4)
                last = dve.reduce_sum(upath[:, :, FIRST_CHUNK[lv]:FIRST_CHUNK[lv] + low, :]
                                      .rearrange("p q c s -> p q (c s)"),
                                      pathw[:, :, n0:2 * n0 + 1].rearrange("p q (t l) -> p q l t", t=8), axis=X)
            for lv in (3, 2, 1):
                last = dve.reduce_sum(upath[:, :, 15 + (3 - lv) // 2, (3 - lv) % 2],
                                      pathw[:, :, 2 ** lv - 1:2 ** (lv + 1) - 1], axis=X)
            link(dve.tensor_copy(upath[:, :, 16, 1], pathw[:, :, 0]))

            def spread_token(i, s):
                k = i * 2 + s
                if not first_round(i):
                    dve.wait_ge(sem("z_tr"), k - 1)
                dve.tensor_tensor(zbuf[:, s, :, :, :], bc(xs[5][:, :, :], 2, 2),
                                  bc(upath[:, :, ds(k, 1), :].rearrange("p q k s -> p q (k s)"), 3, D), ALU.mult)\
                    .then_inc(sem("z_ready"), 1)

            over_pairs(dve, spread_token, CHUNKS // 2)
            spread_token(CHUNKS // 2, 0)
            dve.wait_ge(sem("tree_b2"), 1)
            link(dve.tensor_tensor(yacc[:, :, :], hs[5][:, :, :], tiles(3), ALU.add))
            dve.wait_ge(sem("tree_main"), CHUNKS)
            for q in range(Q):
                link(dve.tensor_tensor(wide[:, q % 2, :].rearrange("p (t o) -> p t o", t=8),
                                       bank[4 + q][:, :].rearrange("p (t o) -> p t o", t=8),
                                       bc(onehot[:, q, 7:15], 2, D), ALU.mult))
                link(dve.reduce_sum(inner[:, q, :], wide[:, q % 2, :].rearrange("p (t o) -> p o t", t=8), axis=X))
            link(dve.tensor_tensor(hs[6][:, :, :], yacc[:, :, :], inner[:, :, :], ALU.add))

            for q in range(Q):
                last = dve.bn_stats(bst[:, q, :], hs[6][:, q, :])
            link(last)
            for q in range(Q):
                last = dve.bn_aggr(mv[:, q, :], bst[:, q, :])
            link(last)
            link(dve.tensor_scalar(st[:, 0, :], mv[:, :, 1], 1e-24, 1e-24 * EPS, ALU.mult, ALU.add))
            dve.scalar_tensor_tensor(out=var2[:, 0, :], in0=mv[:, :, 1], scalar=float(D), in1=st[:, 0, :],
                                     op0=ALU.mult, op1=ALU.max).then_inc(sem("f7_var"), 1)
            dve.wait_ge(sem("fn_ones"), 1)
            rsqrt(1, "f7")
            centred(hs[6], fn[:, :, 0:D], 0, "f7_ready")
            dve.wait_ge(sem("sim_av"), 1)
            sim = bank[7][:, 0:Q * (D + 1)].rearrange("p (q d) -> p q d", q=Q)
            link(dve.reciprocal(st[:, 0, :], sim[:, :, D]))
            link(dve.tensor_scalar(st[:, 0, :], st[:, 0, :], 1.0 - 0.8, None, ALU.mult))
            link(dve.tensor_tensor(inner[:, :, :], sim[:, :, 0:D], bc(st[:, 0, :], 2, D), ALU.mult))
            link(dve.scalar_tensor_tensor(out=inner[:, :, :], in0=fn[:, :, 0:D], scalar=0.8, in1=inner[:, :, :],
                                          op0=ALU.mult, op1=ALU.add))
            scaled_by_rms(inner[:, :, :], xc[:, :, :], 1.0, 0.0, 1e-24, "c7", "c7_ready")
            link(dve.tensor_tensor(hs[7][:, :, :], hs[6][:, :, :], xc[:, :, :], ALU.add))

            RMS_EPS = 1e-6
            moments(hs[7], "x8", (1.0, EPS), (1.0 + RMS_EPS, RMS_EPS * EPS))
            rsqrt(2, "x8")
            centred(hs[7], inner, 1, "x8n_ready")
            centred(hs[7], xs[7], 0, "x8_ready")
            dve.wait_ge(*nth("x8n_tr"))
            dve.tensor_scalar(xt[8][0:D, :], bank[2][0:D, :], cols64[:, 2 * NE + 2:2 * NE + 3], None, ALU.mult)\
                .then_inc(sem("x8nt_ready"), 1)
            by8 = lambda ap: ap.rearrange("p (g j) -> p g j", j=SEQ)
            for i in range(2):
                dve.wait_ge(sem("qk3_mm"), 2 * i + 2)
                if i:
                    dve.wait_ge(sem("qk3_ready"), 1)
                link(dve.tensor_tensor(by8(qk4[:, 2, :]), by8(bank[3 + 2 * i][:, :]), bc(rope[:, 0, :], 1, N_IMG), ALU.mult))
                link(dve.tensor_tensor(by8(qk4[:, 3, :]), by8(bank[4 + 2 * i][:, :]), bc(rope[:, 1, :], 1, N_IMG), ALU.mult))
                if i == 0:
                    dve.tensor_tensor(qk4[:, 0, :], qk4[:, 2, :], qk4[:, 3, :], ALU.add).then_inc(sem("qk3_ready"), 1)
            dve.wait_ge(sem("keys_zeroed"), 3)
            for h in range(HEADS4):
                mine = slice(h * HPAD, (h + 1) * HPAD)
                dve.tensor_tensor(key_pads[mine, h, :], qk4[mine, 2, :], qk4[mine, 3, :], ALU.add)\
                    .then_inc(sem("qk3_ready"), 1)
            attention4("a3", causal_bias[:, :], None)
            dve.wait_ge(sem("a3_down"), 1)
            link(dve.tensor_tensor(yacc[:, :, :], xs[7][:, :, :], tiles(7), ALU.add))
            scaled_by_rms(yacc[:, :, :], inner[:, :, :], 1.0 / D, 1e-6, 0.0, "x9", "x9n_ready")
            link(dve.tensor_tensor(yacc[:, :, :], yacc[:, :, :], hs[7][:, :, :], ALU.add))
            dve.wait_ge(*nth("x9n_tr"))
            dve.tensor_scalar(xt[9][0:D, :], bank[2][0:D, :], cols64[:, 2 * NE + 3:2 * NE + 4], None, ALU.mult)\
                .then_inc(sem("x9nt_ready"), 1)
            dve.wait_ge(sem("r3_mm"), 1)
            route("r3", bank[7][:, 0:Q * NE].rearrange("p (q e) -> p q e", q=Q), gates[:, 1, :, :], 1e-9)
            dve.wait_ge(sem("r3_gates"), 1)

            def expert3(i, s):
                e = i * 2 + s
                if not first_round(i):
                    dve.wait_ge(sem("f3_down"), e - 1)
                dve.wait_ge(sem("f3_up"), e * 3 + 2)
                dve.wait_ge(sem("f3_silu"), e * 2 + 1)
                dve.tensor_tensor(ht[:, s, 0, :], silu[:, s, 0, :], bank[3 * s + 1][:, :], ALU.mult)\
                    .then_inc(sem("f3_ht"), 1)
                dve.wait_ge(sem("f3_silu"), e * 2 + 2)
                dve.tensor_tensor(ht[0:TAIL, s, 1, :], silu[0:TAIL, s, 1, :], bank[3 * s + 2][D:D + TAIL, :], ALU.mult)\
                    .then_inc(sem("f3_ht"), 1)
                if not first_round(i) or s:
                    combine(e - 1, 1 - s, 1, 7 - s, "f3")

            over_experts(dve, expert3)
            combine(NE - 1, 1, 1, 7, "f3")

        @block.tensor
        def _(pe):
            def loaded(name):
                pe.wait_ge(sem(name), W[name])

            def to_features(src, b, wait, done):
                pe.wait_ge(*nth(wait))
                for q in range(Q):
                    last = pe.transpose(bank[b][0:D, q * P:(q + 1) * P], src[:, q, :], ident[:, :])
                last.then_inc(sem(done), 1)

            tok = lambda q: slice(q * P, (q + 1) * P)

            loaded("tok_w_in")
            pe.wait_ge(sem("ones_ready"), 1)
            pe.wait_ge(sem("bias_ones"), 3)
            for q in range(Q):
                loaded(f"img_in{q}")
                pe.wait_ge(sem("img_shifted_dve" if q % 2 else "img_shifted_act"), q // 2 + 1)
                for c in range(0, PATCH_W, 2):
                    k = P if c + 1 < PATCH_W else PATCH_H
                    span = slice(c, c + PATCH_STEP * (SEQ - 1) + 1, PATCH_STEP)
                    pe.matmul(bank[0][0:D, tok(q)], tok_w[0:k, c, :], imgs[0:k, q * GRP:(q + 1) * GRP, span],
                              start=(c == 0), stop=False)
                last = pe.matmul(bank[0][0:D, tok(q)], tok_b[:, :], ones_row[0:1, :], start=False, stop=True)
            last.then_inc(sem("tok_mm"), 1)
            pe.wait_ge(sem("ident_ready"), 1)
            loaded("rows_in")
            pe.transpose(bank[1][:, 0:2 + 2 * NE], rows128[:, :], ident[0:2 + 2 * NE, 0:2 + 2 * NE])
            pe.transpose(bank[1][0:D, 64:64 + 2 * NE + 4], rows64[:, :], ident[0:2 * NE + 4, 0:2 * NE + 4])\
                .then_inc(sem("rows_mm"), 1)
            pe.wait_ge(sem("h0t_ready"), 1)
            for q in range(Q):
                last = pe.transpose(tiles(5)[:, q, :], qt0[:, tok(q)], ident[0:D, 0:D])
            last.then_inc(sem("h0_tr"), 1)

            to_features(xs[0], 2, "x1_ready", "x1_tr")
            loaded("l0_in")
            pe.wait_ge(*nth("x1t_ready"))
            pe.matmul(bank[3][0:D, :], a0_w[:, :], xt[0][:, :], start=True, stop=True).then_inc(sem("q0_mm"), 1)
            pe.wait_ge(sem("qt0_ready"), 1)
            for q in range(Q):
                last = pe.matmul(bank[4][:, tok(q)], xt[0][0:D, tok(q)], qt0[:, tok(q)], start=True, stop=True)
            last.then_inc(sem("s0_mm"), 1)
            pe.wait_ge(sem("att0_ready"), 1)
            for q in range(Q):
                last = pe.matmul(tiles(5)[:, q, :], att0[:, q, :], xs[0][:, q, :], start=True, stop=True)
            last.then_inc(sem("a0_mm"), 1)

            loaded("heads_in")
            for i, r in enumerate((D, D, D, D, D, D // 2, D // 2, NE)):
                pe.transpose(bank[6][0:D, i * D:i * D + r], wnat[0:r, i, :], ident[0:r, 0:r])
            for i in range(2):
                last = pe.transpose(bank[7][:, i * D:(i + 1) * D], wo_pad[:, i, :], ident[0:D, 0:D])
            last.then_inc(sem("heads_tr"), 1)

            to_features(xs[1], 2, "x2_ready", "x2_tr")
            pe.wait_ge(*nth("x2t_ready"))
            for q in range(Q):
                last = pe.matmul(bank[5][:, q:q + 1], xt[1][:, tok(q)], f0_wr[:, 0:1], start=True, stop=True)
            last.then_inc(sem("wr_mm"), 1)
            for c in range(2):
                pe.matmul(bank[3 + c][:, :], f0_w1[:, c * P:(c + 1) * P], xt[1][:, :], start=True, stop=True)\
                    .then_inc(sem("f0_mm"), 1)
            pe.wait_ge(sem("heads_w"), 18)
            pe.wait_ge(sem("wr_spread"), 1)
            pe.matmul(bank[6][:, 0:Q * SEQ], same_tok[:, :], small[:, 0, 0:Q * SEQ], start=True, stop=True)\
                .then_inc(sem("wr_gather_mm"), 1)
            pe.wait_ge(sem("f0_ready"), 2)
            for q in range(Q):
                for c in range(2):
                    pe.matmul(tiles(7)[:, q, :], ht[:, 0, c, tok(q)], f0_w2[:, c, :], start=(c == 0), stop=False)
                last = pe.matmul(tiles(7)[:, q, :], ones_row[0:1, :], f0_b2[:, :], start=False, stop=True)
            last.then_inc(sem("f0_down"), 1)

            to_features(xs[2], 2, "x3_ready", "x3_tr")
            loaded("l1_in")
            pe.wait_ge(*nth("x3t_ready"))
            pe.wait_ge(sem("masks_b"), 2)

            def other_images(b):
                pe.matmul(bank[b][:, :], ident_b[:, :], bc(other_b[:, :], 1, 4), start=True, stop=False)

            def project1(c):
                if c >= 2:
                    pe.wait_ge(sem("qt1_ready"), c - 1)
                pe.matmul(bank[c % 2][:, :], a1_w[:, 0, c * P:(c + 1) * P], xt[2][:, :], start=True, stop=True)\
                    .then_inc(sem("q1_mm"), 1)
                if c >= 2:
                    pe.wait_ge(sem("k1_odd"), c - 1)
                    pe.wait_ge(sem("k1_even"), c - 1)
                pe.matmul(bank[2 + c % 2][:, :], a1_w[:, 1, c * P:(c + 1) * P], xt[2][:, :], start=True, stop=True)\
                    .then_inc(sem("k1_mm"), 1)

            def scores1(c):
                pe.wait_ge(sem("qt1_ready"), c + 1)
                pe.wait_ge(sem("k1_odd"), c + 1)
                pe.wait_ge(sem("k1_even"), c + 1)
                for half in range(2):
                    h = 2 * c + half
                    if h >= 2:
                        pe.wait_ge(sem("s1_comp"), h - 1)
                    other_images(4 + half)
                    for q in range(Q):
                        last = pe.matmul(bank[4 + half][:, tok(q)], qt1[:, c, tok(q)], key_pads[:, h, tok(q)],
                                         start=False, stop=(q == Q - 1))
                    last.then_inc(sem("s1_mm"), 1)

            def values1(q):
                if q >= 2:
                    pe.wait_ge(sem("v1_ready"), q - 1)
                pe.matmul(bank[6 + q % 2][:, :], xt[2][:, tok(q)], a1_w[:, 2, :], start=True, stop=True)\
                    .then_inc(sem("v1_mm"), 1)

            project1(0)
            project1(1)
            scores1(0)
            project1(2)
            scores1(1)
            project1(3)
            scores1(2)
            values1(0)
            scores1(3)
            for q in range(1, Q):
                values1(q)
            pe.wait_ge(sem("v1_ready"), 4)
            for n in range(9):
                if n < 8:
                    pe.wait_ge(sem("a1_wide"), n + 1)
                    if n >= 4:
                        pe.wait_ge(sem("a1_att_t"), n - 3)
                    for k in range(4):
                        last = pe.transpose(bank[4 + n % 4][:, k * P:(k + 1) * P], wide[:, n % 2, k * P:(k + 1) * P],
                                            ident[:, :])
                    last.then_inc(sem("a1_tr"), 1)
                if n >= 1:
                    h = n - 1
                    part = slice((h % 2) * D, (h % 2 + 1) * D)
                    pe.wait_ge(sem("a1_att_t"), h + 1)
                    for q in range(Q):
                        last = pe.matmul(bank[h // 2][part, tok(q)], v1[:, q, h * D:(h + 1) * D],
                                         att_t[:, h % 2, tok(q)], start=True, stop=True)
                    last.then_inc(sem("a1_av"), 1)
            pe.wait_ge(sem("a1_out"), 4)
            for q in range(Q):
                for c in range(4):
                    pe.matmul(tiles(4)[:, q, :], out_t[:, c, tok(q)], a1_wu[:, c, :], start=(c == 0), stop=False)
                last = pe.matmul(tiles(4)[:, q, :], ones_row[0:1, :], a1_bu[:, :], start=False, stop=True)
            last.then_inc(sem("a1_down"), 1)

            loaded("moe3_in")
            for j in range(2):
                for g in range(3):
                    if j:
                        pe.wait_ge(sem("w13_t_ready"), g + 1)
                    blocks = range(4 * g, min(4 * g + 4, NB13))
                    for k in blocks:
                        r = min(P, NE * HID3 - k * P)
                        last = pe.transpose(bank[5 + g][0:D, (k % 4) * P:(k % 4) * P + r], w13_nat[0:r, j, k, :],
                                            ident[0:r, 0:r])
                    last.then_inc(sem("w13_tr"), 1)
            for c, (h0, n) in enumerate(((0, P), (P, TAIL))):
                pe.wait_ge(sem("w13_t_ready"), 4 + c)
                for k in range(NE // 2):
                    last = pe.transpose(bank[5 + c][0:n, tok(k)], w2e_nat[:, k, h0:h0 + n], ident[:, :])
                last.then_inc(sem("w2e_tr"), 1)
            pe.wait_ge(sem("w13_t_ready"), 6)
            pe.wait_ge(sem("w2e_t_ready"), 2)

            loaded("f1_in")
            pe.wait_ge(sem("cols_ready"), 2)
            for e in range(NE):
                for c in range(2):
                    last = pe.matmul(bank[0][:, 2 * e + c:2 * e + c + 1], f1_w1[:, e, c * P:(c + 1) * P],
                                     cols64[:, NE + e:NE + e + 1], start=True, stop=True)
            last.then_inc(sem("f1_shift_mm"), 1)
            to_features(xs[3], 2, "x4_ready", "x4_tr")
            pe.wait_ge(*nth("x4t_ready"))
            for q in range(Q):
                last = pe.matmul(bank[3][:, q * NE:(q + 1) * NE], xt[3][:, tok(q)], f1_wr[:, :], start=True, stop=True)
            last.then_inc(sem("r1_mm"), 1)
            to_features(inner, 1, "x4n_ready", "x4n_tr")

            def down1(e, s):
                pe.wait_ge(sem("f1_ht"), e * 2 + 2)
                if not isinstance(e, int) or e >= 2:
                    pe.wait_ge(sem("f1_gated"), e - 1)
                for q in range(Q):
                    for c in range(2):
                        last = pe.matmul(tiles(1 + s)[:, q, :], ht[:, s, c, tok(q)],
                                         f1_w2[:, ds(e, 1), c, :].rearrange("p e d -> p (e d)"),
                                         start=(c == 0), stop=(c == 1))
                last.then_inc(sem("f1_down"), 1)

            def expert1(i, s):
                e = i * 2 + s
                if first_round(i) and s == 0:
                    pe.wait_ge(*nth("x4nt_ready"))
                    pe.wait_ge(sem("f1_bias_ready"), 1)
                pe.wait_ge(sem("f1_slot_in"), e + 1)
                if not first_round(i):
                    pe.wait_ge(sem("f1_ht"), e * 2 - 2)
                for c in range(2):
                    pe.matmul(bank[4 + 2 * s + c][:, :], f1_slot[:, s, c * P:(c + 1) * P], xt[4][:, :],
                              start=True, stop=True).then_inc(sem("f1_up"), 1)
                if not first_round(i) or s:
                    down1(e - 1, 1 - s)

            over_experts(pe, expert1)
            down1(NE - 1, 1)
            pe.wait_ge(sem("r1_gates"), 1)
            for q in range(Q):
                last = pe.transpose(bank[3][0:NE, tok(q)], gates[:, 0, q, :], ident[:, :])
            last.then_inc(sem("g1_tr"), 1)
            pe.wait_ge(sem("g1t_ready"), 1)
            for q in range(Q):
                last = pe.matmul(tiles(0)[:, q, :], gates_t[:, tok(q)], f1_b2[:, :], start=True, stop=True)
            last.then_inc(sem("b1_mm"), 1)

            pe.wait_ge(sem("heads_bias"), 2)
            pe.matmul(bank[7][:, 0:2 * SEQ], wt[:, 4, :], rel[:, :], start=True, stop=True).then_inc(sem("pos_mm"), 1)
            to_features(inner, 2, "x5n_ready", "x5n_tr")
            pe.wait_ge(*nth("x5nt_ready"))
            for c in range(3):
                pe.matmul(bank[3 + c][:, :], wt[:, c, :], xt[5][:, :], start=True, stop=True)\
                    .then_inc(sem("qk2_mm"), 1)
            for q in range(Q):
                last = pe.matmul(bank[6][:, tok(q)], xt[5][:, tok(q)], wt[:, 3, :], start=True, stop=True)
            last.then_inc(sem("qk2_mm"), 1)
            pe.wait_ge(sem("qk2_ready"), 5)
            pe.wait_ge(sem("k2_ready"), 2)
            pe.wait_ge(sem("pos_bd_ready"), 4)
            for q in range(Q):
                last = pe.matmul(bank[0][:, 0:Q * HEADS4 * 2 * SEQ].rearrange("p (h q r) -> p h q r", h=HEADS4, q=Q)
                                 [:, :, q, :], qk4[:, 1, tok(q)], pos_bd[:, :, :], start=True, stop=True)
            last.then_inc(sem("p2_mm"), 1)

            def attention4(name, out_w, bias):
                for h in range(HEADS4):
                    other_images(1 + h)
                    for q in range(Q):
                        last = pe.matmul(bank[1 + h][:, tok(q)], qk4[:, 0, tok(q)], key_pads[:, h, tok(q)],
                                         start=False, stop=(q == Q - 1))
                    last.then_inc(sem(f"{name}_s_mm"), 1)
                for n in range(HEADS4 + 1):
                    if n < HEADS4:
                        pe.wait_ge(sem(f"{name}_wide"), n + 1)
                        if n >= 2:
                            pe.wait_ge(sem(f"{name}_att_t"), n - 1)
                        for k in range(4):
                            last = pe.transpose(bank[4 + n % 2][:, k * P:(k + 1) * P],
                                                wide[:, n % 2, k * P:(k + 1) * P], ident[:, :])
                        last.then_inc(sem(f"{name}_tr"), 1)
                    if n >= 1:
                        h = n - 1
                        part = slice(h * HPAD, (h + 1) * HPAD)
                        pe.wait_ge(sem(f"{name}_att_t"), h + 1)
                        for q in range(Q):
                            last = pe.matmul(bank[6][part, tok(q)], v4[:, q, part], att_t[:, h % 2, tok(q)],
                                             start=True, stop=True)
                        last.then_inc(sem(f"{name}_av"), 1)
                pe.wait_ge(sem(f"{name}_out"), 1)
                for q in range(Q):
                    last = pe.matmul(tiles(7)[:, q, :], out_t[:, 0, tok(q)], wo_t[:, out_w, :], start=True,
                                     stop=bias is None)
                    if bias is not None:
                        last = pe.matmul(tiles(7)[:, q, :], ones_row[0:1, :], bias, start=False, stop=True)
                last.then_inc(sem(f"{name}_down"), 1)

            attention4("a2", 0, bo2[:, :])

            loaded("tree_in")
            for c, n in ((0, P), (1, NODES - P)):
                last = pe.transpose(bank[3][0:D, c * P:c * P + n], w1s_nat[0:n, c, :], ident[0:n, 0:n])
            last.then_inc(sem("w1s_tr"), 1)
            to_features(xs[5], 2, "x6_ready", "x6_tr")
            pe.wait_ge(*nth("x6t_ready"))
            pe.wait_ge(sem("w1s_ready"), 1)
            for q in range(Q):
                last = pe.matmul(bank[q // 2][:, (q % 2) * 256:(q % 2) * 256 + NODES], xt[6][:, tok(q)],
                                 w1s_t[:, 0:NODES], start=True, stop=True)
            last.then_inc(sem("tree_mm"), 1)
            pe.wait_ge(sem("pathw_ready"), 1)
            for c, n in ((0, P), (1, NODES - P)):
                for q in range(Q):
                    last = pe.transpose(bank[4 + c][0:n, tok(q)], pathw[:, q, c * P:c * P + n], ident[:, :])
                last.then_inc(sem("pathw_tr"), 1)
            pe.wait_ge(sem("pathw_t"), 2)
            for q in range(Q):
                for c, n in ((0, P), (1, NODES - P)):
                    last = pe.matmul(tiles(3)[:, q, :], pathw_t[0:n, c, tok(q)], b2s[0:n, c, :],
                                     start=(c == 0), stop=(c == 1))
            last.then_inc(sem("tree_b2"), 1)
            loaded("w2s_in")

            def transpose_z(k, s):
                pe.wait_ge(sem("z_ready"), k + 1)
                if not isinstance(k, int) or k >= 2:
                    pe.wait_ge(sem("z_t_ready"), k - 1)
                for q in range(Q):
                    last = pe.transpose(bank[s][:, tok(q)], zbuf[:, s, q, :, :].rearrange("p a d -> p (a d)"),
                                        ident[:, :])
                last.then_inc(sem("z_tr"), 1)

            def outputs(k, s, weights):
                pe.wait_ge(sem("z_t_ready"), k + 1)
                for q in range(Q):
                    first = isinstance(k, int) and k == 0
                    last = pe.matmul(bank[4 + q][:, :], z_t[:, s, tok(q)], weights, start=first,
                                     stop=isinstance(k, int) and k == CHUNKS - 1, skip_group_check=True)
                last.then_inc(sem("tree_main"), 1)

            def level_chunks(lv, i, s):
                k = i * 2 + (FIRST_CHUNK[lv] + s)
                parents = w2s[:, 2 ** (lv - 1) - 1:2 ** lv - 1, :].rearrange("p (t c) o -> p t c o", t=8)
                transpose_z(k + 1, 1 - s)
                outputs(k, s, parents[:, :, ds(i * 2 + s, 1), :].rearrange("p t c o -> p t (c o)"))

            transpose_z(0, 0)
            level_chunks(7, 0, 0)
            for lv in (7, 6, 5):
                if lv == 7:
                    level_chunks(lv, 0, 1)
                else:
                    level_chunks(lv, 0, 0)
                    level_chunks(lv, 0, 1)
                if lv > 5:
                    with pe.Fori(1, 2 ** (lv - 5)) as i:
                        level_chunks(lv, i, 0)
                        level_chunks(lv, i, 1)
            level_chunks(4, 0, 0)
            transpose_z(CHUNKS - 1, 0)
            outputs(CHUNKS - 2, 1, w2low[:, 0, :, :])
            outputs(CHUNKS - 1, 0, w2low[:, 1, :, :])

            to_features(fn[:, :, 0:D], 2, "f7_ready", "f7_tr")
            pe.wait_ge(*nth("f7t_ready"))
            for q in range(Q):
                pe.matmul(bank[3 + q][:, :], ft[:, tok(q)], ft[:, :], start=True, stop=True)\
                    .then_inc(sem("sim_mm"), 1)
            pe.wait_ge(sem("sim_exp"), 4)
            for q in range(Q):
                for m in range(Q):
                    last = pe.matmul(bank[7][:, q * (D + 1):(q + 1) * (D + 1)], esim[:, m, tok(q)], fn[:, m, :],
                                     start=(m == 0), stop=(m == Q - 1))
            last.then_inc(sem("sim_av"), 1)

            to_features(inner, 2, "x8n_ready", "x8n_tr")
            pe.wait_ge(*nth("x8nt_ready"))
            for c in range(4):
                pe.matmul(bank[3 + c][:, :], wt[:, 5 + c, :], xt[8][:, :], start=True, stop=True)\
                    .then_inc(sem("qk3_mm"), 1)
            for q in range(Q):
                last = pe.matmul(bank[7][:, tok(q)], xt[8][:, tok(q)], wt_v3[:, :], start=True, stop=True)
            last.then_inc(sem("qk3_mm"), 1)
            pe.wait_ge(sem("v3_ready"), 1)
            pe.wait_ge(sem("qk3_ready"), 5)
            attention4("a3", 1, None)
            to_features(inner, 2, "x9n_ready", "x9n_tr")
            pe.wait_ge(*nth("x9nt_ready"))
            for q in range(Q):
                last = pe.matmul(bank[7][:, q * NE:(q + 1) * NE], xt[9][:, tok(q)], router_t[:, :],
                                 start=True, stop=True)
            last.then_inc(sem("r3_mm"), 1)

            def down3(e, s):
                pe.wait_ge(sem("f3_ht"), e * 2 + 2)
                if not isinstance(e, int) or e >= 2:
                    pe.wait_ge(sem("f3_gated"), e - 1)
                for q in range(Q):
                    pe.matmul(tiles(6 + s)[:, q, :], ht[:, s, 0, tok(q)], w2e_t[:, 0, ds(e * D, D)],
                              start=True, stop=False)
                    last = pe.matmul(tiles(6 + s)[:, q, :], ht[0:TAIL, s, 1, tok(q)],
                                     w2e_t[0:TAIL, 1, ds(e * D, D)], start=False, stop=True)
                last.then_inc(sem("f3_down"), 1)

            def expert3(i, s):
                e = i * 2 + s
                pe.wait_ge(sem(f"e3_slot_in{s}"), i * 4 + 4)
                if not first_round(i):
                    pe.wait_ge(sem("f3_ht"), e * 2 - 2)
                for c in range(3):
                    m = P if c < 2 else D + TAIL
                    pe.matmul(bank[3 * s + c][0:m, :], e3_slot[:, s, c * P:c * P + m], xt[9][:, :],
                              start=True, stop=True).then_inc(sem("f3_up"), 1)
                if not first_round(i) or s:
                    down3(e - 1, 1 - s)

            over_experts(pe, expert3)
            down3(NE - 1, 1)


_INS = ["x", "L0_tok_weight", "L0_tok_bias", "L0_attn_q_weight", "L0_ffn_wr", "L0_ffn_br", "L0_ffn_w1",
        "L0_ffn_b1", "L0_ffn_w2", "L0_ffn_b2", "L1_attn_Wq", "L1_attn_bq", "L1_attn_Wk", "L1_attn_bk",
        "L1_attn_Wv", "L1_attn_bv", "L1_attn_Wu", "L1_attn_bu", "L1_ffn_Wr", "L1_ffn_br", "L1_ffn_ln_g",
        "L1_ffn_ln_b", "L1_ffn_W1", "L1_ffn_b1", "L1_ffn_W2", "L1_ffn_b2", "L2_attn_ln_gamma",
        "L2_attn_ln_beta", "L2_attn_Wq", "L2_attn_bq", "L2_attn_Wk", "L2_attn_bk", "L2_attn_Wv", "L2_attn_bv",
        "L2_attn_Wpos", "L2_attn_bpos", "L2_attn_Wo", "L2_attn_bo", "L2_attn_u_bias", "L2_attn_v_bias",
        "L2_ffn_w1s", "L2_ffn_b1s", "L2_ffn_w2s", "L2_ffn_b2s", "L3_ffn_ln1_w", "L3_ffn_ln2_w", "L3_ffn_wq",
        "L3_ffn_wk", "L3_ffn_wv", "L3_ffn_wo", "L3_ffn_router_w", "L3_ffn_w1", "L3_ffn_w2", "L3_ffn_w3"]


def kernel(**inputs):
    import numpy as _np
    import concourse.bacc as _bacc
    from concourse import mybir as _mybir
    from concourse.bass_utils import run_bass_kernel_spmd as _run

    nc = _bacc.Bacc("TRN2", target_bir_lowering=False, num_devices=1)
    arrays, drams = {}, {}
    rope, rel = shape_constants()
    for name, value in [(n, inputs[n]) for n in _INS] + [("rope", rope), ("rel", rel)]:
        value = _np.ascontiguousarray(value)
        arrays[f"in_{name}_dram"] = value
        drams[name] = nc.dram_tensor(f"in_{name}_dram", value.shape, _mybir.dt.from_np(value.dtype),
                                     kind="ExternalInput").ap()
    out = nc.dram_tensor("out_0_dram", (N_IMG, SEQ, D), F32, kind="ExternalOutput").ap()
    vit_tower(nc, drams, drams["rope"], drams["rel"], out)
    r = _run(nc, [arrays], core_ids=[0])
    return r.results[0]["out_0_dram"]
```

```python
import math
from contextlib import ExitStack

import concourse.bass as bass
import numpy as np
from concourse import mybir

P = 128
D = 64
F32 = mybir.dt.float32
BF16 = mybir.dt.bfloat16
ALU = mybir.AluOpType
ACT = mybir.ActivationFunctionType
X = mybir.AxisListType.X
ds = bass.ds

N_IMG = 64
IMG_H = IMG_W = 112
PATCH_H, PATCH_W, PATCH_STEP = 64, 25, 12
SEQ = (IMG_W - PATCH_W) // PATCH_STEP + 1
T = N_IMG * SEQ
Q = T // P
GRP = P // SEQ
HEADS4, HD, HPAD = 4, 16, 32
MAX_REL = 30
NE = 8
NODES = 255
PARENTS = NODES // 2
HID3 = int(8 / 3 * D)
TAIL = HID3 - P
BIG = 1e30


def shape_constants():
    inv_freq = 1.0 / 10000.0 ** (np.arange(0, HD, 2, dtype=np.float32) / HD)
    freqs = np.outer(np.arange(SEQ, dtype=np.float32), inv_freq)
    emb = np.concatenate([freqs, freqs], axis=-1).astype(np.float32)
    rope = np.zeros((P, 2, SEQ), np.float32)
    for h in range(HEADS4):
        rope[h * HPAD:h * HPAD + HD, 0] = np.cos(emb).T
        rope[h * HPAD:h * HPAD + HD, 1] = np.sin(emb).T
    n = 2 * MAX_REL + 1
    div = np.exp(np.arange(0, D, 2, dtype=np.float32) * np.float32(-math.log(10000.0) / D))
    ang = (np.arange(n, dtype=np.float32)[:, None] * div).astype(np.float32)
    enc = np.stack([np.sin(ang), np.cos(ang)], axis=-1).reshape(n, D).astype(np.float32)
    rel = np.ones((D + 1, 2 * SEQ), np.float32)
    rel[:D, 2 * SEQ - 1] = 0.0
    rel[:D, :2 * SEQ - 1] = enc[MAX_REL - SEQ + 1:MAX_REL + SEQ].T
    return rope, rel


def bc(ap, axis, n):
    ap = ap.unsqueeze(axis)
    shape = list(ap.shape)
    shape[axis] = n
    return ap.broadcast_to(tuple(shape))


def vit_tower(nc, a, rope_dram, rel_dram, out):
    ctx = ExitStack()
    with ctx:
        ctx.enter_context(nc.allow_non_contiguous_dma("weights in layouts of their own"))
        sems = {}
        STEPS = {
            "constants": ("probe_zeroed", "padded_zeroed", "pads_zeroed", "w2e_tails_zeroed", "ft_zeroed",
                          "half_neg_ready", "ones_ready", "ident_ready", "same_ready", "same_lt_ready",
                          "lower8_ready", "pos_bd_zeroed"),
            "normed": ("x1_ready", "x2_ready", "x3_ready", "x4n_ready", "x4_ready", "x5n_ready",
                       "x6_ready", "f7_ready", "c7_ready", "x8n_ready", "x8_ready", "x9n_ready"),
            "features_tr": ("x1_tr", "x2_tr", "x3_tr", "x4n_tr", "x4_tr", "x5n_tr", "x6_tr", "f7_tr", "x8n_tr",
                            "x9n_tr"),
            "features_by_act": ("x1t_ready", "x2t_ready", "x3t_ready", "x4nt_ready", "x4t_ready", "x6t_ready",
                                "f7t_ready"),
            "features_by_dve": ("x5nt_ready", "x8nt_ready", "x9nt_ready"),
            "variance": ("x1_var", "x2_var", "x3_var", "x4_var", "x5_var", "x6_var", "f7_var", "c7_var",
                         "x8_var", "x9_var"),
        }
        ROOTS = (("x1", 0), ("x2", 0), ("x3", 0), ("x4", 1), ("x4", 0), ("x5", 0), ("x6", 0), ("f7", 0), ("c7", 0),
                 ("x8", 1), ("x8", 0), ("x9", 0))
        STEP = {name: (counter, n) for counter, names in STEPS.items() for n, name in enumerate(names)}

        def nth(name, value=1):
            return sem(name), value + (STEP[name][1] if name in STEP else 0)

        def tile_of(name, q=Q - 1):
            return sem(name), STEP[name][1] * Q + q + 1

        def sem(name):
            name = STEP[name][0] if name in STEP else name
            if name not in sems:
                sems[name] = ctx.enter_context(nc.semaphore(name))
            return sems[name]

        def sb(name, shape, dt=F32):
            return ctx.enter_context(nc.sbuf_tensor(name, shape, dt))

        bank = [ctx.enter_context(nc.psum_tensor(f"bank{i}", [P, 512], F32)) for i in range(8)]

        def tiles(b, n=D):
            return bank[b][:, 0:Q * n].rearrange("p (q n) -> p q n", q=Q)

        def views(region, *shapes):
            at = 0
            for shape in shapes:
                n = int(np.prod(shape))
                names = " ".join("abc"[:len(shape)])
                yield region[:, at:at + n].rearrange(f"p ({names}) -> p {names}", **dict(zip("abc", shape)))
                at += n

        region_a = sb("region_a", [P, N_IMG * IMG_W])
        region_b = sb("region_b", [P, (4 + 8 + 4) * T])
        region_c = sb("region_c", [P, PATCH_W * D])
        imgs, = views(region_a, (N_IMG, IMG_W))
        pathw, onehot, right, esim, silu = views(region_a, (Q, 256), (Q, 256), (Q, 256), (Q, T), (4, T))
        picked = esim
        out_t = silu
        silu = silu.rearrange("p (s c) t -> p s c t", s=2)
        qt0 = region_b[0:D, 12 * T:13 * T]
        tok_half = region_b[0:D, 13 * T:14 * T]
        att0 = region_b[:, 13 * T:14 * T].rearrange("p (q n) -> p q n", q=Q)
        key_pads, qt1, v1 = views(region_b, (8, T), (4, T), (Q, 512))
        _, qk4, v4 = views(region_b, (8, T), (4, T), (Q, P))
        z_t, zbuf, pathw_t = views(region_b, (2, T), (2, Q * 2 * D), (2, T))
        zbuf = zbuf.rearrange("p b (q s d) -> p b q s d", q=Q, s=2)
        tok_w, tok_w_last = views(region_c, (PATCH_STEP // 2, 2 * D), (1, D))
        wide, ranks = views(region_c, (2, 512), (2, Q * NE * NE))
        padded = sb("padded", [P, 64 + 8 + 256 + 3 * 512 + NE + 9 * P + P + NE + 256 + 6 * P + 512 + 2 * SEQ])
        (a0_w, f0_wr, f0_w1, a1_w, f1_wr, wt, wt_v3, router_t, w1s_t, e3_slot, f1_slot, rel) = views(
            padded, (D,), (8,), (256,), (3, 512), (NE,), (9, P), (P,), (NE,), (256,), (2, 3 * P), (2, 256),
            (2 * SEQ,))
        ident = sb("ident", [P, P])
        same = sb("same", [P, GRP])
        same_tok = sb("same_tok", [P, P])
        same_lt = sb("same_lt", [P, P])
        pos1h = sb("pos1h", [P, SEQ])
        before = sb("before", [P, SEQ])
        strict_bias = sb("strict_bias", [P, SEQ])
        causal_bias = sb("causal_bias", [P, SEQ])
        not_first = sb("not_first", [P, 1])
        lower8 = sb("lower8", [P, NE, NE])
        ones_row = sb("ones_row", [P, P])
        rope = sb("rope", [P, 2, SEQ])
        tok_b = sb("tok_b", [1, D])
        f0_w2 = sb("f0_w2", [P, 2, D])
        f0_b2 = sb("f0_b2", [1, D])
        rows128 = sb("rows128", [2 + 2 * NE, P])
        cols128 = sb("cols128", [P, 2 + 2 * NE])
        rows64 = sb("rows64", [2 * NE + 4, D])
        cols64 = sb("cols64", [D, 2 * NE + 4])
        a1_wu = sb("a1_wu", [P, 4, D])
        a1_bu = sb("a1_bu", [1, D])
        f1_w1 = sb("f1_w1", [D, NE, 256])
        f1_w2 = sb("f1_w2", [P, NE, 2, D])
        f1_bias = sb("f1_bias", [P, 2 * NE])
        f1_b2 = sb("f1_b2", [NE, D])
        wnat = sb("wnat", [D, 8, D])
        wo_pad = sb("wo_pad", [D, 2, P])
        uv_rows = sb("uv_rows", [D + 1, 2, D])
        wo_t = sb("wo_t", [P, 2, D])
        bo2 = sb("bo2", [1, D])
        w1s_nat = sb("w1s_nat", [P, 2, D])
        b2s = sb("b2s", [P, 2, D])
        w2s = sb("w2s", [P, PARENTS, D])
        w2low = sb("w2low", [P, 8 + 2, D])
        NB13 = -(-NE * HID3 // P)
        w13_nat = sb("w13_nat", [P, 2, NB13, D])
        w13_t = sb("w13_t", [D, 2, NB13 * P])
        w2e_nat = sb("w2e_nat", [P, NE // 2, HID3])
        w2e_t = sb("w2e_t", [P, 2, NE * D])
        CHUNKS = 17
        FIRST_CHUNK = {7: 1, 6: 9, 5: 13, 4: 15}
        hs = [sb(f"h{i}", [P, Q, D]) for i in range(2)] * 4
        xs = [sb(f"x{i}", [P, Q, D]) for i in range(2)] * 4
        xc = sb("xc", [P, Q, D])
        sq = sb("sq", [P, Q, D])
        st = sb("st", [P, 8, Q])
        xt = [sb(f"xt{i}", [P, T]) for i in range(3)]
        xt = [xt[i % 3] for i in range(10)]
        ft = sb("ft", [P, T])
        bst = sb("bst", [P, Q, 6])
        mv = sb("mv", [P, Q, 2])
        var2 = sb("var2", [P, 2, Q])
        rs = sb("rs", [P, 2, Q])
        rs_t = sb("rs_t", [P, 2, Q])
        half_neg = sb("half_neg", [P, Q])
        ident_b = sb("ident_b", [P, P], BF16)
        other_b = sb("other_b", [P, P], BF16)
        upath = sb("upath", [P, Q, CHUNKS, 2])
        inner = sb("inner", [P, Q, D])
        small = sb("small", [P, 8, Q * NE])
        ht = sb("ht", [P, 2, 2, T])
        comp = sb("comp", [P, 32, SEQ])
        cexp = sb("cexp", [P, 32, SEQ])
        att_t = sb("att_t", [P, 2, 512])
        gates = sb("gates", [P, 2, Q, NE])
        gates_t = sb("gates_t", [NE, T])
        yacc = sb("yacc", [P, Q, D])
        ytmp = sb("ytmp", [P, 2, Q, D])
        posadd = sb("posadd", [P, Q * HEADS4, SEQ])
        pos_bd = sb("pos_bd", [P, HEADS4, 2 * SEQ])
        fn = sb("fn", [P, Q, D + 1])
        table_probe = sb("table_probe", [1, 1])

        block = ctx.enter_context(nc.Block())

        def first_round(i):
            return isinstance(i, int) and i == 0

        def over_pairs(eng, step, rounds):
            step(0, 0)
            step(0, 1)
            with eng.Fori(1, rounds) as i:
                step(i, 0)
                step(i, 1)

        def over_experts(eng, step):
            over_pairs(eng, step, NE // 2)

        SIM_BANKS = (0, 1, 2, 7)

        W = {}

        @block.sync
        def _(sp):
            def load(name, dst, src):
                W[name] = W.get(name, 0) + 16
                sp.dma_start(dst, src).then_inc(sem(name), 16)

            patch_rows = a["x"][:, 0, 0:PATCH_H, :].rearrange("b r w -> r b w")
            tw = a["L0_tok_weight"].rearrange("(r c) d -> r c d", c=PATCH_W)
            for s in range(2):
                for half in range(2):
                    load("tok_w_in", tok_w[s * PATCH_H:(s + 1) * PATCH_H, :, half * D:(half + 1) * D],
                         tw[:, half * PATCH_STEP + s:(half + 1) * PATCH_STEP:2, :])
            load("tok_w_in", tok_w_last[0:PATCH_H, :, :], tw[:, PATCH_W - 1:PATCH_W, :])
            load("tok_w_in", tok_b[:, :], a["L0_tok_bias"].unsqueeze(0))
            for q in range(Q):
                mine = slice(q * GRP, (q + 1) * GRP)
                load(f"img_in{q}", imgs[0:PATCH_H, mine, :], patch_rows[:, mine, :])
            sp.wait_ge(*nth("padded_zeroed"))
            load("l0_in", a0_w[0:D, :], a["L0_attn_q_weight"])
            load("l0_in", f0_wr[0:D, 0:1], a["L0_ffn_wr"])
            load("l0_in", f0_wr[D:D + 1, 0:1], a["L0_ffn_br"].unsqueeze(0))
            load("l0_in", f0_w1[0:D, :], a["L0_ffn_w1"])
            load("l0_in", f0_w2[:, :, :], a["L0_ffn_w2"].rearrange("(c k) d -> k c d", c=2))
            load("l0_in", f0_b2[:, :], a["L0_ffn_b2"].unsqueeze(0))
            load("rows_in", rows128[0:2, :], a["L0_ffn_b1"].rearrange("(c k) -> c k", c=2))
            load("rows_in", rows128[2:2 + 2 * NE, :], a["L1_ffn_b1"].rearrange("e (c k) -> (e c) k", c=2))
            load("rows_in", rows64[0:NE, :], a["L1_ffn_ln_g"])
            load("rows_in", rows64[NE:2 * NE, :], a["L1_ffn_ln_b"])
            for i, n in enumerate(("L2_attn_ln_gamma", "L2_attn_ln_beta", "L3_ffn_ln1_w", "L3_ffn_ln2_w")):
                load("rows_in", rows64[2 * NE + i:2 * NE + i + 1, :], a[n].unsqueeze(0))
            for i, n in enumerate("qkv"):
                load("l1_in", a1_w[0:D, i, :], a[f"L1_attn_W{n}"])
                load("l1_in", a1_w[D:D + 1, i, :], a[f"L1_attn_b{n}"].unsqueeze(0))
            load("l1_in", a1_wu[:, :, :], a["L1_attn_Wu"].rearrange("(c k) d -> k c d", c=4))
            load("l1_in", a1_bu[:, :], a["L1_attn_bu"].unsqueeze(0))
            load("l1_in", f1_wr[0:D, :], a["L1_ffn_Wr"])
            load("l1_in", f1_wr[D:D + 1, :], a["L1_ffn_br"].unsqueeze(0))
            load("l1_in", f1_b2[:, :], a["L1_ffn_b2"])
            load("l1_in", f1_w1[:, :, :], a["L1_ffn_W1"].rearrange("e d h -> d e h"))

            load("heads_in", rope[:, :, :], rope_dram)
            load("heads_in", rel[0:D + 1, :], rel_dram)
            for i, n in enumerate(("L2_attn_Wq", "L2_attn_Wk", "L2_attn_Wv", "L2_attn_Wpos")):
                load("heads_in", wnat[:, i, :], a[n])
            for i, (n, r) in enumerate((("L3_ffn_wq", D), ("L3_ffn_wk", D // 2), ("L3_ffn_wv", D // 2),
                                        ("L3_ffn_router_w", NE))):
                load("heads_in", wnat[0:r, 4 + i, :], a[n])
            sp.wait_ge(*nth("pads_zeroed"))
            for i, n in enumerate(("L2_attn_Wo", "L3_ffn_wo")):
                load("heads_in", wo_pad[:, i, :].rearrange("o (h d) -> o h d", h=HEADS4)[:, :, 0:HD],
                     a[n].rearrange("o (h d) -> o h d", h=HEADS4))
            for i, n in ((2, "k"), (3, "v"), (4, "pos")):
                load("heads_in", wt[D:D + 1, i, :].rearrange("o (h d) -> o h d", h=HEADS4)[:, :, 0:HD],
                     a[f"L2_attn_b{n}"].rearrange("(o h d) -> o h d", o=1, h=HEADS4))
            load("heads_in", uv_rows[D:D + 1, 0, :], a["L2_attn_bq"].unsqueeze(0))
            for i, n in ((0, "u"), (1, "v")):
                load("heads_in", wt[D:D + 1, i, :].rearrange("o (h d) -> o h d", h=HEADS4)[:, :, 0:HD],
                     a[f"L2_attn_{n}_bias"].rearrange("o h a d -> o (h a) d"))
            load("heads_in", bo2[:, :], a["L2_attn_bo"].unsqueeze(0))

            load("tree_in", w1s_nat[:, 0, :], a["L2_ffn_w1s"][0:P, :])
            load("tree_in", w1s_nat[0:NODES - P, 1, :], a["L2_ffn_w1s"][P:NODES, :])
            load("tree_in", w1s_t[D:D + 1, 0:NODES], a["L2_ffn_b1s"].unsqueeze(0))
            load("tree_in", b2s[:, 0, :], a["L2_ffn_b2s"][0:P, :])
            load("tree_in", b2s[0:NODES - P, 1, :], a["L2_ffn_b2s"][P:NODES, :])

            rows = (NE * HID3) // P
            for i, n in enumerate(("w1", "w3")):
                flat = a[f"L3_ffn_{n}"].rearrange("e h c -> (e h) c")
                load("moe3_in", w13_nat[:, i, 0:rows, :], flat[0:rows * P, :].rearrange("(k p) c -> p k c", p=P))
                load("moe3_in", w13_nat[0:NE * HID3 - rows * P, i, rows, :], flat[rows * P:NE * HID3, :])
            load("moe3_in", w2e_nat[:, :, :], a["L3_ffn_w2"].rearrange("(k e) c h -> (e c) k h", e=2))
            load("f1_in", f1_w2[:, :, 0, :], a["L1_ffn_W2"][:, 0:P, :].rearrange("e k d -> k e d"))
            load("f1_in", f1_w2[:, :, 1, :], a["L1_ffn_W2"][:, P:2 * P, :].rearrange("e k d -> k e d"))
            for side in range(2):
                load("w2s_in", w2s[side * D:(side + 1) * D, :, :],
                     a["L2_ffn_w2s"][1:NODES, :, :].rearrange("(m s) d o -> s d m o", s=2)[side])
            for lv, side, cols, reps in ((3, 0, slice(0, 8), 1), (2, 1, slice(0, 8), 2), (1, 0, slice(8, 10), 1),
                                         (0, 1, slice(8, 10), 2)):
                dst = w2low[side * D:(side + 1) * D, cols, :].rearrange("d (n r) o -> d n r o", r=reps)
                for r in range(reps):
                    load("w2s_in", dst[:, :, r, :], a["L2_ffn_w2s"][2 ** lv - 1:2 ** (lv + 1) - 1].rearrange(
                        "n d o -> d n o"))

            sp.wait_ge(sem("f3_acc"), NE // 2 + 1)
            sp.dma_start(out.rearrange("(q g) n d -> (g n) q d", q=Q), yacc[:, :, :]).then_inc(sem("out_done"), 16)
            sp.wait_ge(sem("out_done"), 16)

        @block.gpsimd
        def _(pool):
            made = [0]

            def link(ins):
                made[0] += 1
                ins.then_inc(sem("pool_step"), 1)
                pool.wait_ge(sem("pool_step"), made[0])

            pool.memset(table_probe[:, :], 0.0).then_inc(sem("probe_zeroed"), 1)
            pool.memset(padded[:, :], 0.0).then_inc(sem("padded_zeroed"), 1)
            pool.memset(wo_pad[:, :, :], 0.0).then_inc(sem("pads_zeroed"), 1)
            pool.memset(w2e_t[:, 1, :], 0.0).then_inc(sem("w2e_tails_zeroed"), 1)
            pool.memset(ft[:, :], 0.0).then_inc(sem("ft_zeroed"), 1)
            pool.memset(half_neg[:, :], -0.5).then_inc(sem("half_neg_ready"), 1)
            pool.memset(ones_row[:, :], 1.0).then_inc(sem("ones_ready"), 1)
            link(pool.memset(ident[:, :], 0.0))
            pool.affine_select(out=ident[:, :], in_=ident[:, :], compare_op=ALU.not_equal, fill=1.0, base=0,
                               pattern=[[-1, P]], channel_multiplier=1).then_inc(sem("ident_ready"), 1)
            pool.wait_ge(*nth("ident_ready"))
            pool.tensor_copy(ident_b[:, :], ident[:, :]).then_inc(sem("masks_b"), 1)
            link(pool.memset(same[:, :], 1.0))
            link(pool.affine_select(out=same[:, :], in_=same[:, :], compare_op=ALU.is_ge, fill=0.0, base=0,
                                    pattern=[[-SEQ, GRP]], channel_multiplier=1))
            link(pool.affine_select(out=same[:, :], in_=same[:, :], compare_op=ALU.is_ge, fill=0.0,
                                    base=SEQ - 1, pattern=[[SEQ, GRP]], channel_multiplier=-1))
            pool.tensor_copy(same_tok[:, :].rearrange("p (g j) -> p g j", g=GRP), bc(same[:, :], 2, SEQ))\
                .then_inc(sem("same_ready"), 1)
            pool.wait_ge(*nth("same_ready"))
            pool.tensor_scalar(other_b[:, :], same_tok[:, :], BIG, -BIG, ALU.mult, ALU.add)\
                .then_inc(sem("masks_b"), 1)
            pool.affine_select(out=same_lt[:, :], in_=same_tok[:, :], compare_op=ALU.is_gt, fill=0.0, base=0,
                               pattern=[[-1, P]], channel_multiplier=1).then_inc(sem("same_lt_ready"), 1)
            link(pool.memset(lower8[:, :, :], 1.0))
            pool.affine_select(out=lower8[:, :, :], in_=lower8[:, :, :], compare_op=ALU.is_gt, fill=0.0, base=0,
                               pattern=[[1, NE], [-1, NE]], channel_multiplier=0)\
                .then_inc(sem("lower8_ready"), 1)
            pool.memset(pos_bd[:, :, :], 0.0).then_inc(sem("pos_bd_zeroed"), 1)
            pool.memset(key_pads[:, :, :], 0.0).then_inc(sem("keys_zeroed"), 1)
            pool.memset(fn[:, :, D:D + 1], 1.0 / (1.0 - 0.8)).then_inc(sem("fn_ones"), 1)

            def root(name, row):
                pool.wait_ge(*nth(f"{name}_var"))
                pool.tensor_tensor(rs[:, row, :], var2[:, row, :], half_neg[:, :], ALU.pow)\
                    .then_inc(sem("rooted"), 1)

            pool.wait_ge(*nth("half_neg_ready"))
            for name, row in ROOTS[0:5]:
                root(name, row)
            pool.wait_ge(sem("a1_out"), 4)
            pool.memset(key_pads[:, 0:4, :], 0.0).then_inc(sem("keys_zeroed"), 1)
            for name, row in ROOTS[5:7]:
                root(name, row)
            for q in range(2):
                pool.wait_ge(sem("tree_picked"), q + 1)
                for n in (4 * D, 2 * D):
                    link(pool.tensor_tensor(picked[:, q, 0:n], picked[:, q, 0:n], picked[:, q, n:2 * n], ALU.add))
                pool.tensor_tensor(inner[:, q, :], picked[:, q, 0:D], picked[:, q, D:2 * D], ALU.add)\
                    .then_inc(sem("tree_summed"), 1)
            root(*ROOTS[7])
            pool.memset(key_pads[:, 0:4, :], 0.0).then_inc(sem("keys_zeroed"), 1)
            for name, row in ROOTS[8:]:
                root(name, row)

            pool.wait_ge(sem("w13_t_ready"), 6)

            def fill_slot(i, s):
                e = i * 2 + s
                if not first_round(i):
                    pool.wait_ge(sem("f3_up"), e * 3 - 3)
                for j in range(2):
                    pool.tensor_copy(e3_slot[0:D, s, j * P:(j + 1) * P], w13_t[:, j, ds(e * HID3, P)])\
                        .then_inc(sem(f"e3_slot_in{s}"), 1)
                    pool.tensor_copy(e3_slot[0:D, s, 2 * P + j * D:2 * P + j * D + TAIL],
                                     w13_t[:, j, ds(e * HID3 + P, TAIL)]).then_inc(sem(f"e3_slot_in{s}"), 1)

            over_experts(pool, fill_slot)

        @block.scalar
        def _(act):
            def evac(dst, src, wait, value, done, func=ACT.Copy, **kw):
                act.wait_ge(*nth(wait, value))
                return act.activation(dst, src, func, **kw).then_inc(sem(done), 1)

            def table_for(func):
                act.activation(table_probe[:, :], table_probe[:, :], func)

            act.wait_ge(*nth("probe_zeroed"))
            table_for(ACT.Gelu)
            for q in (0, 2):
                act.wait_ge(sem(f"img_in{q}"), W[f"img_in{q}"])
                act.activation(imgs[PATCH_H:P, q * GRP:(q + 1) * GRP, 0:IMG_W:2],
                               imgs[0:PATCH_H, q * GRP:(q + 1) * GRP, 1:IMG_W:2], ACT.Copy)\
                   .then_inc(sem("img_shifted_act"), 1)
            by_image = lambda ap: ap.rearrange("p (g j) -> p g j", g=GRP)
            for q in range(Q + 1):
                if q < Q:
                    evac(by_image(tok_half[:, q * P:(q + 1) * P]),
                         by_image(bank[q][D:P, 0:GRP * (SEQ + 1)])[:, :, 1:SEQ + 1], "tok_mm", q + 1, "tok_half_ready")
                if q:
                    last = qt0[:, (q - 1) * P:q * P]
                    evac(last, last, "tok_sum", q, "h0t_ready", ACT.Gelu)
            evac(hs[0][:, :, :], tiles(5), "h0_tr", Q, "h0_ready")
            table_for(ACT.Sigmoid)
            evac(cols128[:, :], bank[7][:, 0:2 + 2 * NE], "rows_mm", 1, "cols_ready")
            evac(cols64[:, :], bank[7][0:D, 64:64 + 2 * NE + 4], "rows_mm", 1, "cols_ready")
            evac(xt[0][0:D, :], bank[2][0:D, :], "x1_tr", 1, "x1t_ready")
            evac(qt0[:, :], bank[3][0:D, :], "q0_mm", 1, "qt0_ready")
            evac(att0[:, :, :], tiles(4, P), "s0_mm", 1, "sig_ready", ACT.Sigmoid)
            table_for(ACT.Gelu_apprx_tanh)
            act.wait_ge(sem("heads_tr"), 1)
            act.wait_ge(*nth("pads_zeroed"))
            hv = lambda ap: ap.rearrange("p (h d) -> p h d", h=HEADS4)
            tr = lambda i: bank[6][0:D, i * D:(i + 1) * D].rearrange("p (h d) -> p h d", d=HD)
            for slot, i in ((0, 0), (1, 0), (2, 1), (3, 2), (4, 3), (5, 4)):
                act.activation(hv(wt[0:D, slot, :])[:, :, 0:HD], tr(i), ACT.Copy).then_inc(sem("heads_w"), 1)
            half = HD // 2
            act.activation(hv(wt[0:D, 6, :])[:, :, 0:half], tr(4)[:, :, half:HD], ACT.Copy, scale=-1.0)\
                .then_inc(sem("heads_w"), 1)
            act.activation(hv(wt[0:D, 6, :])[:, :, half:HD], tr(4)[:, :, 0:half], ACT.Copy)\
                .then_inc(sem("heads_w"), 1)
            for rep in range(2):
                two = lambda ap: ap.rearrange("p (k r d) -> p k r d", k=2, r=2)[:, :, rep, :]
                k3, v3 = (bank[6][0:D, i * D:i * D + 32].rearrange("p (k d) -> p k d", k=2) for i in (5, 6))
                act.activation(two(wt[0:D, 7, :])[:, :, 0:HD], k3, ACT.Copy).then_inc(sem("heads_w"), 1)
                act.activation(two(wt[0:D, 8, :])[:, :, 0:half], k3[:, :, half:HD], ACT.Copy, scale=-1.0)\
                    .then_inc(sem("heads_w"), 1)
                act.activation(two(wt[0:D, 8, :])[:, :, half:HD], k3[:, :, 0:half], ACT.Copy)\
                    .then_inc(sem("heads_w"), 1)
                act.activation(two(wt_v3[0:D, :])[:, :, 0:HD], v3, ACT.Copy).then_inc(sem("heads_w"), 1)
            act.activation(router_t[0:D, :], bank[6][0:D, 7 * D:7 * D + NE], ACT.Copy).then_inc(sem("heads_w"), 1)
            act.activation(wo_t[:, :, :], bank[7][:, 0:2 * D].rearrange("p (i o) -> p i o", i=2), ACT.Copy)\
                .then_inc(sem("heads_w"), 1)

            evac(xt[1][0:D, :], bank[2][0:D, :], "x2_tr", 1, "x2t_ready")
            for c in range(2):
                evac(ht[:, 0, c, :], bank[3 + c][:, :], "f0_mm", c + 1, "f0_ready", ACT.Gelu_apprx_tanh,
                     bias=cols128[:, c:c + 1])

            table_for(ACT.Exp)
            evac(xt[2][0:D, :], bank[2][0:D, :], "x3_tr", 1, "x3t_ready")
            act.wait_ge(sem("keys_zeroed"), 1)
            for c in range(4):
                evac(qt1[:, c, :], bank[c % 2][:, :], "q1_mm", c + 1, "qt1_ready")
                evac(key_pads[D:P, 2 * c + 1, :], bank[2 + c % 2][D:P, :], "k1_mm", c + 1, "k1_odd")
            for half in range(2):
                blocks = slice(16 * half, 16 * half + 16)
                evac(cexp[:, blocks, :], comp[:, blocks, :], "a1_shifted", half + 1, "a1_exp", ACT.Exp,
                     scale=1.0 / 8.0)
                if half == 0:
                    for q in range(Q):
                        evac(v1[:, q, :], bank[q][:, :], "v1_mm", q + 1, "v1_ready")
            for b in range(10):
                if 2 <= b < 8:
                    act.wait_ge(sem("a1_av"), b - 1)
                if b < 8:
                    evac(att_t[:, b % 2, :], bank[4 + b % 4][:, :], "a1_tr", b + 1, "a1_att_t")
                c = (b - 3) // 2
                if b >= 3 and b % 2:
                    evac(out_t[:, c, :], bank[c][:, :], "a1_av", 2 * c + 2, "a1_out")

            evac(xt[4][0:D, :], bank[1][0:D, :], "x4n_tr", 1, "x4nt_ready")
            evac(xt[3][0:D, :], bank[2][0:D, :], "x4_tr", 1, "x4t_ready")
            evac(small[:, 0, 0:Q * NE].rearrange("p (q e) -> p q e", q=Q),
                 small[:, 1, 0:Q * NE].rearrange("p (q e) -> p q e", q=Q), "r1_shifted", 1, "r1_exp", ACT.Exp)
            table_for(ACT.Gelu)

            def gelu1(i, s):
                e = i * 2 + s
                if not first_round(i):
                    act.wait_ge(sem("f1_down"), e - 1)
                for c in range(2):
                    evac(ht[:, s, c, :], bank[4 + 2 * s + c][:, :], "f1_up", e * 2 + (c + 1), "f1_ht",
                         ACT.Gelu, bias=f1_bias[:, ds(e * 2 + c, 1)])

            act.wait_ge(sem("f1_bias_ready"), 1)
            over_experts(act, gelu1)
            evac(gates_t[:, :], bank[3][0:NE, :], "g1_tr", 1, "g1t_ready")

            table_for(ACT.Exp)
            act.wait_ge(sem("pos_mm"), 1)
            act.wait_ge(*nth("pos_bd_zeroed"))
            for h in range(HEADS4):
                mine = slice(h * HPAD, h * HPAD + HD)
                act.activation(pos_bd[mine, h, :], bank[7][mine, 0:2 * SEQ], ACT.Copy)\
                    .then_inc(sem("pos_bd_ready"), 1)
            for n, c in enumerate((1, 0)):
                evac(qk4[:, c, :], bank[3 + c][:, :], "qk2_mm", n + 1, "qk2_ready")
            act.wait_ge(sem("keys_zeroed"), 2)
            for h in range(HEADS4):
                mine = slice(h * HPAD, (h + 1) * HPAD)
                evac(key_pads[mine, h, :], bank[5][mine, :], "qk2_mm", 3, "qk2_ready")
            evac(v4[:, :, :], tiles(6, P), "qk2_mm", 4, "v2_ready")

            def attention4(name, next_func):
                evac(cexp[:, 0:16, :], comp[:, 0:16, :], f"{name}_shifted", 1, f"{name}_exp", ACT.Exp, scale=0.25)
                table_for(next_func)
                for q in range(Q):
                    if q >= 2:
                        act.wait_ge(sem(f"{name}_av"), q - 1)
                    evac(att_t[:, q % 2, :], bank[4 + q % 2][:, :], f"{name}_tr", q + 1, f"{name}_att_t")
                evac(out_t[:, 0, :], bank[6][:, :], f"{name}_av", 4, f"{name}_out")

            attention4("a2", ACT.Gelu)

            evac(w1s_t[0:D, 0:NODES], bank[3][0:D, 0:NODES], "w1s_tr", 1, "w1s_ready")
            evac(w2e_t[:, 0, :], bank[5][:, :], "w2e_tr", 1, "w2e_t_ready")
            for odd in range(2):
                experts = lambda ap: ap.rearrange("p (k e c) -> p k e c", e=2, c=D)[:, :, odd, :]
                evac(experts(w2e_t[odd * D:odd * D + TAIL, 1, :]), experts(bank[6][0:TAIL, :]), "w2e_tr", 2,
                     "w2e_t_ready")
            evac(xt[6][0:D, :], bank[2][0:D, :], "x6_tr", 1, "x6t_ready")
            for c in range(2):
                evac(pathw[:, 2 * c:2 * c + 2, 0:NODES],
                     bank[c][:, :].rearrange("p (q n) -> p q n", q=2)[:, :, 0:NODES], "tree_choice", c + 1,
                     "tree_abs", ACT.Abs)
            for c in range(2):
                evac(pathw[:, 2 * c:2 * c + 2, 0:NODES], pathw[:, 2 * c:2 * c + 2, 0:NODES], "tree_abs", c + 1,
                     "tree_gelu", ACT.Gelu)
            table_for(ACT.Exp)
            def copy_z_round(i, s):
                k = i * 2 + s
                if not first_round(i):
                    act.wait_ge(sem("tree_main"), k - 1)
                evac(z_t[:, s, :], bank[s][:, :], "z_tr", k + 1, "z_t_ready")

            for c, n in ((0, P), (1, NODES - P)):
                evac(pathw_t[0:n, c, :], bank[2 + c][0:n, :], "pathw_tr", c + 1, "pathw_t")
            over_pairs(act, copy_z_round, CHUNKS // 2)
            act.wait_ge(sem("tree_main"), CHUNKS - 2)
            evac(z_t[:, 0, :], bank[0][:, :], "z_tr", CHUNKS, "z_t_ready")

            for n in range(6):
                j, g = n // 3, n % 3
                cols = min(512, NE * HID3 - 512 * g)
                evac(w13_t[:, j, g * 512:g * 512 + cols], bank[n % 2][0:D, 0:cols], "w13_tr", n + 1, "w13_t_ready")

            act.wait_ge(*nth("ft_zeroed"))
            evac(ft[0:D, :], bank[2][0:D, :], "f7_tr", 1, "f7t_ready")
            for q in range(Q):
                evac(esim[:, q, :], bank[3 + q][:, :], "sim_mm", q + 1, "sim_exp", ACT.Exp)

            evac(v4[:, :, :], tiles(7, P), "qk3_mm", 5, "v3_ready")
            attention4("a3", ACT.Exp)
            evac(small[:, 0, 0:Q * NE].rearrange("p (q e) -> p q e", q=Q),
                 small[:, 1, 0:Q * NE].rearrange("p (q e) -> p q e", q=Q), "r3_shifted", 1, "r3_exp", ACT.Exp)

            def silu3(i, s):
                e = i * 2 + s
                if not first_round(i):
                    act.wait_ge(sem("f3_ht"), e * 2 - 2)
                evac(silu[:, s, 0, :], bank[3 * s][:, :], "f3_up", e * 3 + 1, "f3_silu", ACT.Silu)
                evac(silu[0:TAIL, s, 1, :], bank[3 * s + 2][0:TAIL, :], "f3_up", e * 3 + 3, "f3_silu", ACT.Silu)

            over_experts(act, silu3)

        @block.vector
        def _(dve):
            made = [0]

            def link(ins):
                made[0] += 1
                ins.then_inc(sem("dve_step"), 1)
                dve.wait_ge(sem("dve_step"), made[0])

            def rsqrt(row, name):
                dve.wait_ge(sem("rooted"), ROOTS.index((name, row)) + 1)
                v, y, t = var2[:, row, :], rs[:, row, :], rs_t[:, row, :]
                link(dve.tensor_tensor(t, y, y, ALU.mult))
                link(dve.scalar_tensor_tensor(out=t, in0=t, scalar=-0.5, in1=v, op0=ALU.mult, op1=ALU.mult))
                link(dve.scalar_tensor_tensor(out=y, in0=t, scalar=1.5, in1=y, op0=ALU.add, op1=ALU.mult))

            def moments(src, name, *rows):
                for q in range(Q):
                    last = dve.bn_stats(bst[:, q, :], src[:, q, :])
                link(last)
                for q in range(Q):
                    last = dve.bn_aggr(mv[:, q, :], bst[:, q, :])
                link(last)
                for i, (a, b) in enumerate(rows):
                    last = dve.tensor_scalar(var2[:, i, :], mv[:, :, 1], a, b, ALU.mult, ALU.add)
                last.then_inc(sem(f"{name}_var"), 1)

            def centred(src, dst, row, done):
                for q in range(Q):
                    dve.tensor_scalar(dst[:, q, :], src[:, q, :], mv[:, q, 0:1], rs[:, row, q:q + 1],
                                      ALU.subtract, ALU.mult).then_inc(sem(done), 1)
                dve.wait_ge(*tile_of(done))

            EPS = 1e-5

            def layernorm(src, dst, name):
                moments(src, name, (1.0, EPS))
                rsqrt(0, name)
                centred(src, dst, 0, f"{name}_ready")

            def mean_square(src, name, scale, shift, least):
                link(dve.tensor_tensor(sq[:, :, :], src, src, ALU.mult))
                link(dve.reduce_sum(st[:, 2, :], sq[:, :, :], axis=X))
                if shift:
                    last = dve.tensor_scalar(var2[:, 0, :], st[:, 2, :], scale, shift, ALU.mult, ALU.add)
                else:
                    last = dve.tensor_scalar(var2[:, 0, :], st[:, 2, :], least, None, ALU.max)
                last.then_inc(sem(f"{name}_var"), 1)

            def scaled_by_rms(src, dst, scale, shift, least, name, done):
                mean_square(src, name, scale, shift, least)
                rsqrt(0, name)
                dve.tensor_tensor(dst, src, bc(rs[:, 0, :], 2, D), ALU.mult).then_inc(sem(done), Q)
                dve.wait_ge(*tile_of(done))

            for i in range(3):
                link(dve.memset(xt[i][D:P, :], 0.0))
                dve.memset(xt[i][D:D + 1, :], 1.0).then_inc(sem("bias_ones"), 1)
            for q in (1, 3):
                dve.wait_ge(sem(f"img_in{q}"), W[f"img_in{q}"])
                dve.tensor_copy(imgs[PATCH_H:P, q * GRP:(q + 1) * GRP, 0:IMG_W:2],
                                imgs[0:PATCH_H, q * GRP:(q + 1) * GRP, 1:IMG_W:2]).then_inc(sem("img_shifted_dve"), 1)
            dve.wait_ge(*nth("ident_ready"))
            dve.wait_ge(*nth("same_lt_ready"))
            by_pos = lambda m: m[:, :].rearrange("p (g j) -> p j g", g=GRP)
            link(dve.reduce_sum(pos1h[:, :], by_pos(ident), axis=X))
            link(dve.reduce_sum(before[:, :], by_pos(same_lt), axis=X))
            link(dve.tensor_scalar(not_first[:, :], pos1h[:, 0:1], -1.0, 1.0, ALU.mult, ALU.add))
            link(dve.tensor_scalar(strict_bias[:, :], pos1h[:, :], pos1h[:, 0:1], None, ALU.mult))
            link(dve.tensor_tensor(strict_bias[:, :], strict_bias[:, :], before[:, :], ALU.add))
            link(dve.tensor_scalar(strict_bias[:, :], strict_bias[:, :], BIG, -BIG, ALU.mult, ALU.add))
            link(dve.tensor_tensor(causal_bias[:, :], pos1h[:, :], before[:, :], ALU.add))
            link(dve.tensor_scalar(causal_bias[:, :], causal_bias[:, :], BIG, -BIG, ALU.mult, ALU.add))

            by_image = lambda ap: ap.rearrange("p (g j) -> p g j", g=GRP)
            for q in range(Q):
                dve.wait_ge(sem("tok_half_ready"), q + 1)
                dve.tensor_tensor(by_image(qt0[:, q * P:(q + 1) * P]),
                                  by_image(bank[q][0:D, 0:GRP * (SEQ + 1)])[:, :, 0:SEQ],
                                  by_image(tok_half[:, q * P:(q + 1) * P]), ALU.add)\
                   .then_inc(sem("tok_sum"), 1)

            dve.wait_ge(sem("h0_ready"), 1)
            layernorm(hs[0], xs[0], "x1")
            dve.wait_ge(sem("sig_ready"), 1)
            dve.tensor_tensor(att0[:, :, :], att0[:, :, :], bc(same_tok[:, :], 1, Q), ALU.mult)\
                .then_inc(sem("att0_ready"), 1)
            dve.wait_ge(sem("a0_mm"), 1)
            link(dve.tensor_tensor(hs[1][:, :, :], hs[0][:, :, :], tiles(5), ALU.add))
            layernorm(hs[1], xs[1], "x2")

            sv = lambda i, n=SEQ: small[:, i, 0:Q * n].rearrange("p (q j) -> p q j", q=Q)
            dve.wait_ge(sem("wr_mm"), 1)
            link(dve.tensor_copy(st[:, 0, :], bank[5][:, 0:Q]))
            dve.tensor_tensor(sv(0), bc(pos1h[:, :], 1, Q), bc(st[:, 0, :], 2, SEQ), ALU.mult)\
                .then_inc(sem("wr_spread"), 1)
            dve.wait_ge(sem("wr_gather_mm"), 1)
            link(dve.tensor_copy(sv(1), bank[6][:, 0:Q * SEQ].rearrange("p (q j) -> p q j", q=Q)))
            link(dve.tensor_tensor(sv(2), sv(1), bc(pos1h[:, :], 1, Q), ALU.mult))
            link(dve.reduce_sum(st[:, 1, :], sv(2), axis=X))
            link(dve.tensor_tensor(sv(3), sv(1), bc(st[:, 1, :], 2, SEQ), ALU.is_gt))
            link(dve.tensor_tensor(sv(4), sv(1), bc(st[:, 1, :], 2, SEQ), ALU.is_equal))
            link(dve.tensor_tensor(sv(4), sv(4), bc(before[:, :], 1, Q), ALU.mult))
            link(dve.tensor_tensor(sv(3), sv(3), sv(4), ALU.add))
            link(dve.reduce_sum(st[:, 2, :], sv(3), axis=X))
            kept = max(1, SEQ // 2) - 1
            link(dve.scalar_tensor_tensor(out=st[:, 4, :], in0=st[:, 2, :], scalar=kept - 0.5, in1=st[:, 1, :],
                                          op0=ALU.is_lt, op1=ALU.mult))
            link(dve.tensor_tensor(hs[2][:, :, :], hs[1][:, :, :], xs[1][:, :, :], ALU.add))
            dve.wait_ge(sem("f0_down"), 1)
            link(dve.tensor_tensor(xc[:, :, :], tiles(7), bc(st[:, 4, :], 2, D), ALU.mult))
            link(dve.tensor_tensor(hs[2][:, :, :], hs[2][:, :, :], xc[:, :, :], ALU.add))
            layernorm(hs[2], xs[2], "x3")
            dve.wait_ge(sem("f1_shift_mm"), 1)
            dve.tensor_tensor(f1_bias[:, :], bank[1][:, 0:2 * NE], cols128[:, 2:2 + 2 * NE], ALU.add)\
                .then_inc(sem("f1_bias_ready"), 1)

            def compact(n, b, name):
                dve.wait_ge(sem(f"{name}_mm"), n + 1)
                dve.reduce_max(comp[:, 4 * n:4 * n + 4, :],
                               bank[b][:, :].rearrange("p (k g j) -> p k j g", k=4, g=GRP), axis=X)\
                    .then_inc(sem(f"{name}_comp"), 1)

            def shift(blocks, name, bias, extra=None):
                nb = blocks.stop - blocks.start
                c, mx = comp[:, blocks, :], small[:, 2, blocks]
                if extra is not None:
                    link(dve.tensor_tensor(c, c, extra, ALU.add))
                if bias is not None:
                    link(dve.tensor_tensor(c, c, bc(bias, 1, nb), ALU.add))
                link(dve.reduce_max(mx, c, axis=X))
                dve.tensor_tensor(c, c, bc(mx, 2, SEQ), ALU.subtract).then_inc(sem(f"{name}_shifted"), 1)

            def normalize(blocks, name, value, zero_first=False):
                c, e = comp[:, blocks, :], cexp[:, blocks, :]
                mx, sm = small[:, 2, blocks], small[:, 3, blocks]
                dve.wait_ge(sem(f"{name}_exp"), value)
                link(dve.reduce_sum(sm, e, axis=X))
                link(dve.reciprocal(mx, sm))
                if zero_first:
                    link(dve.tensor_scalar(mx, mx, not_first[:, :], None, ALU.mult))
                link(dve.tensor_tensor(c, e, bc(mx, 2, SEQ), ALU.mult))

            def spread(n, name):
                if n >= 2:
                    dve.wait_ge(sem(f"{name}_tr"), n - 1)
                dve.tensor_tensor(wide[:, n % 2, :].rearrange("p (k g j) -> p k g j", k=4, g=GRP),
                                  bc(comp[:, 4 * n:4 * n + 4, :], 2, GRP),
                                  bc(bc(same[:, :], 2, SEQ), 1, 4), ALU.mult).then_inc(sem(f"{name}_wide"), 1)

            dve.wait_ge(sem("heads_in"), W["heads_in"])
            for i in range(2):
                row = wt[D:D + 1, i, :].rearrange("o (h d) -> o h d", h=HEADS4)[:, :, 0:HD]
                dve.tensor_tensor(row, row, uv_rows[D:D + 1, 0, :].rearrange("o (h d) -> o h d", h=HEADS4), ALU.add)\
                    .then_inc(sem("heads_bias"), 1)

            dve.wait_ge(sem("keys_zeroed"), 1)
            for c in range(4):
                dve.wait_ge(sem("k1_mm"), c + 1)
                dve.tensor_copy(key_pads[0:D, 2 * c, :], bank[2 + c % 2][0:D, :]).then_inc(sem("k1_even"), 1)
                if c == 3:
                    dve.wait_ge(sem("s1_comp"), 4)
                    shift(slice(0, 16), "a1", strict_bias[:, :])
                if c:
                    for h in (2 * c - 2, 2 * c - 1):
                        compact(h, 4 + h % 4, "s1")
            normalize(slice(0, 16), "a1", 1, zero_first=True)
            compact(6, 6, "s1")
            compact(7, 7, "s1")
            dve.wait_ge(sem("s1_comp"), 8)
            shift(slice(16, 32), "a1", strict_bias[:, :])
            for n in range(2):
                spread(n, "a1")
            normalize(slice(16, 32), "a1", 2, zero_first=True)
            for n in range(2, 8):
                spread(n, "a1")

            def scale_weights(i, s):
                e = i * 2 + s
                if not first_round(i):
                    dve.wait_ge(sem("f1_up"), e * 2 - 2)
                dve.tensor_scalar(f1_slot[0:D, s, :], f1_w1[:, ds(e, 1), :].squeeze(1), cols64[:, ds(e, 1)], None,
                                  ALU.mult)\
                    .then_inc(sem("f1_slot_in"), 1)

            dve.wait_ge(sem("cols_ready"), 2)
            scale_weights(0, 0)
            scale_weights(0, 1)
            dve.wait_ge(sem("a1_down"), 1)
            link(dve.tensor_tensor(hs[3][:, :, :], hs[2][:, :, :], tiles(4), ALU.add))

            def route(name, b):
                dve.wait_ge(sem(f"{name}_mm"), 1)
                logits = bank[b][:, 0:Q * NE].rearrange("p (q e) -> p q e", q=Q)
                link(dve.reduce_max(small[:, 2, 0:Q], logits, axis=X))
                dve.tensor_tensor(sv(1), logits, bc(small[:, 2, 0:Q], 2, NE), ALU.subtract)\
                    .then_inc(sem(f"{name}_shifted"), 1)

            def two_gates(name, g, eps):
                probs = small[:, 4, 0:Q * NE].rearrange("p (q e) -> p q e", q=Q)
                mx, sm = small[:, 2, 0:Q], small[:, 3, 0:Q]
                dve.wait_ge(sem(f"{name}_exp"), 1)
                link(dve.reduce_sum(sm, sv(0), axis=X))
                link(dve.reciprocal(mx, sm))
                link(dve.tensor_tensor(probs, sv(0), bc(mx, 2, NE), ALU.mult))
                cmp = [ranks[:, i, :].rearrange("p (q e f) -> p q e f", q=Q, e=NE) for i in range(2)]
                other, own = bc(probs, 2, NE), bc(probs, 3, NE)
                link(dve.tensor_tensor(cmp[0], other, own, ALU.is_gt))
                link(dve.tensor_tensor(cmp[1], other, own, ALU.is_equal))
                link(dve.tensor_tensor(cmp[1], cmp[1], bc(lower8[:, :, :], 1, Q), ALU.mult))
                link(dve.tensor_tensor(cmp[0], cmp[0], cmp[1], ALU.add))
                link(dve.reduce_sum(sv(5), cmp[0], axis=X))
                link(dve.scalar_tensor_tensor(out=sv(6), in0=sv(5), scalar=1.5, in1=probs,
                                              op0=ALU.is_lt, op1=ALU.mult))
                link(dve.reduce_sum(sm, sv(6), axis=X))
                if eps:
                    link(dve.tensor_scalar(sm, sm, eps, None, ALU.add))
                link(dve.reciprocal(mx, sm))
                dve.tensor_tensor(g, sv(6), bc(mx, 2, NE), ALU.mult).then_inc(sem(f"{name}_gates"), 1)

            moments(hs[3], "x4", (1.0, EPS), (1.0 + EPS, EPS * EPS))
            rsqrt(1, "x4")
            centred(hs[3], inner, 1, "x4n_ready")
            rsqrt(0, "x4")
            centred(hs[3], xs[3], 0, "x4_ready")
            dve.wait_ge(*nth("lower8_ready"))
            route("r1", 3)
            two_gates("r1", gates[:, 0, :, :], 0.0)
            dve.wait_ge(sem("r1_gates"), 1)
            dve.tensor_copy(yacc[:, :, :], hs[3][:, :, :]).then_inc(sem("f1_acc"), 1)

            def combine(e, s, g, b, name):
                dve.wait_ge(sem(f"{name}_down"), e + 1)
                dve.tensor_tensor(ytmp[:, s, :, :], tiles(b), gates[:, g, :, ds(e, 1)].broadcast_to((P, Q, D)),
                                  ALU.mult).then_inc(sem(f"{name}_gated"), 1)
                dve.wait_ge(sem(f"{name}_gated"), e + 1)
                dve.wait_ge(sem(f"{name}_acc"), e + 1)
                dve.tensor_tensor(yacc[:, :, :], yacc[:, :, :], ytmp[:, s, :, :], ALU.add)\
                    .then_inc(sem(f"{name}_acc"), 1)

            with dve.Fori(1, NE // 2) as i:
                for s in range(2):
                    scale_weights(i, s)
                    combine(i * 2 + (s - 2), s, 0, 1 + s, "f1")
            combine(NE - 2, 0, 0, 1, "f1")
            combine(NE - 1, 1, 0, 2, "f1")
            dve.wait_ge(sem("f1_acc"), NE + 1)
            dve.wait_ge(sem("b1_mm"), 1)
            link(dve.tensor_tensor(hs[4][:, :, :], yacc[:, :, :], tiles(0), ALU.add))

            moments(hs[4], "x5", (1.0 + EPS, EPS * EPS))
            rsqrt(0, "x5")
            centred(hs[4], inner, 0, "x5n_ready")
            dve.wait_ge(*nth("x5n_tr"))
            dve.tensor_scalar(xt[5][0:D, :], bank[2][0:D, :], cols64[:, 2 * NE:2 * NE + 1],
                              cols64[:, 2 * NE + 1:2 * NE + 2], ALU.mult, ALU.add).then_inc(sem("x5nt_ready"), 1)
            dve.wait_ge(sem("p2_mm"), 1)
            pview = bank[0][:, 0:Q * HEADS4 * 2 * SEQ].rearrange("p (b r) -> p b r", r=2 * SEQ)
            for i in range(SEQ):
                off = SEQ - 1 - i
                if i == 0:
                    link(dve.tensor_scalar(posadd[:, :, :], pview[:, :, off:off + SEQ], pos1h[:, 0:1], None, ALU.mult))
                else:
                    link(dve.scalar_tensor_tensor(out=posadd[:, :, :], in0=pview[:, :, off:off + SEQ],
                                                  scalar=pos1h[:, i:i + 1], in1=posadd[:, :, :],
                                                  op0=ALU.mult, op1=ALU.add))

            def attention4(name, bias, extra):
                for q in range(Q):
                    compact(q, 1 + q, f"{name}_s")
                dve.wait_ge(sem(f"{name}_s_comp"), 4)
                shift(slice(0, 16), name, bias, extra)
                normalize(slice(0, 16), name, 1)
                for q in range(Q):
                    spread(q, name)

            attention4("a2", None, posadd[:, :, :])
            dve.wait_ge(sem("a2_down"), 1)
            link(dve.tensor_tensor(hs[5][:, :, :], hs[4][:, :, :], tiles(7), ALU.add))

            layernorm(hs[5], xs[5], "x6")
            dve.memset(onehot[:, :, 0:1], 1.0)
            dve.wait_ge(sem("tree_mm"), 1)
            lg = [bank[b][:, :].rearrange("p (q n) -> p q n", q=2) for b in (0, 1)]
            turns = right[:, :, 0:2 * PARENTS].rearrange("p q (m s) -> p q m s", s=2)
            for c in range(2):
                for side, op in enumerate((ALU.is_le, ALU.is_gt)):
                    last = dve.tensor_scalar(turns[:, 2 * c:2 * c + 2, :, side], lg[c][:, :, 0:PARENTS], 0.0, None, op)
                last.then_inc(sem("tree_choice"), 1)
            dve.wait_ge(sem("tree_choice"), 2)
            link(dve.tensor_copy(onehot[:, :, 1:3], turns[:, :, 0, :]))
            for lv in range(1, 7):
                n0, n1 = 2 ** lv - 1, 2 ** (lv + 1) - 1
                kids = onehot[:, :, 2 * n0 + 1:2 * n1 + 1].rearrange("p q (m s) -> p q m s", s=2)
                link(dve.tensor_tensor(kids, bc(onehot[:, :, n0:n1], 3, 2), turns[:, :, n0:n1, :], ALU.mult))
            dve.wait_ge(sem("tree_gelu"), 2)
            for nodes in (slice(PARENTS, NODES), slice(0, PARENTS)):
                dve.tensor_tensor(pathw[:, :, nodes], pathw[:, :, nodes], onehot[:, :, nodes], ALU.mult)\
                    .then_inc(sem("pathw_ready"), 1)
            def node_weights(lv):
                n0, low = 2 ** lv - 1, 2 ** (lv - 4)
                return dve.reduce_sum(upath[:, :, FIRST_CHUNK[lv]:FIRST_CHUNK[lv] + low, :]
                                      .rearrange("p q c s -> p q (c s)"),
                                      pathw[:, :, n0:2 * n0 + 1].rearrange("p q (t l) -> p q l t", t=8), axis=X)

            dve.wait_ge(sem("pathw_ready"), 2)
            dve.reduce_sum(upath[:, :, 0, 0], pathw[:, :, 1:3], axis=X)
            link(dve.tensor_copy(upath[:, :, 0, 1], pathw[:, :, 0]))

            def spread_token(i, s):
                k = i * 2 + s
                if not first_round(i):
                    dve.wait_ge(sem("z_tr"), k - 1)
                dve.tensor_tensor(zbuf[:, s, :, :, :], bc(xs[5][:, :, :], 2, 2),
                                  bc(upath[:, :, ds(k, 1), :].rearrange("p q k s -> p q (k s)"), 3, D), ALU.mult)\
                    .then_inc(sem("z_ready"), 1)

            spread_token(0, 0)
            link(node_weights(7))
            spread_token(0, 1)
            for lv in (6, 5, 4):
                node_weights(lv)
            for lv in (3, 2):
                last = dve.reduce_sum(upath[:, :, CHUNKS - 1, 3 - lv], pathw[:, :, 2 ** lv - 1:2 ** (lv + 1) - 1],
                                      axis=X)
            link(last)
            with dve.Fori(1, CHUNKS // 2) as i:
                spread_token(i, 0)
                spread_token(i, 1)
            spread_token(CHUNKS // 2, 0)
            dve.wait_ge(sem("tree_main"), 1)
            for q in range(Q):
                last = dve.tensor_scalar(yacc[:, q, :], bank[2][:, q * P:q * P + D], onehot[:, q, 1:2], None, ALU.mult)
            link(last)
            for q in range(Q):
                last = dve.scalar_tensor_tensor(out=yacc[:, q, :], in0=bank[2][:, q * P + D:(q + 1) * P],
                                                scalar=onehot[:, q, 2:3], in1=yacc[:, q, :], op0=ALU.mult,
                                                op1=ALU.add)
            link(last)
            link(dve.tensor_tensor(yacc[:, :, :], yacc[:, :, :], hs[5][:, :, :], ALU.add))
            for q in range(Q):
                dve.wait_ge(sem("tree_done"), q + 1)
                dve.tensor_tensor(picked[:, q, :].rearrange("p (t o) -> p t o", t=8),
                                  bank[4 + q][:, :].rearrange("p (t o) -> p t o", t=8),
                                  bc(onehot[:, q, 7:15], 2, D), ALU.mult).then_inc(sem("tree_picked"), 1)
            dve.wait_ge(sem("tree_picked"), Q)
            link(dve.reduce_sum(inner[:, 2:Q, :], picked[:, 2:Q, :].rearrange("p q (t o) -> p q o t", t=8), axis=X))
            dve.wait_ge(sem("tree_summed"), 2)
            link(dve.tensor_tensor(hs[6][:, :, :], yacc[:, :, :], inner[:, :, :], ALU.add))
            dve.wait_ge(sem("tree_b2"), 1)
            link(dve.tensor_tensor(hs[6][:, :, :], hs[6][:, :, :], tiles(3), ALU.add))

            for q in range(Q):
                last = dve.bn_stats(bst[:, q, :], hs[6][:, q, :])
            link(last)
            for q in range(Q):
                last = dve.bn_aggr(mv[:, q, :], bst[:, q, :])
            link(last)
            link(dve.tensor_scalar(st[:, 0, :], mv[:, :, 1], 1e-24, 1e-24 * EPS, ALU.mult, ALU.add))
            dve.scalar_tensor_tensor(out=var2[:, 0, :], in0=mv[:, :, 1], scalar=float(D), in1=st[:, 0, :],
                                     op0=ALU.mult, op1=ALU.max).then_inc(sem("f7_var"), 1)
            dve.wait_ge(sem("fn_ones"), 1)
            rsqrt(0, "f7")
            centred(hs[6], fn[:, :, 0:D], 0, "f7_ready")
            link(dve.tensor_scalar(inner[:, :, :], fn[:, :, 0:D], 0.8, None, ALU.mult))
            for q in range(Q):
                dve.wait_ge(sem("sim_av"), q + 1)
                sim = bank[SIM_BANKS[q]]
                link(dve.reciprocal(st[:, 0, q:q + 1], sim[:, D:D + 1]))
                last = dve.scalar_tensor_tensor(out=inner[:, q, :], in0=sim[:, 0:D], scalar=st[:, 0, q:q + 1],
                                                in1=inner[:, q, :], op0=ALU.mult, op1=ALU.add)
            link(last)
            scaled_by_rms(inner[:, :, :], xc[:, :, :], 1.0, 0.0, 1e-24, "c7", "c7_ready")
            link(dve.tensor_tensor(hs[7][:, :, :], hs[6][:, :, :], xc[:, :, :], ALU.add))

            RMS_EPS = 1e-6
            moments(hs[7], "x8", (1.0, EPS), (1.0 + RMS_EPS, RMS_EPS * EPS))
            rsqrt(1, "x8")
            centred(hs[7], inner, 1, "x8n_ready")
            rsqrt(0, "x8")
            dve.wait_ge(*nth("x8n_tr"))
            dve.tensor_scalar(xt[8][0:D, :], bank[2][0:D, :], cols64[:, 2 * NE + 2:2 * NE + 3], None, ALU.mult)\
                .then_inc(sem("x8nt_ready"), 1)
            centred(hs[7], xs[7], 0, "x8_ready")
            dve.memset(ht[HPAD:D, 0, 1, :], 0.0)
            by8 = lambda ap: ap.rearrange("p (g j) -> p g j", j=SEQ)
            for i in range(2):
                dve.wait_ge(sem("qk3_mm"), 2 * i + 2)
                if i:
                    dve.wait_ge(sem("q3_ready"), 1)
                for turned in range(2):
                    link(dve.tensor_tensor(by8(qk4[:, 2 + turned, :]), by8(bank[3 + 2 * i + turned][:, :]),
                                           bc(rope[:, turned, :], 1, N_IMG), ALU.mult))
                if i == 0:
                    dve.tensor_tensor(qk4[:, 0, :], qk4[:, 2, :], qk4[:, 3, :], ALU.add).then_inc(sem("q3_ready"), 1)
            dve.wait_ge(sem("keys_zeroed"), 3)
            for h in range(HEADS4):
                mine = slice(h * HPAD, (h + 1) * HPAD)
                dve.tensor_tensor(key_pads[mine, h, :], qk4[mine, 2, :], qk4[mine, 3, :], ALU.add)\
                    .then_inc(sem("k3_ready"), 1)
            attention4("a3", causal_bias[:, :], None)
            dve.wait_ge(sem("a3_down"), 1)
            link(dve.tensor_tensor(yacc[:, :, :], xs[7][:, :, :], tiles(7), ALU.add))
            scaled_by_rms(yacc[:, :, :], inner[:, :, :], 1.0 / D, 1e-6, 0.0, "x9", "x9n_ready")
            dve.tensor_tensor(yacc[:, :, :], yacc[:, :, :], hs[7][:, :, :], ALU.add).then_inc(sem("f3_acc"), 1)
            dve.wait_ge(*nth("x9n_tr"))
            dve.tensor_scalar(xt[9][0:D, :], bank[2][0:D, :], cols64[:, 2 * NE + 3:2 * NE + 4], None, ALU.mult)\
                .then_inc(sem("x9nt_ready"), 1)

            def hidden3(i, s):
                e = i * 2 + s
                if not first_round(i):
                    dve.wait_ge(sem("f3_down"), i)
                dve.wait_ge(sem("f3_up"), e * 3 + 2)
                dve.wait_ge(sem("f3_silu"), e * 2 + 1)
                dve.tensor_tensor(ht[:, s, 0, :], silu[:, s, 0, :], bank[3 * s + 1][:, :], ALU.mult)\
                    .then_inc(sem("f3_ht"), 1)
                dve.wait_ge(sem("f3_silu"), e * 2 + 2)
                dve.tensor_tensor(ht[s * D:s * D + TAIL, 0, 1, :], silu[0:TAIL, s, 1, :],
                                  bank[3 * s + 2][D:D + TAIL, :], ALU.mult).then_inc(sem("f3_ht"), 1)

            def combine3(i):
                pair = ytmp[:, :, :, :].rearrange("p s q d -> p (s q d)").rearrange("p (q s d) -> p q s d", q=Q, s=2)
                dve.wait_ge(sem("f3_down"), i + 1)
                dve.tensor_tensor(pair, bank[6][:, :].rearrange("p (q s d) -> p q s d", q=Q, s=2),
                                  bc(gates[:, 1, :, ds(i * 2, 2)], 3, D), ALU.mult).then_inc(sem("f3_gated"), 1)
                dve.wait_ge(sem("f3_gated"), i + 1)
                dve.wait_ge(sem("f3_acc"), i + 1)
                dve.tensor_tensor(yacc[:, :, :], yacc[:, :, :], pair[:, :, 0, :], ALU.add)\
                    .then_inc(sem("f3_half"), 1)
                dve.wait_ge(sem("f3_half"), i + 1)
                dve.tensor_tensor(yacc[:, :, :], yacc[:, :, :], pair[:, :, 1, :], ALU.add)\
                    .then_inc(sem("f3_acc"), 1)

            route("r3", 7)
            hidden3(0, 0)
            hidden3(0, 1)
            two_gates("r3", gates[:, 1, :, :], 1e-9)
            dve.wait_ge(sem("r3_gates"), 1)
            with dve.Fori(1, NE // 2) as i:
                hidden3(i, 0)
                combine3(i - 1)
                hidden3(i, 1)
            combine3(NE // 2 - 1)

        @block.tensor
        def _(pe):
            def loaded(name):
                pe.wait_ge(sem(name), W[name])

            def to_features(src, b, wait, done):
                for q in range(Q):
                    pe.wait_ge(*tile_of(wait, q))
                    last = pe.transpose(bank[b][0:D, q * P:(q + 1) * P], src[:, q, :], ident[:, :])
                last.then_inc(sem(done), 1)

            def stay_busy(b, n):
                for _ in range(n):
                    pe.matmul(bank[b][:, :], ident_b[:, :], bc(other_b[:, :], 1, 4), start=True, stop=True)

            def every_token(b, bias):
                pe.matmul(tiles(b), ones_row[0:1, :], bc(bias[:, :], 1, Q), start=True, stop=False)

            tok = lambda q: slice(q * P, (q + 1) * P)

            def shifts(experts):
                for e in experts:
                    for c in range(2):
                        last = pe.matmul(bank[1][:, 2 * e + c:2 * e + c + 1], f1_w1[:, e, c * P:(c + 1) * P],
                                         cols64[:, NE + e:NE + e + 1], start=True, stop=True)
                return last

            loaded("tok_w_in")
            pe.wait_ge(*nth("ones_ready"))
            pe.wait_ge(sem("bias_ones"), 3)
            for q in range(Q):
                loaded(f"img_in{q}")
                pe.wait_ge(sem("img_shifted_dve" if q % 2 else "img_shifted_act"), q // 2 + 1)
                mine = slice(q * GRP, (q + 1) * GRP)
                steps = bank[q][:, 0:GRP * (SEQ + 1)].rearrange("p (g m) -> p g m", g=GRP)
                for c in range(0, PATCH_STEP, 2):
                    if c == 2:
                        last_col = slice(PATCH_W - 1, PATCH_W + PATCH_STEP * (SEQ - 1), PATCH_STEP)
                        pe.matmul(steps[0:D, :, 0:SEQ], tok_w_last[0:PATCH_H, 0, :], imgs[0:PATCH_H, mine, last_col],
                                  start=False, stop=False, skip_group_check=True)
                        pe.matmul(steps[0:D, :, 0:SEQ], tok_b[:, :], ones_row[0:1, :], start=False, stop=False,
                                  skip_group_check=True)
                    last = pe.matmul(steps, tok_w[:, c // 2, :], imgs[:, mine, c:c + PATCH_STEP * SEQ + 1:PATCH_STEP],
                                     start=(c == 0), stop=(c == PATCH_STEP - 2), skip_group_check=True)
                last.then_inc(sem("tok_mm"), 1)
            pe.wait_ge(*nth("ident_ready"))
            loaded("rows_in")
            pe.transpose(bank[7][:, 0:2 + 2 * NE], rows128[:, :], ident[0:2 + 2 * NE, 0:2 + 2 * NE])
            pe.transpose(bank[7][0:D, 64:64 + 2 * NE + 4], rows64[:, :], ident[0:2 * NE + 4, 0:2 * NE + 4])\
                .then_inc(sem("rows_mm"), 1)
            for q in range(Q):
                pe.wait_ge(sem("h0t_ready"), q + 1)
                pe.transpose(tiles(5)[:, q, :], qt0[:, tok(q)], ident[0:D, 0:D]).then_inc(sem("h0_tr"), 1)

            pe.wait_ge(sem("masks_b"), 2)
            stay_busy(0, 19)
            to_features(xs[0], 2, "x1_ready", "x1_tr")
            loaded("l0_in")
            pe.wait_ge(*nth("x1t_ready"))
            pe.matmul(bank[3][0:D, :], a0_w[:, :], xt[0][:, :], start=True, stop=True).then_inc(sem("q0_mm"), 1)
            pe.wait_ge(sem("qt0_ready"), 1)
            for q in range(Q):
                last = pe.matmul(bank[4][:, tok(q)], xt[0][0:D, tok(q)], qt0[:, tok(q)], start=True, stop=True)
            last.then_inc(sem("s0_mm"), 1)
            pe.wait_ge(sem("att0_ready"), 1)
            for q in range(Q):
                last = pe.matmul(tiles(5)[:, q, :], att0[:, q, :], xs[0][:, q, :], start=True, stop=True)
            last.then_inc(sem("a0_mm"), 1)

            loaded("heads_in")
            for i, r in enumerate((D, D, D, D, D, D // 2, D // 2, NE)):
                pe.transpose(bank[6][0:D, i * D:i * D + r], wnat[0:r, i, :], ident[0:r, 0:r])
            for i in range(2):
                last = pe.transpose(bank[7][:, i * D:(i + 1) * D], wo_pad[:, i, :], ident[0:D, 0:D])
            last.then_inc(sem("heads_tr"), 1)

            loaded("l1_in")
            pe.wait_ge(sem("cols_ready"), 2)
            shifts(range(0, NE // 2))
            stay_busy(0, 4)
            to_features(xs[1], 2, "x2_ready", "x2_tr")
            pe.wait_ge(*nth("x2t_ready"))
            for q in range(Q):
                last = pe.matmul(bank[5][:, q:q + 1], xt[1][:, tok(q)], f0_wr[:, 0:1], start=True, stop=True)
            last.then_inc(sem("wr_mm"), 1)
            for c in range(2):
                pe.matmul(bank[3 + c][:, :], f0_w1[:, c * P:(c + 1) * P], xt[1][:, :], start=True, stop=True)\
                    .then_inc(sem("f0_mm"), 1)
            pe.wait_ge(sem("heads_w"), 18)
            pe.wait_ge(sem("wr_spread"), 1)
            pe.matmul(bank[6][:, 0:Q * SEQ], same_tok[:, :], small[:, 0, 0:Q * SEQ], start=True, stop=True)\
                .then_inc(sem("wr_gather_mm"), 1)
            every_token(7, f0_b2)
            for c in range(2):
                pe.wait_ge(sem("f0_ready"), c + 1)
                for q in range(Q):
                    last = pe.matmul(tiles(7)[:, q, :], ht[:, 0, c, tok(q)], f0_w2[:, c, :], start=False,
                                     stop=(q == Q - 1 and c == 1))
            last.then_inc(sem("f0_down"), 1)

            shifts(range(NE // 2, NE)).then_inc(sem("f1_shift_mm"), 1)
            stay_busy(0, 13)
            to_features(xs[2], 2, "x3_ready", "x3_tr")
            pe.wait_ge(sem("f1_bias_ready"), 1)
            pe.wait_ge(*nth("x3t_ready"))
            pe.wait_ge(sem("masks_b"), 2)

            def other_images(b):
                pe.matmul(bank[b][:, :], ident_b[:, :], bc(other_b[:, :], 1, 4), start=True, stop=False)

            def project1(c):
                if c >= 2:
                    pe.wait_ge(sem("qt1_ready"), c - 1)
                pe.matmul(bank[c % 2][:, :], a1_w[:, 0, c * P:(c + 1) * P], xt[2][:, :], start=True, stop=True)\
                    .then_inc(sem("q1_mm"), 1)
                if c >= 2:
                    pe.wait_ge(sem("k1_odd"), c - 1)
                    pe.wait_ge(sem("k1_even"), c - 1)
                pe.matmul(bank[2 + c % 2][:, :], a1_w[:, 1, c * P:(c + 1) * P], xt[2][:, :], start=True, stop=True)\
                    .then_inc(sem("k1_mm"), 1)

            def scores1(c):
                pe.wait_ge(sem("qt1_ready"), c + 1)
                pe.wait_ge(sem("k1_odd"), c + 1)
                pe.wait_ge(sem("k1_even"), c + 1)
                for half in range(2):
                    h = 2 * c + half
                    if h >= 4:
                        pe.wait_ge(sem("s1_comp"), h - 3)
                    b = 4 + h % 4
                    other_images(b)
                    for q in range(Q):
                        last = pe.matmul(bank[b][:, tok(q)], qt1[:, c, tok(q)], key_pads[:, h, tok(q)],
                                         start=False, stop=(q == Q - 1))
                    last.then_inc(sem("s1_mm"), 1)

            def values1(q):
                pe.matmul(bank[q][:, :], xt[2][:, tok(q)], a1_w[:, 2, :], start=True, stop=True)\
                    .then_inc(sem("v1_mm"), 1)

            project1(0)
            project1(1)
            scores1(0)
            project1(2)
            scores1(1)
            project1(3)
            scores1(2)
            values1(0)
            scores1(3)
            for q in range(1, Q):
                values1(q)
            pe.wait_ge(sem("v1_ready"), 4)
            stay_busy(0, 1)
            for n in range(10):
                if n < 8:
                    pe.wait_ge(sem("a1_wide"), n + 1)
                    if n >= 4:
                        pe.wait_ge(sem("a1_att_t"), n - 3)
                    for k in range(4):
                        last = pe.transpose(bank[4 + n % 4][:, k * P:(k + 1) * P], wide[:, n % 2, k * P:(k + 1) * P],
                                            ident[:, :])
                    last.then_inc(sem("a1_tr"), 1)
                if n >= 2:
                    h = n - 2
                    part = slice((h % 2) * D, (h % 2 + 1) * D)
                    pe.wait_ge(sem("a1_att_t"), h + 1)
                    for q in range(Q):
                        last = pe.matmul(bank[h // 2][part, tok(q)], v1[:, q, h * D:(h + 1) * D],
                                         att_t[:, h % 2, tok(q)], start=True, stop=True)
                    last.then_inc(sem("a1_av"), 1)
            every_token(4, a1_bu)
            for c in range(4):
                pe.wait_ge(sem("a1_out"), c + 1)
                for q in range(Q):
                    last = pe.matmul(tiles(4)[:, q, :], out_t[:, c, tok(q)], a1_wu[:, c, :], start=False,
                                     stop=(q == Q - 1 and c == 3))
            last.then_inc(sem("a1_down"), 1)

            stay_busy(3, 14)
            to_features(inner, 1, "x4n_ready", "x4n_tr")
            to_features(xs[3], 2, "x4_ready", "x4_tr")

            loaded("f1_in")

            def logits(b, x, ready, weights, done):
                pe.wait_ge(*nth(ready))
                for q in range(Q):
                    last = pe.matmul(bank[b][:, q * NE:(q + 1) * NE], x[:, tok(q)], weights[:, :], start=True,
                                     stop=True)
                last.then_inc(sem(done), 1)

            def down1(e, s):
                pe.wait_ge(sem("f1_ht"), e * 2 + 2)
                if not isinstance(e, int) or e >= 2:
                    pe.wait_ge(sem("f1_gated"), e - 1)
                for q in range(Q):
                    for c in range(2):
                        last = pe.matmul(tiles(1 + s)[:, q, :], ht[:, s, c, tok(q)],
                                         f1_w2[:, ds(e, 1), c, :].rearrange("p e d -> p (e d)"),
                                         start=(c == 0), stop=(c == 1))
                last.then_inc(sem("f1_down"), 1)

            def expert1(i, s):
                e = i * 2 + s
                if first_round(i) and s == 0:
                    pe.wait_ge(*nth("x4nt_ready"))
                pe.wait_ge(sem("f1_slot_in"), e + 1)
                if not first_round(i):
                    pe.wait_ge(sem("f1_ht"), e * 2 - 2)
                for c in range(2):
                    pe.matmul(bank[4 + 2 * s + c][:, :], f1_slot[:, s, c * P:(c + 1) * P], xt[4][:, :],
                              start=True, stop=True).then_inc(sem("f1_up"), 1)
                if first_round(i) and s == 0:
                    logits(3, xt[3], "x4t_ready", f1_wr, "r1_mm")
                else:
                    down1(e - 1, 1 - s)

            over_experts(pe, expert1)
            pe.wait_ge(sem("r1_gates"), 1)
            for q in range(Q):
                last = pe.transpose(bank[3][0:NE, tok(q)], gates[:, 0, q, :], ident[:, :])
            last.then_inc(sem("g1_tr"), 1)
            down1(NE - 1, 1)
            pe.wait_ge(sem("g1t_ready"), 1)
            for q in range(Q):
                last = pe.matmul(tiles(0)[:, q, :], gates_t[:, tok(q)], f1_b2[:, :], start=True, stop=True)
            last.then_inc(sem("b1_mm"), 1)

            pe.wait_ge(sem("heads_bias"), 2)
            pe.matmul(bank[7][:, 0:2 * SEQ], wt[:, 4, :], rel[:, :], start=True, stop=True).then_inc(sem("pos_mm"), 1)
            stay_busy(3, 10)
            to_features(inner, 2, "x5n_ready", "x5n_tr")
            pe.wait_ge(*nth("x5nt_ready"))
            for c in (1, 0, 2):
                pe.matmul(bank[3 + c][:, :], wt[:, c, :], xt[5][:, :], start=True, stop=True)\
                    .then_inc(sem("qk2_mm"), 1)
            pe.wait_ge(sem("qk2_ready"), 1)
            pe.wait_ge(sem("pos_bd_ready"), 4)
            for q in range(Q):
                last = pe.matmul(bank[0][:, 0:Q * HEADS4 * 2 * SEQ].rearrange("p (h q r) -> p h q r", h=HEADS4, q=Q)
                                 [:, :, q, :], qk4[:, 1, tok(q)], pos_bd[:, :, :], start=True, stop=True)
            last.then_inc(sem("p2_mm"), 1)
            for q in range(Q):
                last = pe.matmul(bank[6][:, tok(q)], xt[5][:, tok(q)], wt[:, 3, :], start=True, stop=True)
            last.then_inc(sem("qk2_mm"), 1)

            def attention4(name, out_w, bias, keys, first_key, values):
                for h in range(HEADS4):
                    pe.wait_ge(sem(keys), first_key + h)
                    other_images(1 + h)
                    for q in range(Q):
                        last = pe.matmul(bank[1 + h][:, tok(q)], qk4[:, 0, tok(q)], key_pads[:, h, tok(q)],
                                         start=False, stop=(q == Q - 1))
                    last.then_inc(sem(f"{name}_s_mm"), 1)
                pe.wait_ge(sem(values), 1)
                stay_busy(5, 10)
                for n in range(HEADS4 + 2):
                    if n < HEADS4:
                        pe.wait_ge(sem(f"{name}_wide"), n + 1)
                        if n >= 2:
                            pe.wait_ge(sem(f"{name}_att_t"), n - 1)
                        for k in range(4):
                            last = pe.transpose(bank[4 + n % 2][:, k * P:(k + 1) * P],
                                                wide[:, n % 2, k * P:(k + 1) * P], ident[:, :])
                        last.then_inc(sem(f"{name}_tr"), 1)
                    if n >= 2:
                        h = n - 2
                        part = slice(h * HPAD, (h + 1) * HPAD)
                        pe.wait_ge(sem(f"{name}_att_t"), h + 1)
                        for q in range(Q):
                            last = pe.matmul(bank[6][part, tok(q)], v4[:, q, part], att_t[:, h % 2, tok(q)],
                                             start=True, stop=True)
                        last.then_inc(sem(f"{name}_av"), 1)
                if bias is not None:
                    every_token(7, bias)
                pe.wait_ge(sem(f"{name}_out"), 1)
                for q in range(Q):
                    last = pe.matmul(tiles(7)[:, q, :], out_t[:, 0, tok(q)], wo_t[:, out_w, :], start=bias is None,
                                     stop=(bias is None or q == Q - 1))
                last.then_inc(sem(f"{name}_down"), 1)

            attention4("a2", 0, bo2, "qk2_ready", 3, "v2_ready")

            loaded("tree_in")
            for c, n in ((0, P), (1, NODES - P)):
                last = pe.transpose(bank[3][0:D, c * P:c * P + n], w1s_nat[0:n, c, :], ident[0:n, 0:n])
            last.then_inc(sem("w1s_tr"), 1)
            stay_busy(4, 7)
            loaded("moe3_in")
            for c, (h0, n) in enumerate(((0, P), (P, TAIL))):
                for k in range(NE // 2):
                    last = pe.transpose(bank[5 + c][0:n, tok(k)], w2e_nat[:, k, h0:h0 + n], ident[:, :])
                last.then_inc(sem("w2e_tr"), 1)
            to_features(xs[5], 2, "x6_ready", "x6_tr")
            pe.wait_ge(*nth("x6t_ready"))
            pe.wait_ge(sem("w1s_ready"), 1)
            for q in range(Q):
                last = pe.matmul(bank[q // 2][:, (q % 2) * 256:(q % 2) * 256 + NODES], xt[6][:, tok(q)],
                                 w1s_t[:, 0:NODES], start=True, stop=True)
            last.then_inc(sem("tree_mm"), 1)
            loaded("w2s_in")
            pe.wait_ge(sem("w2e_t_ready"), 3)

            def transpose_z(k, s):
                pe.wait_ge(sem("z_ready"), k + 1)
                if not isinstance(k, int) or k >= 2:
                    pe.wait_ge(sem("z_t_ready"), k - 1)
                for q in range(Q):
                    last = pe.transpose(bank[s][:, tok(q)], zbuf[:, s, q, :, :].rearrange("p a d -> p (a d)"),
                                        ident[:, :])
                last.then_inc(sem("z_tr"), 1)

            def outputs(k, s, weights):
                pe.wait_ge(sem("z_t_ready"), k + 1)
                first, final = (isinstance(k, int) and k == n for n in (1, CHUNKS - 1))
                for q in range(Q):
                    last = pe.matmul(bank[4 + q][:, :], z_t[:, s, tok(q)], weights, start=first,
                                     stop=final, skip_group_check=True)
                    if final:
                        last.then_inc(sem("tree_done"), 1)
                if not final:
                    last.then_inc(sem("tree_main"), 1)

            def level_chunks(lv, i, s):
                k = i * 2 + (FIRST_CHUNK[lv] + s)
                parents = w2s[:, 2 ** (lv - 1) - 1:2 ** lv - 1, :].rearrange("p (t c) o -> p t c o", t=8)
                transpose_z(k + 1, s)
                outputs(k, 1 - s, parents[:, :, ds(i * 2 + s, 1), :].rearrange("p t c o -> p t (c o)"))

            pe.wait_ge(sem("pathw_ready"), 2)
            for c, n in ((0, P), (1, NODES - P)):
                for q in range(Q):
                    last = pe.transpose(bank[2 + c][0:n, tok(q)], pathw[:, q, c * P:c * P + n], ident[:, :])
                last.then_inc(sem("pathw_tr"), 1)
            transpose_z(0, 0)
            transpose_z(1, 1)
            pe.wait_ge(sem("z_t_ready"), 1)
            pe.wait_ge(sem("pathw_t"), 2)
            for q in range(Q):
                last = pe.matmul(bank[2][:, tok(q)], z_t[:, 0, tok(q)], w2low[:, 8:10, :], start=True, stop=True)
            last.then_inc(sem("tree_main"), 1)
            for lv in (7, 6, 5):
                level_chunks(lv, 0, 0)
                level_chunks(lv, 0, 1)
                if lv > 5:
                    with pe.Fori(1, 2 ** (lv - 5)) as i:
                        level_chunks(lv, i, 0)
                        level_chunks(lv, i, 1)
            level_chunks(4, 0, 0)
            outputs(CHUNKS - 1, 0, w2low[:, 0:8, :])
            for q in range(Q):
                for c, n in ((0, P), (1, NODES - P)):
                    last = pe.matmul(tiles(3)[:, q, :], pathw_t[0:n, c, tok(q)], b2s[0:n, c, :],
                                     start=(c == 0), stop=(c == 1))
            last.then_inc(sem("tree_b2"), 1)

            for n in range(6):
                j, g = n // 3, n % 3
                if n >= 2:
                    pe.wait_ge(sem("w13_t_ready"), n - 1)
                for k in range(4 * g, min(4 * g + 4, NB13)):
                    r = min(P, NE * HID3 - k * P)
                    last = pe.transpose(bank[n % 2][0:D, (k % 4) * P:(k % 4) * P + r], w13_nat[0:r, j, k, :],
                                        ident[0:r, 0:r])
                last.then_inc(sem("w13_tr"), 1)
            pe.wait_ge(sem("w13_t_ready"), 6)
            stay_busy(0, 11)
            to_features(fn[:, :, 0:D], 2, "f7_ready", "f7_tr")
            pe.wait_ge(*nth("f7t_ready"))
            for q in range(Q):
                pe.matmul(bank[3 + q][:, :], ft[:, tok(q)], ft[:, :], start=True, stop=True)\
                    .then_inc(sem("sim_mm"), 1)
            for m in range(Q):
                pe.wait_ge(sem("sim_exp"), m + 1)
                for q in range(Q):
                    last = pe.matmul(bank[SIM_BANKS[q]][:, 0:D + 1], esim[:, m, tok(q)], fn[:, m, :],
                                     start=(m == 0), stop=(m == Q - 1), skip_group_check=True)
                    if m == Q - 1:
                        last.then_inc(sem("sim_av"), 1)

            stay_busy(3, 10)
            to_features(inner, 2, "x8n_ready", "x8n_tr")
            pe.wait_ge(*nth("x8nt_ready"))
            for c in range(4):
                pe.matmul(bank[3 + c][:, :], wt[:, 5 + c, :], xt[8][:, :], start=True, stop=True)\
                    .then_inc(sem("qk3_mm"), 1)
            for q in range(Q):
                last = pe.matmul(bank[7][:, tok(q)], xt[8][:, tok(q)], wt_v3[:, :], start=True, stop=True)
            last.then_inc(sem("qk3_mm"), 1)
            pe.wait_ge(sem("q3_ready"), 1)
            attention4("a3", 1, None, "k3_ready", 1, "v3_ready")
            stay_busy(4, 10)
            to_features(inner, 2, "x9n_ready", "x9n_tr")
            logits(7, xt[9], "x9nt_ready", router_t, "r3_mm")

            def down3(i):
                pe.wait_ge(sem("f3_ht"), i * 4 + 4)
                pe.wait_ge(sem("f3_acc"), i + 1)
                for q in range(Q):
                    pe.matmul(bank[6][:, tok(q)], ht[0:D + TAIL, 0, 1, tok(q)],
                              w2e_t[0:D + TAIL, 1, ds(i * 2 * D, 2 * D)], start=True, stop=False)
                    for s in range(2):
                        last = pe.matmul(tiles(6, P)[:, q, s * D:(s + 1) * D], ht[:, s, 0, tok(q)],
                                         w2e_t[:, 0, ds((i * 2 + s) * D, D)], start=False, stop=(s == 1))
                last.then_inc(sem("f3_down"), 1)

            def up3(i, s):
                e = i * 2 + s
                pe.wait_ge(sem(f"e3_slot_in{s}"), i * 4 + 4)
                if not first_round(i):
                    pe.wait_ge(sem("f3_ht"), e * 2 - 2)
                for c in range(3):
                    m = P if c < 2 else D + TAIL
                    pe.matmul(bank[3 * s + c][0:m, :], e3_slot[:, s, c * P:c * P + m], xt[9][:, :],
                              start=True, stop=True).then_inc(sem("f3_up"), 1)

            up3(0, 0)
            up3(0, 1)
            with pe.Fori(1, NE // 2) as i:
                up3(i, 0)
                down3(i - 1)
                up3(i, 1)
            down3(NE // 2 - 1)


_INS = ["x", "L0_tok_weight", "L0_tok_bias", "L0_attn_q_weight", "L0_ffn_wr", "L0_ffn_br", "L0_ffn_w1",
        "L0_ffn_b1", "L0_ffn_w2", "L0_ffn_b2", "L1_attn_Wq", "L1_attn_bq", "L1_attn_Wk", "L1_attn_bk",
        "L1_attn_Wv", "L1_attn_bv", "L1_attn_Wu", "L1_attn_bu", "L1_ffn_Wr", "L1_ffn_br", "L1_ffn_ln_g",
        "L1_ffn_ln_b", "L1_ffn_W1", "L1_ffn_b1", "L1_ffn_W2", "L1_ffn_b2", "L2_attn_ln_gamma",
        "L2_attn_ln_beta", "L2_attn_Wq", "L2_attn_bq", "L2_attn_Wk", "L2_attn_bk", "L2_attn_Wv", "L2_attn_bv",
        "L2_attn_Wpos", "L2_attn_bpos", "L2_attn_Wo", "L2_attn_bo", "L2_attn_u_bias", "L2_attn_v_bias",
        "L2_ffn_w1s", "L2_ffn_b1s", "L2_ffn_w2s", "L2_ffn_b2s", "L3_ffn_ln1_w", "L3_ffn_ln2_w", "L3_ffn_wq",
        "L3_ffn_wk", "L3_ffn_wv", "L3_ffn_wo", "L3_ffn_router_w", "L3_ffn_w1", "L3_ffn_w2", "L3_ffn_w3"]


def kernel(**inputs):
    import numpy as _np
    import concourse.bacc as _bacc
    from concourse import mybir as _mybir
    from concourse.bass_utils import run_bass_kernel_spmd as _run

    nc = _bacc.Bacc("TRN2", target_bir_lowering=False, num_devices=1)
    arrays, drams = {}, {}
    rope, rel = shape_constants()
    for name, value in [(n, inputs[n]) for n in _INS] + [("rope", rope), ("rel", rel)]:
        value = _np.ascontiguousarray(value)
        arrays[f"in_{name}_dram"] = value
        drams[name] = nc.dram_tensor(f"in_{name}_dram", value.shape, _mybir.dt.from_np(value.dtype),
                                     kind="ExternalInput").ap()
    out = nc.dram_tensor("out_0_dram", (N_IMG, SEQ, D), F32, kind="ExternalOutput").ap()
    vit_tower(nc, drams, drams["rope"], drams["rel"], out)
    r = _run(nc, [arrays], core_ids=[0])
    return r.results[0]["out_0_dram"]
```
